# Optimizing a Trainium2 kernel written in Bass

```python
import numpy as np
import jax
import jax.numpy as jnp

def _softmax(x, axis=-1):
    return jax.nn.softmax(x, axis=axis)

def _gelu(x):
    return jax.nn.gelu(x, approximate=True)

def _silu(x):
    return jax.nn.silu(x)

def _sigmoid(x):
    return jax.nn.sigmoid(x)

def _layernorm(x, axis=-1, eps=1e-05):
    m = jnp.mean(x, axis=axis, keepdims=True)
    v = jnp.var(x, axis=axis, keepdims=True)
    return (x - m) / jnp.sqrt(v + eps)

def _scatter_add(tgt, idx, src, axis=0):
    return tgt.at[idx].add(src)

def _segment_sum(src, seg, n):
    return jax.ops.segment_sum(src, seg, n)
kernel_name = 'mk_xattn_ffn_d1_seqx_r8_3b0d31'

def setup_inputs(seed: int=0):
    np.random.seed(seed)
    _w = jnp.asarray

    def _rec_inputs():
        import jax
        import jax.numpy as jnp
        _rk = jax.random.key(seed)
        x = 7.22e-05 + 1 * jax.random.normal(jax.random.fold_in(_rk, 1), (32, 56, 128), jnp.float32)
        _lenS = 56 - jax.random.randint(jax.random.fold_in(_rk, 7), (32,), 0, max(1, 56 // 4) + 1, jnp.int32)
        _lenS2 = 1500 - jax.random.randint(jax.random.fold_in(_rk, 8), (32,), 0, max(1, 1500 // 4) + 1, jnp.int32)
        _ctx_1024P = jax.random.normal(jax.random.fold_in(_rk, 11), (32, 16, 128), jnp.float32)
        _ctx_1024c = jax.random.dirichlet(jax.random.fold_in(_rk, 511), 0.3 * jnp.ones((16,), jnp.float32), (32, 1500))
        _ctx_1024t = jnp.einsum('bsk,bkd->bsd', _ctx_1024c, _ctx_1024P)
        _ctx_1024t = _ctx_1024t * jax.lax.rsqrt(jnp.mean(jnp.square(_ctx_1024t)) + 1e-12) * 0.953939
        ctx_1024 = 4.13588e-05 + 0.999923 * (_ctx_1024t + 0.3 * jax.random.normal(jax.random.fold_in(_rk, 611), (32, 1500, 128), jnp.float32))
        return (x, ctx_1024)
    x, ctx_1024 = _rec_inputs()

    def _L0_xattn_setup():
        import jax, jax.numpy as jnp
        import numpy as np
        import math
        D = 128
        H = 16
        B = 4
        S = 256

        def _split_heads(x):
            b, s, d = x.shape
            return x.reshape(b, s, H, d // H).transpose(0, 2, 1, 3)
        key = jax.random.key(seed)
        ks = jax.random.split(key, 11)
        s = 1.0 / math.sqrt(D)
        inp = {'queries': jax.random.normal(ks[0], (B, S, D), jnp.float32), 'keys': jax.random.normal(ks[1], (B, S, D), jnp.float32), 'values': jax.random.normal(ks[2], (B, S, D), jnp.float32), 'Wq': jax.random.normal(ks[3], (D, D), jnp.float32) * s, 'bq': jnp.zeros((D,), jnp.float32), 'Wk': jax.random.normal(ks[4], (D, D), jnp.float32) * s, 'bk': jnp.zeros((D,), jnp.float32), 'Wv': jax.random.normal(ks[5], (D, D), jnp.float32) * s, 'bv': jnp.zeros((D,), jnp.float32), 'Wo': jax.random.normal(ks[6], (D, D), jnp.float32) * s, 'bo': jnp.zeros((D,), jnp.float32)}
        return inp
    _L0_xattn_all = _L0_xattn_setup()
    _L0_xattn_in = {k: v for k, v in _L0_xattn_all.items() if k in ('Wq', 'bq', 'Wk', 'bk', 'Wv', 'bv', 'Wo', 'bo')}
    del _L0_xattn_all

    def _L0_ffn_setup():
        import jax, jax.numpy as jnp
        import numpy as np
        D_MODEL = 128
        NUM_HEADS = 4
        NUM_EXPERTS = 8
        TOP_K = 2
        D_FF = 128
        EPS = 1e-06

        def _rmsnorm(x, g):
            return x * jax.lax.rsqrt(jnp.mean(x * x, axis=-1, keepdims=True) + EPS) * g

        def _swiglu(x, w1, w2, w3):
            return jax.nn.silu(x @ w1.T) * (x @ w3.T) @ w2.T
        key = jax.random.key(seed)
        ks = jax.random.split(key, 16)
        d, e, f = (D_MODEL, NUM_EXPERTS, D_FF)
        dc = d // 4
        s = 0.02
        return {'X': jax.random.normal(ks[0], (2, 128, d), dtype=jnp.float32), 'g1': jnp.ones((d,), jnp.float32), 'g2': jnp.ones((d,), jnp.float32), 'Wq': jax.random.normal(ks[1], (d, d), jnp.float32) * s, 'Wkc': jax.random.normal(ks[2], (dc, d), jnp.float32) * s, 'Wvc': jax.random.normal(ks[3], (dc, d), jnp.float32) * s, 'Wo': jax.random.normal(ks[4], (d, d), jnp.float32) * s, 'Wr': jax.random.normal(ks[5], (e, d), jnp.float32) * s, 'expert_bias': jnp.zeros((e,), jnp.float32), 'sW1': jax.random.normal(ks[6], (f, d), jnp.float32) * s, 'sW2': jax.random.normal(ks[7], (d, f), jnp.float32) * s, 'sW3': jax.random.normal(ks[8], (f, d), jnp.float32) * s, 'eW1': jax.random.normal(ks[9], (e, f, d), jnp.float32) * s, 'eW2': jax.random.normal(ks[10], (e, d, f), jnp.float32) * s, 'eW3': jax.random.normal(ks[11], (e, f, d), jnp.float32) * s}
    _L0_ffn_all = _L0_ffn_setup()
    _L0_ffn_in = {k: v for k, v in _L0_ffn_all.items() if k in ('g1', 'g2', 'Wq', 'Wkc', 'Wvc', 'Wo', 'Wr', 'expert_bias', 'sW1', 'sW2', 'sW3', 'eW1', 'eW2', 'eW3')}
    del _L0_ffn_all
    return {'x': x, 'ctx_1024': ctx_1024, 'L0_xattn_Wq': _L0_xattn_in['Wq'], 'L0_xattn_bq': _L0_xattn_in['bq'], 'L0_xattn_Wk': _L0_xattn_in['Wk'], 'L0_xattn_bk': _L0_xattn_in['bk'], 'L0_xattn_Wv': _L0_xattn_in['Wv'], 'L0_xattn_bv': _L0_xattn_in['bv'], 'L0_xattn_Wo': _L0_xattn_in['Wo'], 'L0_xattn_bo': _L0_xattn_in['bo'], 'L0_ffn_g1': _L0_ffn_in['g1'], 'L0_ffn_g2': _L0_ffn_in['g2'], 'L0_ffn_Wq': _L0_ffn_in['Wq'], 'L0_ffn_Wkc': _L0_ffn_in['Wkc'], 'L0_ffn_Wvc': _L0_ffn_in['Wvc'], 'L0_ffn_Wo': _L0_ffn_in['Wo'], 'L0_ffn_Wr': _L0_ffn_in['Wr'], 'L0_ffn_expert_bias': _L0_ffn_in['expert_bias'], 'L0_ffn_sW1': _L0_ffn_in['sW1'], 'L0_ffn_sW2': _L0_ffn_in['sW2'], 'L0_ffn_sW3': _L0_ffn_in['sW3'], 'L0_ffn_eW1': _L0_ffn_in['eW1'], 'L0_ffn_eW2': _L0_ffn_in['eW2'], 'L0_ffn_eW3': _L0_ffn_in['eW3']}

def reference(x, ctx_1024, L0_xattn_Wq, L0_xattn_bq, L0_xattn_Wk, L0_xattn_bk, L0_xattn_Wv, L0_xattn_bv, L0_xattn_Wo, L0_xattn_bo, L0_ffn_g1, L0_ffn_g2, L0_ffn_Wq, L0_ffn_Wkc, L0_ffn_Wvc, L0_ffn_Wo, L0_ffn_Wr, L0_ffn_expert_bias, L0_ffn_sW1, L0_ffn_sW2, L0_ffn_sW3, L0_ffn_eW1, L0_ffn_eW2, L0_ffn_eW3):
    import jax
    import jax.numpy as jnp

    def _L0_xattn_ref(queries, keys, values, Wq, bq, Wk, bk, Wv, bv, Wo, bo):
        import jax, jax.numpy as jnp
        import numpy as np
        import math
        D = 128
        H = 16
        B = 4
        S = 256

        def _split_heads(x):
            b, s, d = x.shape
            return x.reshape(b, s, H, d // H).transpose(0, 2, 1, 3)
        q = jax.nn.relu(queries @ Wq + bq)
        k = jax.nn.relu(keys @ Wk + bk)
        v = jax.nn.relu(values @ Wv + bv)
        q, k, v = (_split_heads(q), _split_heads(k), _split_heads(v))
        dk = q.shape[-1]
        scores = jnp.einsum('bhqd,bhkd->bhqk', q, k) / jnp.sqrt(jnp.float32(dk))
        attn = jax.nn.softmax(scores, axis=-1)
        y = jnp.einsum('bhqk,bhkd->bhqd', attn, v)
        y = y.transpose(0, 2, 1, 3).reshape(queries.shape[0], queries.shape[1], -1)
        return jax.nn.relu(y @ Wo + bo)

    def _L0_ffn_ref(X, g1, g2, Wq, Wkc, Wvc, Wo, Wr, expert_bias, sW1, sW2, sW3, eW1, eW2, eW3):
        import jax, jax.numpy as jnp
        import numpy as np
        D_MODEL = 128
        NUM_HEADS = 4
        NUM_EXPERTS = 8
        TOP_K = 2
        D_FF = 128
        EPS = 1e-06

        def _rmsnorm(x, g):
            return x * jax.lax.rsqrt(jnp.mean(x * x, axis=-1, keepdims=True) + EPS) * g

        def _swiglu(x, w1, w2, w3):
            return jax.nn.silu(x @ w1.T) * (x @ w3.T) @ w2.T
        B, S, d = X.shape
        H = NUM_HEADS
        dk = d // H
        scale = 1.0 / jnp.sqrt(jnp.float32(dk))
        nx = _rmsnorm(X, g1)
        Q = (nx @ Wq.T).reshape(B, S, H, dk).transpose(0, 2, 1, 3)
        Kc = nx @ Wkc.T
        Vc = nx @ Wvc.T
        scores = jnp.einsum('bhsd,btd->bhst', Q, Kc) * scale
        attn = jax.nn.softmax(scores, axis=-1)
        out = jnp.einsum('bhst,btd->bhsd', attn, Vc)
        out = out.transpose(0, 2, 1, 3).reshape(B, S, d) @ Wo.T
        X = X + out
        nx = _rmsnorm(X, g2)
        xf = nx.reshape(-1, d)
        logits = xf @ Wr.T + expert_bias
        rw = jax.nn.softmax(logits, axis=-1)
        topw, topi = jax.lax.top_k(rw, TOP_K)
        topw = jax.nn.softmax(topw, axis=-1)
        combine = jnp.sum(jax.nn.one_hot(topi, NUM_EXPERTS, dtype=xf.dtype) * topw[..., None], axis=1)
        shared = _swiglu(xf, sW1, sW2, sW3)
        h = jax.nn.silu(jnp.einsum('td,efd->etf', xf, eW1)) * jnp.einsum('td,efd->etf', xf, eW3)
        eo = jnp.einsum('etf,edf->etd', h, eW2)
        specialist = jnp.einsum('te,etd->td', combine, eo)
        moe_out = (shared + specialist).reshape(B, S, d)
        return X + moe_out
    x = x + _L0_xattn_ref(_layernorm(x, axis=-1), ctx_1024, ctx_1024, L0_xattn_Wq, L0_xattn_bq, L0_xattn_Wk, L0_xattn_bk, L0_xattn_Wv, L0_xattn_bv, L0_xattn_Wo, L0_xattn_bo)
    x = x + _L0_ffn_ref(_layernorm(x, axis=-1), L0_ffn_g1, L0_ffn_g2, L0_ffn_Wq, L0_ffn_Wkc, L0_ffn_Wvc, L0_ffn_Wo, L0_ffn_Wr, L0_ffn_expert_bias, L0_ffn_sW1, L0_ffn_sW2, L0_ffn_sW3, L0_ffn_eW1, L0_ffn_eW2, L0_ffn_eW3)
    return x

_drawn_inputs = setup_inputs


def setup_inputs(seed=0):
    import zlib

    import numpy as np

    out = dict(_drawn_inputs(seed))
    spreads = {'L0_xattn_bq': (0.0, 0.8),
     'L0_xattn_bk': (0.0, 0.8),
     'L0_xattn_bv': (0.0, 0.1),
     'L0_xattn_bo': (0.0, 0.1),
     'L0_ffn_g1': (1.0, 0.6),
     'L0_ffn_g2': (1.0, 0.6),
     'L0_ffn_expert_bias': (0.0, 0.8)}
    factors = {'L0_ffn_Wq': 8.0,
     'L0_ffn_Wkc': 8.0,
     'L0_ffn_Wvc': 7.236,
     'L0_ffn_Wo': 7.177,
     'L0_ffn_Wr': 8.0,
     'L0_ffn_sW1': 8.0,
     'L0_ffn_sW2': 8.0,
     'L0_ffn_sW3': 8.0,
     'L0_ffn_eW1': 8.0,
     'L0_ffn_eW2': 8.0,
     'L0_ffn_eW3': 8.0}
    for name, (base, spread) in spreads.items():
        noise = np.random.default_rng([zlib.crc32(name.encode()), seed]).standard_normal(out[name].shape)
        drawn = base * np.exp(spread * noise) if base else spread * noise
        out[name] = jnp.asarray(drawn.astype(out[name].dtype))
    for name, factor in factors.items():
        out[name] = (out[name] * factor).astype(out[name].dtype)
    return out
```

```python
import concourse.bass as bass
from concourse import mybir
from contextlib import ExitStack

F32 = mybir.dt.float32
BF16 = mybir.dt.bfloat16
U32 = mybir.dt.uint32
ALU = mybir.AluOpType
ACT = mybir.ActivationFunctionType
AX_X = mybir.AxisListType.X

D = 128
B, SQ, SK = 32, 56, 1500
H, DK = 16, 8
HP = H // 2
PQ = 2 * SQ
CH = 500
TK = 125
NT = CH // TK
CPB = SK // CH
NCH = B * CPB
PERIOD = 2 * CPB
PAIRS = B // 2
HALF = HP // 2 * PQ
K_PART = [0, 0, 0, 1, 1, 2]
Q_PART = [0, 1, 2, 0, 1, 0]
NSLOT = len(K_PART)
ROWS = 16 * NSLOT
SHIFT = ROWS
SCALE = DK ** -0.5
TWO_ONES = 0x3F803F80
EPS_LN, EPS_RMS = 1e-5, 1e-6

GROUPS = [(0, 3, 0, 0, 0), (3, 3, 1, 0, 25), (6, 3, 2, 0, 50), (9, 3, 3, 0, 75),
          (12, 2, 0, 3 * SQ, 100), (14, 2, 1, 3 * SQ, 117)]
VW = 134
YW = 5 * SQ

FH, FDK = 4, 32
NE, FF = 8, 128
W = 64 * B
G = W // 512


def wait(eng, sem, value):
    if not isinstance(value, int) or value > 0:
        eng.wait_ge(sem, value)


def there(n, count=NCH):
    return not isinstance(n, int) or 0 <= n < count


def setup(nc, ins, t):
    with ExitStack() as ctx:
        def sb(name, shape, dt=F32):
            return ctx.enter_context(nc.sbuf_tensor(name, shape, dt))

        def sem(name):
            return ctx.enter_context(nc.semaphore(name))

        wq = sb("wq", [D, D])
        bq = sb("bq", [D, 1])
        wo_flat = sb("wo_flat", [D, D])
        bv_col = sb("bv_col", [D, 1])
        bv_wide = sb("bv_wide", [D, D])
        bo_row = sb("bo_row", [D, D])
        xn = sb("xn", [128, PAIRS, D])
        xsq = sb("xsq", [128, PAIRS, D])
        st = sb("st", [128, 4, PAIRS])
        xnT = sb("xnT", [D, PAIRS, 2, 64])
        q32 = sb("q32", [D, B, SQ])
        qres = sb("qres", [D, B, SQ])
        qp = sb("qp", [D, 3, B, SQ], BF16)
        ps = [ctx.enter_context(nc.psum_tensor(f"ps_setup{i}", [128, 512], F32)) for i in range(5)]

        padded = sem("padded")
        x_in = sem("x_in")
        w_in = sem("w_in")
        wo_in = sem("wo_in")
        dve = sem("dve_chain")
        pool = sem("pool_chain")
        ident = sem("ident_ready")
        var_done = sem("var_done")
        std_done = sem("std_done")
        xn_done = sem("xn_done")
        xT_done = sem("xT_done")
        xT_copied = sem("xT_copied")
        q_done = sem("q_done")
        q_ready = sem("q_ready")
        q_cut = sem("q_cut")
        q_zero = sem("q_zero")
        q_stacked = sem("q_stacked")
        c_done = sem("c_done")
        bvw = sem("bvw")

        block = ctx.enter_context(nc.Block())

        @block.sync
        def _(sp):
            sp.wait_ge(padded, 1)
            for par in range(2):
                sp.dma_start(t.x[64 * par:64 * par + SQ, :, :],
                             ins["x"].rearrange("(n par) q d -> par q n d", par=2)[par]).then_inc(x_in, 16)
            for dst, src in ((wq[:, :], ins["Wq"]), (bq[:, :], ins["bq"]), (t.wk[:, :], ins["Wk"]),
                             (t.bk[:, :], ins["bk"]), (t.wv[:, :], ins["Wv"]), (wo_flat[:, :], ins["Wo"]),
                             (bv_col[:, :], ins["bv"].rearrange("a d -> d a"))):
                sp.dma_start(dst, src).then_inc(w_in, 16)
            sp.dma_start(t.neg_bv[:, :], ins["bv"].partition_broadcast(128)).then_inc(w_in, 16)
            sp.dma_start(bo_row[:, :], ins["bo"].partition_broadcast(128)).then_inc(w_in, 16)
            sp.wait_ge(padded, 2)
            for first, n, tile, col, _ in GROUPS:
                for j in range(n):
                    r = 32 * tile + DK * j
                    sp.dma_start(t.wo_rows[r:r + DK, col // SQ + j, :],
                                 ins["Wo"][DK * (first + j):DK * (first + j + 1), :]).then_inc(wo_in, 16)
            sp.wait_ge(q_zero, 2)
            sp.wait_ge(q_cut, 3)
            for s in range(NSLOT):
                for h2 in range(2):
                    r = 16 * s + 8 * h2
                    sp.dma_start(t.q_stack[r:r + 8, :, h2, :, :].rearrange("p g b q -> p g (b q)"),
                                 qp[64 * h2:64 * h2 + 64, Q_PART[s], :, :].rearrange("p b q -> p (b q)"))\
                        .then_inc(q_stacked, 16)
            sp.wait_ge(q_stacked, 16 * 2 * NSLOT)
            sp.wait_ge(wo_in, 16 * H)
            sp.wait_ge(w_in, 16 * 9)

        @block.gpsimd
        def _(g):
            g.memset(t.ident[:, :], 0.0).then_inc(pool, 1)
            g.wait_ge(pool, 1)
            g.affine_select(out=t.ident[:, :], in_=t.ident[:, :], compare_op=ALU.not_equal, fill=1.0, base=0,
                            pattern=[[-1, 128]], channel_multiplier=1).then_inc(ident, 1)
            for c in range(2):
                z = t.q_stack[:, 4 * c:4 * c + 4, :, :, :].bitcast(U32)
                g.memset(z, 0).then_inc(q_zero, 1)
            g.wait_ge(ident, 1)
            g.wait_ge(q_zero, 2)
            g.memset(t.k_stack[SHIFT:128, :, :, :].bitcast(U32), TWO_ONES).then_inc(pool, 1)
            g.wait_ge(pool, 2)
            g.memset(t.q_turn[SHIFT:128, :, :], 0.0).then_inc(pool, 1)
            g.wait_ge(pool, 3)
            g.memset(t.yn[:, :], 0.0).then_inc(pool, 1)

        @block.vector
        def _(v):
            links = [0]

            def chain(ins):
                links[0] += 1
                ins.then_inc(dve, 1)
                v.wait_ge(dve, links[0])

            v.memset(t.x[:, :, :], 0.0).then_inc(padded, 1)
            v.memset(t.wo_rows[:, :, :], 0.0).then_inc(padded, 1)
            v.memset(t.v_aug[:, :, :, :], 1.0)
            v.memset(t.y_sum[:, :], 0.0)
            v.wait_ge(x_in, 32)
            mean, var = st[:, 0, :], st[:, 1, :]
            chain(v.tensor_reduce(mean, t.x[:, :, :], AX_X, ALU.add))
            chain(v.tensor_scalar(mean, mean, 1.0 / D, None, ALU.mult))
            chain(v.tensor_tensor(xn[:, :, :], t.x[:, :, :], mean.unsqueeze(2).broadcast_to([128, PAIRS, D]),
                                  ALU.subtract))
            chain(v.tensor_tensor(xsq[:, :, :], xn[:, :, :], xn[:, :, :], ALU.mult))
            chain(v.tensor_reduce(var, xsq[:, :, :], AX_X, ALU.add))
            v.tensor_scalar(var, var, 1.0 / D, EPS_LN, ALU.mult, ALU.add).then_inc(var_done, 1)
            v.wait_ge(std_done, 1)
            chain(v.reciprocal(st[:, 3, :], st[:, 2, :]))
            v.tensor_tensor(xn[:, :, :], xn[:, :, :], st[:, 3, :].unsqueeze(2).broadcast_to([128, PAIRS, D]),
                            ALU.mult).then_inc(xn_done, 1)
            v.wait_ge(ident, 1)
            v.tensor_copy(t.ident_b[:, :], t.ident[:, :])
            v.tensor_copy(t.sel_a[:, :].rearrange("p (j x) -> p j x", x=32),
                          t.ident[:, 24::32].unsqueeze(2).broadcast_to([128, 4, 32]))
            v.tensor_copy(t.sel_b[:, :].rearrange("p (j x) -> p j x", x=32),
                          t.ident[:, 16:64:32].unsqueeze(2).broadcast_to([128, 2, 32]))
            v.wait_ge(w_in, 16 * 9)
            v.tensor_scalar(t.neg_bv[:, :], t.neg_bv[:, :], -1.0, None, ALU.mult)
            v.tensor_copy(bv_wide[:, :], bv_col[:, 0:1].broadcast_to([D, D])).then_inc(bvw, 1)
            v.wait_ge(q_ready, G)
            q_all, r_all = q32[:, :, :], qres[:, :, :]
            v.tensor_copy(qp[:, 0, :, :], q_all).then_inc(q_cut, 1)
            v.wait_ge(q_cut, 1)
            chain(v.tensor_tensor(r_all, q_all, qp[:, 0, :, :], ALU.subtract))
            v.tensor_copy(qp[:, 1, :, :], r_all).then_inc(q_cut, 1)
            v.wait_ge(q_cut, 2)
            v.tensor_tensor(qp[:, 2, :, :], r_all, qp[:, 1, :, :], ALU.subtract).then_inc(q_cut, 1)
            v.wait_ge(c_done, 1)
            v.tensor_tensor(t.const_row[:, :], ps[4][:, 0:D], bo_row[:, :], ALU.add)

        @block.scalar
        def _(a):
            a.wait_ge(var_done, 1)
            a.activation(st[:, 2, :], st[:, 1, :], ACT.Sqrt).then_inc(std_done, 1)
            for c in range(G):
                a.wait_ge(xT_done, c + 1)
                a.copy(xnT[:, 4 * c:4 * c + 4, :, :], ps[c][:, :].rearrange("p (n h q) -> p n h q", n=4, h=2)
                       ).then_inc(xT_copied, 1)
            a.wait_ge(w_in, 16 * 9)
            for c in range(G):
                a.wait_ge(q_done, c + 1)
                a.activation(q32[:, 8 * c:8 * c + 8, :], ps[c][:, 0:8 * SQ].rearrange("p (b q) -> p b q", b=8),
                             ACT.Relu, bias=bq[:, 0:1]).then_inc(q_ready, 1)

        @block.tensor
        def _(pe):
            pe.wait_ge(ident, 1)
            pe.wait_ge(xn_done, 1)
            for c in range(G):
                for n in range(4):
                    m = pe.transpose(ps[c][:, 128 * n:128 * n + 128], xn[:, 4 * c + n, :], t.ident[:, :])
                m.then_inc(xT_done, 1)
            pe.wait_ge(w_in, 16 * 9)
            for c in range(G):
                pe.wait_ge(xT_copied, c + 1)
                pe.matmul(ps[c][:, 0:8 * SQ], wq[:, :], xnT[:, 4 * c:4 * c + 4, :, 0:SQ], start=True,
                          stop=True).then_inc(q_done, 1)
            pe.wait_ge(bvw, 1)
            pe.matmul(ps[4][:, 0:D], bv_wide[:, :], wo_flat[:, :], start=True, stop=True).then_inc(c_done, 1)


def cross_attention(nc, ins, t):
    with ExitStack() as ctx:
        def sb(name, shape, dt=F32):
            return ctx.enter_context(nc.sbuf_tensor(name, shape, dt))

        def pb(name):
            return ctx.enter_context(nc.psum_tensor(name, [128, 512], F32))

        def sem(name):
            return ctx.enter_context(nc.semaphore(name))

        c_in = sb("c_in", [TK, 3, NT, D])
        cT = sb("cT", [D, 2, CH])
        k32 = sb("k32", [D, 2, CH])
        k_res = sb("k_res", [D, CH])
        kp = sb("kp", [D, 3, 3, CH], BF16)
        probs = sb("probs", [TK, 3, H * SQ])
        q_max = sb("q_max", [ROWS, 2, HP * PQ], BF16)
        max_part = sb("max_part", [PQ, 2, HP, CPB])
        neg_max = sb("neg_max", [PQ, HP])
        max_res = sb("max_res", [PQ, HP])
        max_cut = sb("max_cut", [PQ, HP, 3], BF16)
        y_raw = sb("y_raw", [128, YW])
        y_rec = sb("y_rec", [128, YW])
        o_tmp = sb("o_tmp", [128, D])

        s_bank = [pb(f"s_bank{i}") for i in range(3)]
        m_bank = [pb(f"m_bank{i}") for i in range(2)]
        bank_a = pb("bank_a")
        bank_b = pb("bank_b")
        y_bank = t.y_sum

        ctx_loaded = [sem(f"ctx_loaded{i}") for i in range(3)]
        stack_loaded = [sem(f"stack_loaded{i}") for i in range(PERIOD)]
        turned = sem("turned")
        keys_done = sem("keys_done")
        vals_done = sem("vals_done")
        maxs_done = sem("maxs_done")
        scores_done = sem("scores_done")
        pv_done = sem("pv_done")
        mrow_done = sem("mrow_done")
        den_done = sem("den_done")
        out_done = sem("out_done")
        cT_ready = sem("cT_ready")
        k32_ready = sem("k32_ready")
        k1_ready = sem("k1_ready")
        probs_ready = sem("probs_ready")
        shift_ready = sem("shift_ready")
        v_ready = sem("v_ready")
        max_read = sem("max_read")
        negmax_ready = sem("negmax_ready")
        y_ready = sem("y_ready")
        rec_ready = sem("rec_ready")
        yn_ready = sem("yn_ready")
        o_ready = sem("o_ready")
        x_ready = sem("x_ready")
        maxcut_ready = sem("maxcut_ready")
        res_ready = sem("res_ready")
        kcut_ready = sem("kcut_ready")
        qmax_ready = sem("qmax_ready")
        qturn_ready = sem("qturn_ready")

        ctx_rows = ins["ctx"].rearrange("b (c n p) d -> (b c) p n d", c=CPB, n=NT)

        def at(i, k):
            return i * PERIOD + k

        def steps(eng, step):
            for k in range(PERIOD):
                step(-1, k)
            for k in range(PERIOD):
                step(0, k)
            with eng.Fori(1, NCH // PERIOD - 1) as i:
                for k in range(PERIOD):
                    step(i, k)
            for k in range(PERIOD):
                step(NCH // PERIOD - 1, k)

        block = ctx.enter_context(nc.Block())

        @block.sync
        def _(sp):
            def load_ctx(i, k):
                n = at(i, k)
                if there(n):
                    if isinstance(n, int):
                        src = ctx_rows[n]
                    else:
                        src = ctx_rows[bass.ds(sp.snap(n), 1)].rearrange("o p n d -> (o p) n d")
                    wait(sp, turned, n - 2)
                    sp.dma_start(c_in[:, k % 3, :, :], src).then_inc(ctx_loaded[k % 3], 16)

            def step(i, k):
                load_ctx(i, k + 6)
                n = at(i, k + 5)
                if there(n):
                    wait(sp, scores_done, 2 * NT * (n - 5))
                    sp.wait_ge(kcut_ready, n + 1)
                    for s in range(NSLOT):
                        sp.dma_start(t.k_stack[16 * s:16 * s + 16, (k + 5) % PERIOD, :, :],
                                     kp[:, (k + 5) % 3, K_PART[s], :]).then_inc(stack_loaded[(k + 5) % PERIOD], 16)

            steps(sp, step)

        @block.gpsimd
        def _(g):
            def step(i, k):
                b, kb = 2 * i + (k + 5) // 3, (k + 5) // 3
                if k % 3 == 1 and there(b, B):
                    wait(g, maxs_done, HP * CPB * (b - 1))
                b, kb = 2 * i + k // 3 + 1, k // 3 + 1
                if k % 3 == 0 and there(b, B):
                    wait(g, scores_done, 2 * NT * CPB * (b - 1))
                b = 2 * i + (k + 1) // 3
                if k % 3 == 2 and there(b, B):
                    g.wait_ge(negmax_ready, b + 1)
                    wait(g, maxcut_ready, b)
                    g.tensor_tensor(max_cut[:, :, 1], neg_max[:, :], max_cut[:, :, 0], ALU.subtract)
                    g.tensor_tensor(max_res[:, :], neg_max[:, :], max_cut[:, :, 0], ALU.subtract).then_inc(res_ready, 1)
                    g.wait_ge(res_ready, cuts(i, k) + 1)
                    g.tensor_tensor(max_cut[:, :, 2], max_res[:, :], max_cut[:, :, 1], ALU.subtract)\
                        .then_inc(maxcut_ready, 1)
                n = at(i, k + 6)
                if there(n):
                    done = cuts(i, k) + (1 if k % 3 == 2 and there(b, B) else 0)
                    g.wait_ge(k1_ready, n + 1)
                    wait(g, kcut_ready, n)
                    g.tensor_tensor(kp[:, k % 3, 1, :], k32[:, k % 2, :], kp[:, k % 3, 0, :], ALU.subtract)
                    g.tensor_tensor(k_res[:, :], k32[:, k % 2, :], kp[:, k % 3, 0, :], ALU.subtract)\
                        .then_inc(res_ready, 1)
                    g.wait_ge(res_ready, done + 1)
                    g.tensor_tensor(kp[:, k % 3, 2, :], k_res[:, :], kp[:, k % 3, 1, :], ALU.subtract)\
                        .then_inc(kcut_ready, 1)
                b, kb = 2 * i + (k + 5) // 3, (k + 5) // 3
                if k % 3 == 1 and there(b, B):
                    g.tensor_copy(grid(q_max[:, kb % 2, :]), q_rows(b)).then_inc(qmax_ready, 1)
                b, kb = 2 * i + k // 3 + 1, k // 3 + 1
                if k % 3 == 0 and there(b, B):
                    g.tensor_copy(grid(t.q_turn[0:ROWS, kb % 2, :]), q_rows(b)).then_inc(qturn_ready, 1)

            def grid(a):
                return a.rearrange("p (g q) -> p g q", q=SQ)

            def q_rows(b):
                a = t.q_stack[:, :, :, :, :].rearrange("p g h b q -> p (g h) b q")
                if isinstance(b, int):
                    return a[:, :, b, :]
                return a[:, :, bass.ds(b, 1), :].rearrange("p g o q -> p g (o q)")

            def cuts(i, k):
                chunks, maxima = at(i, k + 6), 2 * i + 1 + k // 3
                if isinstance(i, int):
                    chunks, maxima = min(chunks, NCH), max(maxima, 0)
                return chunks + maxima

            steps(g, step)

        @block.scalar
        def _(a):
            def exp(i, k, tile, half):
                n = at(i, k)
                if there(n):
                    j = 2 * NT * k + 2 * tile + half
                    a.wait_ge(scores_done, 2 * NT * n + 2 * tile + half + 1)
                    if half == 0:
                        wait(a, pv_done, NT * n + tile - 2)
                    a.activation(probs[:, (NT * k + tile) % 3, HALF * half:HALF * (half + 1)],
                                 s_bank[j % 3][0:TK, 0:HALF], ACT.Exp, scale=SCALE).then_inc(probs_ready, 1)

            def step(i, k):
                n = at(i, k + 6)
                exp(i, k, 0, 0)
                exp(i, k, 0, 1)
                if there(n):
                    a.wait_ge(turned, n + 1)
                    wait(a, vals_done, n - 1)
                    a.copy(cT[:, k % 2, :], bank_a[:, 0:CH]).then_inc(cT_ready, 1)
                exp(i, k, 1, 0)
                exp(i, k, 1, 1)
                if there(n):
                    a.wait_ge(keys_done, n + 1)
                    wait(a, kcut_ready, n - 1)
                    a.activation(k32[:, k % 2, :], bank_b[:, 0:CH], ACT.Relu, bias=t.bk[:, 0:1])\
                        .then_inc(k32_ready, 1)
                    wait(a, stack_loaded[(k + 3) % PERIOD], 16 * NSLOT * (i + (k + 3) // PERIOD + 1)
                         if there(at(i, k + 3)) else 0)
                    a.activation(kp[:, k % 3, 0, :], bank_b[:, 0:CH], ACT.Relu, bias=t.bk[:, 0:1])\
                        .then_inc(k1_ready, 1)
                exp(i, k, 2, 0)
                exp(i, k, 2, 1)
                b = 2 * i + (k + 1) // 3
                if k % 3 == 2 and there(b, B):
                    for half, bank in enumerate((bank_a, bank_b)):
                        a.wait_ge(mrow_done, 2 * b + half + 1)
                        a.copy(t.q_turn[SHIFT:SHIFT + 3, (k + 1) // 3 % 2, HALF * half:HALF * (half + 1)],
                               bank[SHIFT:SHIFT + 3, 0:HALF]).then_inc(shift_ready, 1)
                exp(i, k, 3, 0)
                exp(i, k, 3, 1)

            steps(a, step)

        @block.vector
        def _(v):
            def pair_max(i, k, pair):
                n, kk = at(i, k + 4), k + 4
                if there(n):
                    v.wait_ge(maxs_done, HP * n + pair + 1)
                    v.tensor_reduce(max_part[:, kk // CPB % 2, pair, kk % CPB:kk % CPB + 1],
                                    m_bank[pair % 2][0:PQ, 0:CH], AX_X, ALU.max).then_inc(max_read, 1)

            def finish_a(i, k):
                b = 2 * i + k // 3 - 1
                if k % 3 == 0 and there(b, B):
                    v.wait_ge(pv_done, NT * CPB * (b + 1))
                    v.tensor_copy(y_raw[:, :], y_bank[:, 0:YW]).then_inc(y_ready, 1)

            def finish_b(i, k):
                b = 2 * i + k // 3 - 1
                if k % 3 == 0 and there(b, B):
                    v.wait_ge(den_done, b + 1)
                    v.reciprocal(y_rec[:, 0:3 * SQ], bank_b[:, 0:3 * SQ])
                    v.reciprocal(y_rec[0:64, 3 * SQ:YW], bank_b[0:64, 3 * SQ:YW]).then_inc(rec_ready, 1)
                    v.wait_ge(rec_ready, b + 1)
                    wait(v, out_done, b)
                    v.tensor_tensor(t.yn[:, 0:3 * SQ], y_raw[:, 0:3 * SQ], y_rec[:, 0:3 * SQ], ALU.mult)
                    v.tensor_tensor(t.yn[0:64, 3 * SQ:YW], y_raw[0:64, 3 * SQ:YW], y_rec[0:64, 3 * SQ:YW],
                                    ALU.mult).then_inc(yn_ready, 1)

            def finish_c(i, k):
                b = 2 * i + k // 3 - 1
                if k % 3 == 0 and there(b, B):
                    par, pair = (1, i - 1) if k == 0 else (0, i)
                    r = slice(64 * par, 64 * par + SQ)
                    xb = t.x[r, pair, :] if isinstance(pair, int) else t.x[r, bass.ds(pair, 1), :].rearrange(
                        "p o d -> p (o d)")
                    v.wait_ge(out_done, b + 1)
                    v.tensor_tensor(o_tmp[r, :], bank_a[r, 0:D], t.const_row[r, :], ALU.add).then_inc(o_ready, 1)
                    v.wait_ge(o_ready, b + 1)
                    v.scalar_tensor_tensor(out=xb, in0=o_tmp[r, :], scalar=0.0, in1=xb, op0=ALU.max,
                                           op1=ALU.add).then_inc(x_ready, 1)

            def values(i, k):
                n, kk = at(i, k + 5), k + 5
                if there(n):
                    v.wait_ge(vals_done, n + 1)
                    wait(v, pv_done, NT * (n - 5))
                    va = t.v_aug[:, kk % PERIOD, :, :]
                    pv = bank_a[0:TK, :].rearrange("p (t c) -> p t c", t=NT)
                    v.tensor_tensor(va[:, :, 0:100].rearrange("p t (j c) -> p t j c", c=25)[:, :, :, 0:24],
                                    pv[:, :, 0:96].rearrange("p t (j c) -> p t j c", c=24),
                                    t.neg_bv[0:TK, 0:96].rearrange("p (j c) -> p j c", c=24).unsqueeze(1)
                                    .broadcast_to([TK, NT, 4, 24]), ALU.max)
                    v.tensor_tensor(va[:, :, 100:134].rearrange("p t (j c) -> p t j c", c=17)[:, :, :, 0:16],
                                    pv[:, :, 96:128].rearrange("p t (j c) -> p t j c", c=16),
                                    t.neg_bv[0:TK, 96:128].rearrange("p (j c) -> p j c", c=16).unsqueeze(1)
                                    .broadcast_to([TK, NT, 2, 16]), ALU.max).then_inc(v_ready, 1)

            def step(i, k):
                b = 2 * i + (k + 1) // 3
                if k % 3 == 2 and there(b, B):
                    v.wait_ge(max_read, HP * CPB * (b + 1))
                    wait(v, maxcut_ready, b)
                    wait(v, mrow_done, 2 * b)
                    v.tensor_reduce(max_cut[:, :, 0], max_part[:, (k + 1) // 3 % 2, :, :], AX_X, ALU.max,
                                    negate=True)
                    v.tensor_reduce(neg_max[:, :], max_part[:, (k + 1) // 3 % 2, :, :], AX_X, ALU.max,
                                    negate=True).then_inc(negmax_ready, 1)
                pair_max(i, k, 0)
                finish_a(i, k)
                pair_max(i, k, 1)
                pair_max(i, k, 2)
                pair_max(i, k, 3)
                pair_max(i, k, 4)
                pair_max(i, k, 5)
                values(i, k)
                finish_b(i, k)
                pair_max(i, k, 6)
                pair_max(i, k, 7)
                finish_c(i, k)

            steps(v, step)
            finish_a(NCH // PERIOD, 0)
            finish_b(NCH // PERIOD, 0)
            finish_c(NCH // PERIOD, 0)

        @block.tensor
        def _(pe):
            def scores(i, k, tile):
                n = at(i, k)
                if not there(n):
                    return
                if k % 3 == 0 and tile == 0:
                    b = 2 * i + k // 3
                    pe.wait_ge(qturn_ready, b + 1)
                    pe.wait_ge(shift_ready, 2 * (b + 1))
                for half in range(2):
                    j = 2 * NT * k + 2 * tile + half
                    wait(pe, probs_ready, 2 * NT * n + 2 * tile + half - 2)
                    for p in range(4):
                        g = 4 * half + p
                        m = pe.matmul(s_bank[j % 3][0:TK, PQ * p:PQ * (p + 1)],
                                      t.k_stack[:, k % PERIOD, g, TK * tile:TK * (tile + 1)],
                                      t.q_turn[:, k // 3 % 2, PQ * g:PQ * (g + 1)], start=True, stop=True)
                    m.then_inc(scores_done, 1)

            def max_scores(i, k, pair):
                n, kk = at(i, k + 4), k + 4
                if not there(n):
                    return
                if pair == 0:
                    pe.wait_ge(stack_loaded[kk % PERIOD], 16 * NSLOT * (i + kk // PERIOD + 1))
                    if kk % CPB == 0:
                        pe.wait_ge(qmax_ready, 2 * i + kk // CPB + 1)
                wait(pe, max_read, HP * n + pair - 1)
                pe.matmul(m_bank[pair % 2][0:PQ, 0:CH], q_max[:, kk // CPB % 2, PQ * pair:PQ * (pair + 1)],
                          t.k_stack[0:ROWS, kk % PERIOD, pair, :], start=True, stop=True).then_inc(maxs_done, 1)

            def pv(i, k, tile):
                n = at(i, k)
                if not there(n):
                    return
                first, last = k % 3 == 0 and tile == 0, k % 3 == 2 and tile == NT - 1
                if first:
                    wait(pe, y_ready, 2 * i + k // 3)
                if tile == 0:
                    pe.wait_ge(v_ready, n + 1)
                pe.wait_ge(probs_ready, 2 * NT * n + 2 * tile + 2)
                for head, cnt, col_tile, col, vcol in GROUPS:
                    wd = DK * cnt + 1
                    m = pe.matmul(y_bank[32 * col_tile:32 * col_tile + wd, col:col + SQ * cnt],
                                  t.v_aug[:, k % PERIOD, tile, vcol:vcol + wd],
                                  probs[:, (NT * k + tile) % 3, SQ * head:SQ * (head + cnt)],
                                  start=first and col == 0, stop=last, skip_group_check=True)
                m.then_inc(pv_done, 1)

            def turn(i, k):
                n = at(i, k + 6)
                if not there(n):
                    return
                pe.wait_ge(ctx_loaded[k % 3], 16 * (2 * i + (k + 6) // 3 + 1))
                wait(pe, v_ready, n - 1)
                if k % 3 == 1:
                    wait(pe, o_ready, 2 * i + k // 3)
                if k % 3 == 0:
                    wait(pe, shift_ready, 2 * (2 * i + k // 3) + 1)
                for tile in range(NT):
                    m = pe.transpose(bank_a[:, TK * tile:TK * (tile + 1)], c_in[:, k % 3, tile, :],
                                     t.ident[0:TK, 0:TK])
                m.then_inc(turned, 1)

            def keys(i, k):
                n = at(i, k + 6)
                if not there(n):
                    return
                pe.wait_ge(cT_ready, n + 1)
                wait(pe, k1_ready, n)
                if k % 3 == 1:
                    wait(pe, rec_ready, 2 * i + k // 3)
                if k % 3 == 0:
                    wait(pe, shift_ready, 2 * (2 * i + k // 3 + 1))
                pe.matmul(bank_b[:, 0:CH], t.wk[:, :], cT[:, k % 2, :], start=True, stop=True).then_inc(keys_done, 1)

            def values(i, k):
                n, kk = at(i, k + 5), k + 5
                if not there(n):
                    return
                if there(n + 1):
                    pe.wait_ge(cT_ready, n + 2)
                else:
                    pe.wait_ge(shift_ready, 2 * (2 * i + k // 3) + 1)
                for tile in range(NT):
                    m = pe.matmul(bank_a[0:TK, D * tile:D * (tile + 1)], cT[:, kk % 2, TK * tile:TK * (tile + 1)],
                                  t.wv[:, :], start=True, stop=True)
                m.then_inc(vals_done, 1)

            def max_rows(i, k):
                b = 2 * i + (k + 1) // 3
                if k % 3 != 2 or not there(b, B):
                    return
                pe.wait_ge(maxcut_ready, b + 1)
                n = at(i, k)
                if not there(n + 6):
                    pe.wait_ge(o_ready, b - 1)
                for half, bank in enumerate((bank_a, bank_b)):
                    if half == 0:
                        pe.wait_ge(v_ready, min_chunk(n + 6))
                    else:
                        pe.wait_ge(k1_ready, min_chunk(n + 7))
                    for p in range(4):
                        m = pe.matmul(bank[SHIFT:SHIFT + 3, PQ * p:PQ * (p + 1)], max_cut[:, 4 * half + p, :],
                                      t.ident_b[0:PQ, 0:PQ], start=True, stop=True)
                    m.then_inc(mrow_done, 1)

            def min_chunk(n):
                return min(n, NCH) if isinstance(n, int) else n

            def denominators(i, k):
                b = 2 * i + k // 3 - 1
                if k % 3 != 0 or not there(b, B):
                    return
                pe.wait_ge(y_ready, b + 1)
                pe.wait_ge(k1_ready, min_chunk(at(i, k + 7)))
                pe.matmul(bank_b[:, 0:3 * SQ], t.sel_a[:, :], y_raw[:, 0:3 * SQ], start=True, stop=True)
                pe.matmul(bank_b[0:64, 3 * SQ:YW], t.sel_b[:, :], y_raw[:, 3 * SQ:YW], start=True,
                          stop=True).then_inc(den_done, 1)

            def out_proj(i, k):
                b = 2 * i + k // 3 - 1
                if k % 3 != 0 or not there(b, B):
                    return
                r = 64 if k == 0 else 0
                pe.wait_ge(yn_ready, b + 1)
                pe.wait_ge(v_ready, min_chunk(at(i, k + 6)))
                for j in range(5):
                    m = pe.matmul(bank_a[r:r + SQ, 0:D], t.yn[:, SQ * j:SQ * (j + 1)], t.wo_rows[:, j, :],
                                  start=(j == 0), stop=(j == 4))
                m.then_inc(out_done, 1)

            def step(i, k):
                scores(i, k, 0)
                max_scores(i, k, 0)
                max_scores(i, k, 1)
                pv(i if k else i - 1, k - 1 if k else PERIOD - 1, 3)
                turn(i, k)
                scores(i, k, 1)
                max_scores(i, k, 2)
                max_scores(i, k, 3)
                keys(i, k)
                pv(i, k, 0)
                scores(i, k, 2)
                max_scores(i, k, 4)
                max_scores(i, k, 5)
                values(i, k)
                pv(i, k, 1)
                denominators(i, k)
                max_rows(i, k)
                scores(i, k, 3)
                max_scores(i, k, 6)
                max_scores(i, k, 7)
                pv(i, k, 2)
                out_proj(i, k)

            steps(pe, step)
            pv(NCH // PERIOD - 1, PERIOD - 1, 3)
            denominators(NCH // PERIOD, 0)
            out_proj(NCH // PERIOD, 0)


class Tiles:
    pass


def program(nc, ins, out):
    with ExitStack() as ctx:
        t = Tiles()

        def sb(name, shape, dt=F32):
            return ctx.enter_context(nc.sbuf_tensor(name, shape, dt))

        t.x = sb("x", [128, PAIRS, D])
        t.ident = sb("ident", [128, 128])
        with ExitStack() as attn:
            def sa(name, shape, dt=F32):
                return attn.enter_context(nc.sbuf_tensor(name, shape, dt))

            t.ident_b = sa("ident_b", [128, 128], BF16)
            t.wk = sa("wk", [D, D])
            t.bk = sa("bk", [D, 1])
            t.wv = sa("wv", [D, D])
            t.neg_bv = sa("neg_bv", [128, D])
            t.wo_rows = sa("wo_rows", [128, 5, D])
            t.const_row = sa("const_row", [128, D])
            t.sel_a = sa("sel_a", [128, 128])
            t.sel_b = sa("sel_b", [128, 64])
            t.yn = sa("yn", [128, YW])
            t.k_stack = sa("k_stack", [128, PERIOD, HP, CH], BF16)
            t.q_turn = sa("q_turn", [128, 2, HP * PQ], BF16)
            t.v_aug = sa("v_aug", [TK, PERIOD, NT, VW])
            t.q_stack = sa("q_stack", [ROWS, HP, 2, B, SQ], BF16)
            t.y_sum = attn.enter_context(nc.psum_tensor("y_sum", [128, 512], F32))
            setup(nc, ins, t)
            cross_attention(nc, ins, t)
        feed_forward(nc, ins, t, out)


def feed_forward(nc, ins, t, out):
    with ExitStack() as ctx:
        def sb(name, shape, dt=F32):
            return ctx.enter_context(nc.sbuf_tensor(name, shape, dt))

        def sem(name):
            return ctx.enter_context(nc.semaphore(name))

        xl = sb("xl", [128, PAIRS, D])
        nx = sb("nx", [128, PAIRS, D])
        sq = sb("sq", [128, PAIRS, D])
        st = sb("ff_st", [128, 8, PAIRS])
        nT = sb("nT", [D, W])
        q_head = sb("q_head", [D, FH, W])
        kT = sb("kT", [D, W])
        vc = sb("vc", [SQ, B, FDK])
        p = sb("p", [128, PAIRS * FH, SQ])
        pmax = sb("pmax", [128, PAIRS * FH])
        psum_ = sb("psum_", [128, PAIRS * FH])
        prec = sb("prec", [128, PAIRS * FH])
        pT = sb("pT", [SQ, PAIRS * FH, 128])
        oT = sb("oT", [D, W])
        hmask = sb("hmask", [D, FH])
        g1 = sb("g1", [D, 1])
        g2 = sb("g2", [D, 1])
        wq = sb("ff_wq", [D, D])
        wkc = sb("ff_wkc", [D, FH, FDK])
        wvc = sb("ff_wvc", [D, FDK])
        wo = sb("ff_wo", [D, D])
        wr = sb("ff_wr", [D, NE])
        ebias = sb("ebias", [128, NE])
        rank = sb("rank", [128, NE])
        rw = sb("rw", [128, PAIRS, NE])
        hot = sb("hot", [128, 2, PAIRS, NE])
        tmp = sb("tmp", [128, PAIRS, NE])
        rs = sb("rs", [128, 8, PAIRS])
        comb = sb("comb", [128, NE, PAIRS])
        comb_e = sb("comb_e", [128, 2, PAIRS])
        w1 = sb("w1", [D, 2, FF])
        w3 = sb("w3", [D, 2, FF])
        w2 = sb("w2", [FF, 2, D])
        th = sb("th", [FF, 2, 512])
        ga = sb("ga", [FF, 2, 512])
        hid = sb("hid", [FF, 2, 512])
        bank = [ctx.enter_context(nc.psum_tensor(f"ff_bank{i}", [128, 512], F32)) for i in range(8)]

        w_in = sem("ff_w_in")
        w_slot = [sem("w_slot0"), sem("w_slot1")]
        dve = sem("ff_dve")
        ranked = sem("ranked")
        sums_ready = sem("sums_ready")
        roots_ready = sem("roots_ready")
        nx_ready = sem("nx_ready")
        nx_turned = sem("nx_turned")
        nT_ready = sem("nT_ready")
        qk_done = sem("qk_done")
        q_taken = sem("q_taken")
        k_taken = sem("k_taken")
        vc_done = sem("vc_done")
        vc_taken = sem("vc_taken")
        s_done = sem("s_done")
        less_max = sem("less_max")
        p_exp = sem("p_exp")
        p_ready = sem("p_ready")
        p_turned = sem("p_turned")
        pT_ready = sem("pT_ready")
        o_done = sem("ff_o_done")
        oT_ready = sem("oT_ready")
        proj_done = sem("proj_done")
        xl_ready = sem("xl_ready")
        logit_done = sem("logit_done")
        r_less = sem("r_less")
        r_exp = sem("r_exp")
        gate_less = sem("gate_less")
        gate_exp = sem("gate_exp")
        up_done = sem("up_done")
        th_ready = sem("th_ready")
        ga_ready = sem("ga_ready")
        hid_ready = sem("hid_ready")
        down_done = sem("down_done")
        acc_ready = sem("acc_ready")
        comb_ready = sem("comb_ready")
        stored = sem("stored")

        up_bank, gate_bank, down_bank = bank[0:2], bank[2:4], bank[4:6]
        block = ctx.enter_context(nc.Block())

        @block.sync
        def _(sp):
            for dst, src in ((g1[:, :], ins["g1"]), (g2[:, :], ins["g2"]), (wq[:, :], ins["fWq"]),
                             (wvc[:, :], ins["Wvc"]), (wo[:, :], ins["fWo"]), (wr[:, :], ins["Wr"]),
                             (ebias[:, :], ins["eb"].partition_broadcast(128))):
                sp.dma_start(dst, src).then_inc(w_in, 16)
            for h in range(FH):
                sp.dma_start(wkc[:, h, :], ins["Wkc"]).then_inc(w_in, 16)
            for dst, src in ((w1, ins["sW1"]), (w3, ins["sW3"]), (w2, ins["sW2"])):
                sp.dma_start(dst[:, 1, :], src).then_inc(w_slot[1], 16)
            with sp.Fori(0, NE // 2) as i:
                for j in range(2):
                    e = sp.snap(2 * i + j)
                    sp.wait_ge(down_done, G * (i * 2 + j))
                    for dst, src in ((w1, ins["eW1"]), (w3, ins["eW3"]), (w2, ins["eW2"])):
                        sp.dma_start(dst[:, j, :], src[bass.ds(e, 1)].rearrange("o p f -> (o p) f"))\
                            .then_inc(w_slot[j], 16)
            for c in range(G):
                sp.wait_ge(acc_ready, G * NE + c + 1)
                for par in range(2):
                    sp.dma_start(out.rearrange("(n par) q d -> par q n d", par=2)[par][:, 4 * c:4 * c + 4, :],
                                 t.x[64 * par:64 * par + SQ, 4 * c:4 * c + 4, :]).then_inc(stored, 16)
            sp.wait_ge(w_in, 16 * 11)
            sp.wait_ge(stored, 16 * 2 * G)

        @block.gpsimd
        def _(g):
            for e in range(NE):
                m = g.memset(rank[:, e:e + 1], float(NE - e))
            m.then_inc(ranked, 1)

        @block.vector
        def _(v):
            links = [0]

            def chain(ins):
                links[0] += 1
                ins.then_inc(dve, 1)
                v.wait_ge(dve, links[0])

            def wide(a):
                return a.unsqueeze(2).broadcast_to([128, PAIRS, D])

            def mean_square(x, k, eps):
                chain(v.tensor_tensor(sq[:, :, :], x, x, ALU.mult))
                chain(v.tensor_reduce(st[:, k, :], sq[:, :, :], AX_X, ALU.add))
                v.tensor_scalar(st[:, k, :], st[:, k, :], 1.0 / D, eps, ALU.mult, ALU.add).then_inc(sums_ready, 1)

            def times_inverse_root(dst, src, k, n):
                v.wait_ge(roots_ready, n)
                chain(v.reciprocal(st[:, k, :], st[:, k, :]))
                return v.tensor_tensor(dst, src, wide(st[:, k, :]), ALU.mult)

            chain(v.tensor_reduce(st[:, 0, :], t.x[:, :, :], AX_X, ALU.add))
            chain(v.tensor_scalar(st[:, 0, :], st[:, 0, :], 1.0 / D, None, ALU.mult))
            chain(v.tensor_tensor(xl[:, :, :], t.x[:, :, :], wide(st[:, 0, :]), ALU.subtract))
            mean_square(xl[:, :, :], 1, EPS_LN)
            chain(times_inverse_root(xl[:, :, :], xl[:, :, :], 1, 1))
            mean_square(xl[:, :, :], 2, EPS_RMS)
            times_inverse_root(nx[:, :, :], xl[:, :, :], 2, 2).then_inc(nx_ready, 1)
            chain(v.tensor_reduce(hmask[:, :], t.ident[:, :].rearrange("p (h x) -> p h x", x=FDK), AX_X, ALU.add))
            chain(v.tensor_tensor(t.x[:, :, :], t.x[:, :, :], xl[:, :, :], ALU.add))
            for c in range(G):
                v.wait_ge(qk_done, 2 * c + 1)
                for h in range(FH):
                    m = v.tensor_scalar(q_head[:, h, 512 * c:512 * c + 512], bank[c][:, :], hmask[:, h:h + 1], None,
                                        ALU.mult)
                m.then_inc(q_taken, 1)
            for c in range(2):
                v.wait_ge(vc_done, c + 1)
                v.tensor_copy(vc[:, 16 * c:16 * c + 16, :], bank[c][0:SQ, :].rearrange("p (b d) -> p b d", d=FDK))\
                    .then_inc(vc_taken, 1)
            for c in range(8):
                r = slice(8 * c, 8 * c + 8)
                s = bank[(c + 2) % 8][:, 0:8 * SQ].rearrange("p (r k) -> p r k", k=SQ)
                v.wait_ge(s_done, c + 1)
                chain(v.tensor_reduce(pmax[:, r], s, AX_X, ALU.max))
                v.tensor_tensor(p[:, r, :], s, pmax[:, r].unsqueeze(2).broadcast_to([128, 8, SQ]), ALU.subtract)\
                    .then_inc(less_max, 1)
            for c in range(8):
                r = slice(8 * c, 8 * c + 8)
                v.wait_ge(p_exp, c + 1)
                chain(v.tensor_reduce(psum_[:, r], p[:, r, :], AX_X, ALU.add))
                chain(v.reciprocal(prec[:, r], psum_[:, r]))
                v.tensor_tensor(p[:, r, :], p[:, r, :], prec[:, r].unsqueeze(2).broadcast_to([128, 8, SQ]), ALU.mult)\
                    .then_inc(p_ready, 1)
            for c in range(G):
                v.wait_ge(proj_done, c + 1)
                x4 = (slice(None), slice(4 * c, 4 * c + 4), slice(None))
                o4 = bank[4 + c][:, :].rearrange("p (n d) -> p n d", d=D)
                chain(v.tensor_tensor(xl[x4], o4, xl[x4], ALU.add))
                v.tensor_tensor(t.x[x4], o4, t.x[x4], ALU.add).then_inc(xl_ready, 1)
            mean_square(xl[:, :, :], 3, EPS_RMS)
            times_inverse_root(nx[:, :, :], xl[:, :, :], 3, 3).then_inc(nx_ready, 1)
            e8 = [128, PAIRS, NE]
            lg = bank[7][:, 0:PAIRS * NE].rearrange("p (n e) -> p n e", e=NE)

            def over_experts(a):
                return a.unsqueeze(2).broadcast_to(e8)

            v.wait_ge(w_in, 16 * 11)
            v.wait_ge(ranked, 1)
            v.wait_ge(logit_done, 1)
            chain(v.tensor_tensor(rw[:, :, :], lg, ebias[:, :].unsqueeze(1).broadcast_to(e8), ALU.add))
            chain(v.tensor_reduce(rs[:, 0, :], rw[:, :, :], AX_X, ALU.max))
            v.tensor_tensor(rw[:, :, :], rw[:, :, :], over_experts(rs[:, 0, :]), ALU.subtract).then_inc(r_less, 1)
            v.wait_ge(r_exp, 1)
            chain(v.tensor_reduce(rs[:, 1, :], rw[:, :, :], AX_X, ALU.add))
            chain(v.reciprocal(rs[:, 2, :], rs[:, 1, :]))
            chain(v.tensor_tensor(rw[:, :, :], rw[:, :, :], over_experts(rs[:, 2, :]), ALU.mult))
            for k in range(2):
                top, first = rs[:, 3 + k, :], rs[:, 5, :]
                chain(v.tensor_reduce(top, rw[:, :, :], AX_X, ALU.max))
                chain(v.tensor_tensor(tmp[:, :, :], rw[:, :, :], over_experts(top), ALU.is_ge))
                chain(v.tensor_tensor(tmp[:, :, :], tmp[:, :, :], rank[:, :].unsqueeze(1).broadcast_to(e8), ALU.mult))
                chain(v.tensor_reduce(first, tmp[:, :, :], AX_X, ALU.max))
                chain(v.tensor_tensor(hot[:, k, :, :], tmp[:, :, :], over_experts(first), ALU.is_equal))
                if k == 0:
                    chain(v.scalar_tensor_tensor(out=rw[:, :, :], in0=hot[:, 0, :, :], scalar=-2.0, in1=rw[:, :, :],
                                                 op0=ALU.mult, op1=ALU.add))
            v.tensor_tensor(rs[:, 6, :], rs[:, 4, :], rs[:, 3, :], ALU.subtract).then_inc(gate_less, 1)
            v.wait_ge(gate_exp, 1)
            chain(v.tensor_scalar(rs[:, 7, :], rs[:, 6, :], 1.0, None, ALU.add))
            chain(v.reciprocal(rs[:, 0, :], rs[:, 7, :]))
            chain(v.tensor_tensor(rs[:, 1, :], rs[:, 6, :], rs[:, 0, :], ALU.mult))
            chain(v.tensor_tensor(tmp[:, :, :], hot[:, 0, :, :], over_experts(rs[:, 0, :]), ALU.mult))
            chain(v.tensor_tensor(rw[:, :, :], hot[:, 1, :, :], over_experts(rs[:, 1, :]), ALU.mult))
            chain(v.tensor_tensor(comb[:, :, :].rearrange("p e n -> p n e"), tmp[:, :, :], rw[:, :, :], ALU.add))

            def hidden(e, c):
                u = G * (e + 1) + c
                v.wait_ge(th_ready, u + 1)
                v.scalar_tensor_tensor(out=ga[:, c % 2, :], in0=th[:, c % 2, :], scalar=1.0,
                                       in1=gate_bank[c % 2][:, :], op0=ALU.add, op1=ALU.mult).then_inc(ga_ready, 1)
                v.wait_ge(ga_ready, u + 1)
                wait(v, down_done, u - 1)
                v.scalar_tensor_tensor(out=hid[:, c % 2, :], in0=up_bank[c % 2][:, :], scalar=0.5,
                                       in1=ga[:, c % 2, :], op0=ALU.mult, op1=ALU.mult).then_inc(hid_ready, 1)

            def collect(e, c, slot):
                u = G * (e + 1) + c
                v.wait_ge(down_done, u + 1)
                wait(v, acc_ready, u - 3)
                for n in range(4):
                    xs = t.x[:, 4 * c + n, :]
                    o = down_bank[c % 2][:, D * n:D * n + D]
                    if slot is None:
                        m = v.tensor_tensor(xs, o, xs, ALU.add)
                    else:
                        m = v.scalar_tensor_tensor(out=xs, in0=o, scalar=comb_e[:, slot, 4 * c + n:4 * c + n + 1],
                                                   in1=xs, op0=ALU.mult, op1=ALU.add)
                m.then_inc(acc_ready, 1)

            def weights(e, slot):
                ce = comb[:, bass.ds(e, 1), :].rearrange("p o n -> p (o n)")
                v.tensor_copy(comb_e[:, slot, :], ce).then_inc(comb_ready, 1)

            for c in range(G):
                hidden(-1, c)
                if c:
                    collect(-1, c - 1, None)
            v.wait_ge(down_done, G)
            collect(-1, G - 1, None)
            with v.Fori(0, NE // 2) as i:
                for j in range(2):
                    e = 2 * i + j
                    weights(e, j)
                    v.wait_ge(comb_ready, e + 1)
                    for c in range(G):
                        hidden(e, c)
                        if c:
                            collect(e, c - 1, j)
                    collect(e, G - 1, j)

        @block.scalar
        def _(a):
            def roots(k):
                a.wait_ge(sums_ready, k)
                a.activation(st[:, k, :], st[:, k, :], ACT.Sqrt).then_inc(roots_ready, 1)

            def turn(n, g):
                for c in range(G):
                    a.wait_ge(nx_turned, G * n + c + 1)
                    a.activation(nT[:, 512 * c:512 * c + 512], bank[c][:, :], ACT.Copy, scale=g)\
                        .then_inc(nT_ready, 1)

            roots(1)
            roots(2)
            a.wait_ge(w_in, 16 * 11)
            turn(0, g1[:, 0:1])
            for c in range(G):
                a.wait_ge(qk_done, 2 * c + 2)
                a.copy(kT[:, 512 * c:512 * c + 512], bank[4 + c][:, :]).then_inc(k_taken, 1)
            for c in range(8):
                a.wait_ge(less_max, c + 1)
                a.activation(p[:, 8 * c:8 * c + 8, :], p[:, 8 * c:8 * c + 8, :], ACT.Exp, scale=FDK ** -0.5)\
                    .then_inc(p_exp, 1)
            for c in range(PAIRS):
                a.wait_ge(p_turned, c + 1)
                a.copy(pT[:, FH * c:FH * c + FH, :], bank[c % 4][0:SQ, :].rearrange("p (h q) -> p h q", h=FH))\
                    .then_inc(pT_ready, 1)
            for c in range(G):
                a.wait_ge(o_done, c + 1)
                a.copy(oT[:, 512 * c:512 * c + 512], bank[4 + c][:, :]).then_inc(oT_ready, 1)
            roots(3)
            turn(1, g2[:, 0:1])
            a.wait_ge(r_less, 1)
            a.activation(rw[:, :, :], rw[:, :, :], ACT.Exp).then_inc(r_exp, 1)
            a.wait_ge(gate_less, 1)
            a.activation(rs[:, 6, :], rs[:, 6, :], ACT.Exp).then_inc(gate_exp, 1)

            def squash(e, c):
                u = G * (e + 1) + c
                a.wait_ge(up_done, u + 1)
                wait(a, ga_ready, u - 1)
                a.activation(th[:, c % 2, :], gate_bank[c % 2][:, :], ACT.Tanh, scale=0.5).then_inc(th_ready, 1)

            for c in range(G):
                squash(-1, c)
            with a.Fori(0, NE // 2) as i:
                for j in range(2):
                    for c in range(G):
                        squash(2 * i + j, c)

        @block.tensor
        def _(pe):
            def turn(n):
                pe.wait_ge(nx_ready, n + 1)
                for c in range(G):
                    for k in range(4):
                        m = pe.transpose(bank[c][:, 128 * k:128 * k + 128], nx[:, 4 * c + k, :], t.ident[:, :])
                    m.then_inc(nx_turned, 1)

            turn(0)
            for c in range(G):
                pe.wait_ge(nT_ready, c + 1)
                cols = nT[:, 512 * c:512 * c + 512]
                pe.matmul(bank[c][:, :], wq[:, :], cols, start=True, stop=True).then_inc(qk_done, 1)
                pe.matmul(bank[4 + c][:, :], wkc[:, :, :].rearrange("p h d -> p (h d)"), cols, start=True,
                          stop=True).then_inc(qk_done, 1)
            for c in range(2):
                pe.wait_ge(q_taken, c + 1)
                for b in range(16):
                    m = pe.matmul(bank[c][0:SQ, FDK * b:FDK * b + FDK],
                                  nT[:, 64 * (16 * c + b):64 * (16 * c + b) + SQ], wvc[:, :], start=True, stop=True)
                m.then_inc(vc_done, 1)
            pe.wait_ge(q_taken, G)
            pe.wait_ge(k_taken, G)
            for c in range(8):
                if c >= 6:
                    pe.wait_ge(vc_taken, c - 5)
                for n in range(2):
                    for h in range(FH):
                        for par in range(2):
                            tok = 64 * (2 * (2 * c + n) + par)
                            m = pe.matmul(bank[(c + 2) % 8][64 * par:64 * par + 64,
                                                            SQ * (FH * n + h):SQ * (FH * n + h) + SQ],
                                          q_head[:, h, tok:tok + 64], kT[:, tok:tok + SQ], start=True, stop=True)
                m.then_inc(s_done, 1)
            pe.wait_ge(less_max, 8)
            for c in range(PAIRS):
                pe.wait_ge(p_ready, c // 2 + 1)
                if c >= 4:
                    pe.wait_ge(pT_ready, c - 3)
                for h in range(FH):
                    m = pe.transpose(bank[c % 4][0:SQ, 128 * h:128 * h + 128], p[:, FH * c + h, :], t.ident[:, :])
                m.then_inc(p_turned, 1)
            for c in range(G):
                pe.wait_ge(pT_ready, 4 * c + 4)
                for n in range(4):
                    for par in range(2):
                        for h in range(FH):
                            col = 64 * (2 * n + par)
                            m = pe.matmul(bank[4 + c][FDK * h:FDK * h + FDK, col:col + 64],
                                          vc[:, 2 * (4 * c + n) + par, :],
                                          pT[:, FH * (4 * c + n) + h, 64 * par:64 * par + 64], start=True, stop=True)
                m.then_inc(o_done, 1)
            for c in range(G):
                pe.wait_ge(oT_ready, c + 1)
                for n in range(4):
                    tok = 128 * (4 * c + n)
                    m = pe.matmul(bank[4 + c][:, D * n:D * n + D], oT[:, tok:tok + 128], wo[:, :], start=True,
                                  stop=True)
                m.then_inc(proj_done, 1)
            turn(1)
            pe.wait_ge(nT_ready, 2 * G)
            pe.wait_ge(xl_ready, G)
            for n in range(PAIRS):
                m = pe.matmul(bank[7][:, NE * n:NE * n + NE], nT[:, 128 * n:128 * n + 128], wr[:, :], start=True,
                              stop=True)
            m.then_inc(logit_done, 1)

            def up(e, c, slot):
                u = G * (e + 1) + c
                wait(pe, hid_ready, u - 1)
                cols = nT[:, 512 * c:512 * c + 512]
                pe.matmul(gate_bank[c % 2][:, :], w1[:, slot, :], cols, start=True, stop=True)
                pe.matmul(up_bank[c % 2][:, :], w3[:, slot, :], cols, start=True, stop=True).then_inc(up_done, 1)

            def down(e, c, slot):
                u = G * (e + 1) + c
                pe.wait_ge(hid_ready, u + 1)
                wait(pe, acc_ready, u - 1)
                for n in range(4):
                    m = pe.matmul(down_bank[c % 2][:, D * n:D * n + D], hid[:, c % 2, 128 * n:128 * n + 128],
                                  w2[:, slot, :], start=True, stop=True)
                m.then_inc(down_done, 1)

            pe.wait_ge(w_slot[1], 16 * 3)
            for c in range(G):
                up(-1, c, 1)
                if c:
                    down(-1, c - 1, 1)
            down(-1, G - 1, 1)
            with pe.Fori(0, NE // 2) as i:
                for j in range(2):
                    pe.wait_ge(w_slot[j], 16 * 3 * (i + 1 + j))
                    for c in range(G):
                        up(2 * i + j, c, j)
                        if c:
                            down(2 * i + j, c - 1, j)
                    down(2 * i + j, G - 1, j)


def _layouts(a):
    import numpy as np
    c = np.ascontiguousarray
    f = {k: np.asarray(x) for k, x in a.items()}
    qcols = np.arange(D).reshape(HP, 2, DK).transpose(1, 2, 0).reshape(D)
    return {
        "x": c(f["x"]), "ctx": c(f["ctx_1024"]),
        "Wq": c(f["L0_xattn_Wq"][:, qcols]), "bq": c(f["L0_xattn_bq"][qcols].reshape(D, 1)),
        "Wk": c(f["L0_xattn_Wk"][:, qcols]), "bk": c(f["L0_xattn_bk"][qcols].reshape(D, 1)),
        "Wv": c(f["L0_xattn_Wv"]), "bv": c(f["L0_xattn_bv"].reshape(1, D)),
        "Wo": c(f["L0_xattn_Wo"]), "bo": c(f["L0_xattn_bo"].reshape(1, D)),
        "g1": c(f["L0_ffn_g1"].reshape(D, 1)), "g2": c(f["L0_ffn_g2"].reshape(D, 1)),
        "fWq": c(f["L0_ffn_Wq"].T), "Wkc": c(f["L0_ffn_Wkc"].T), "Wvc": c(f["L0_ffn_Wvc"].T),
        "fWo": c(f["L0_ffn_Wo"].T), "Wr": c(f["L0_ffn_Wr"].T), "eb": c(f["L0_ffn_expert_bias"].reshape(1, NE)),
        "sW1": c(f["L0_ffn_sW1"].T), "sW2": c(f["L0_ffn_sW2"].T), "sW3": c(f["L0_ffn_sW3"].T),
        "eW1": c(f["L0_ffn_eW1"].transpose(0, 2, 1)), "eW2": c(f["L0_ffn_eW2"].transpose(0, 2, 1)),
        "eW3": c(f["L0_ffn_eW3"].transpose(0, 2, 1)),
    }


def kernel(**inputs):
    import concourse.bacc as _bacc
    from concourse.bass_utils import run_bass_kernel_spmd as _run

    nc = _bacc.Bacc("TRN2", target_bir_lowering=False, num_devices=1)
    arrays, aps = {}, {}
    for name, a in _layouts(inputs).items():
        arrays[f"in_{name}"] = a
        aps[name] = nc.dram_tensor(f"in_{name}", a.shape, F32, kind="ExternalInput").ap()
    out = nc.dram_tensor("out_0", (B, SQ, D), F32, kind="ExternalOutput").ap()
    program(nc, aps, out)
    r = _run(nc, [arrays], core_ids=[0])
    return r.results[0]["out_0"]
```

```python
import concourse.bass as bass
from concourse import mybir
from contextlib import ExitStack

F32 = mybir.dt.float32
BF16 = mybir.dt.bfloat16
U32 = mybir.dt.uint32
ALU = mybir.AluOpType
ACT = mybir.ActivationFunctionType
AX_X = mybir.AxisListType.X

D = 128
B, SQ, SK = 32, 56, 1500
H, DK = 16, 8
HP = H // 2
PQ = 2 * SQ
CH = 500
TK = 125
NT = CH // TK
CPB = SK // CH
NCH = B * CPB
PERIOD = 2 * CPB
PAIRS = B // 2
HALF = HP // 2 * PQ
K_PART = [0, 0, 0, 1, 1, 2]
Q_PART = [0, 1, 2, 0, 1, 0]
NSLOT = len(K_PART)
ROWS = 16 * NSLOT
SHIFT = ROWS
SCALE = DK ** -0.5
TWO_ONES = 0x3F803F80
EPS_LN, EPS_RMS = 1e-5, 1e-6

GROUPS = [(0, 3, 0, 0, 0), (3, 3, 1, 0, 25), (6, 3, 2, 0, 50), (9, 3, 3, 0, 75),
          (12, 2, 0, 3 * SQ, 100), (14, 2, 1, 3 * SQ, 117)]
VW = 134
YW = 5 * SQ
OUT_COL = 128

FH, FDK = 4, 32
NE, FF = 8, 128
W = 64 * B
G = W // 512
SLOTS = 3
UNITS = SLOTS * G


def wait(eng, sem, value):
    if not isinstance(value, int) or value > 0:
        eng.wait_ge(sem, value)


def there(n, count=NCH):
    return not isinstance(n, int) or 0 <= n < count


def cross_attention(nc, ins, t):
    with ExitStack() as ctx:
        def sb(name, shape, dt=F32):
            return ctx.enter_context(nc.sbuf_tensor(name, shape, dt))

        def pb(name):
            return ctx.enter_context(nc.psum_tensor(name, [128, 512], F32))

        def sem(name):
            return ctx.enter_context(nc.semaphore(name))

        cT = sb("cT", [D, 3, CH])
        k32 = sb("k32", [D, 2, CH])
        k_res = sb("k_res", [D, CH])
        kp = sb("kp", [D, 3, 3, CH], BF16)
        probs = sb("probs", [128, 3, H * SQ])
        q_max = sb("q_max", [ROWS, 2, HP * PQ], BF16)
        max_part = sb("max_part", [PQ, 2, HP, CPB])
        neg_max = sb("neg_max", [PQ, HP])
        max_res = sb("max_res", [PQ, HP])
        max_cut = sb("max_cut", [PQ, HP, 3], BF16)
        y_raw = sb("y_raw", [128, YW])
        y_rec = sb("y_rec", [SQ, H])
        yn = sb("yn", [128, D])
        ynT = sb("ynT", [D, SQ])
        o_tmp = sb("o_tmp", [128, D])
        x_new = sb("x_new", [128, D])
        x_stats = sb("x_stats", [128, 6])
        mv_new = sb("mv_new", [128, 2])

        bq = sb("bq", [D, 1])
        bv_col = sb("bv_col", [D, 1])
        bv_wide = sb("bv_wide", [D, D])
        bo_row = sb("bo_row", [D, D])
        wq = sb("wq", [D, D])
        st = sb("st", [128, 6, PAIRS])
        stats = sb("stats", [128, PAIRS, 6])
        mv0 = sb("mv0", [128, PAIRS, 2])
        qp = sb("qp", [D, 3, B, SQ], BF16)
        xn = probs[:, :, :].rearrange("p s c -> p (s c)")[:, 0:PAIRS * D].rearrange("p (n d) -> p n d", d=D)
        early = t.k_stack[:, PERIOD // 2:PERIOD, :, :].rearrange("p s g c -> p (s g c)").bitcast(F32)
        xnT = early[:, 0:W].rearrange("p (n h q) -> p n h q", h=2, q=64)
        q32 = early[:, W:W + B * SQ].rearrange("p (b q) -> p b q", q=SQ)
        qres = early[:, W + B * SQ:W + 2 * B * SQ].rearrange("p (b q) -> p b q", q=SQ)

        s_bank = [pb(f"s_bank{i}") for i in range(3)]
        m_bank = [pb(f"m_bank{i}") for i in range(2)]
        bank_a = pb("bank_a")
        bank_b = pb("bank_b")
        y_bank = t.y_sum
        ps = s_bank + m_bank

        x_in = sem("x_in")
        w_in = sem("w_in")
        dve = sem("dve_chain")
        pool = sem("pool_chain")
        ident = sem("ident_ready")
        ones_ready = sem("ones_ready")
        ones_spread = sem("ones_spread")
        var_done = sem("var_done")
        std_done = sem("std_done")
        xn_done = sem("xn_done")
        xT_done = sem("xT_done")
        xT_copied = sem("xT_copied")
        q_done = sem("q_done")
        q_ready = sem("q_ready")
        q_cut = sem("q_cut")
        q_zero = sem("q_zero")
        q_stacked = sem("q_stacked")
        c_done = sem("c_done")
        bvw = sem("bvw")

        ctx_loaded = [sem(f"ctx_loaded{i}") for i in range(3)]
        stack_loaded = [sem(f"stack_loaded{i}") for i in range(PERIOD)]
        keys_done = sem("keys_done")
        vals_done = sem("vals_done")
        maxs_done = sem("maxs_done")
        scores_done = sem("scores_done")
        pv_done = sem("pv_done")
        mrow_done = sem("mrow_done")
        y_turned = sem("y_turned")
        yn_turned = sem("yn_turned")
        out_done = sem("out_done")
        k32_ready = sem("k32_ready")
        k1_ready = sem("k1_ready")
        probs_ready = sem("probs_ready")
        shift_ready = sem("shift_ready")
        v_ready = sem("v_ready")
        max_read = sem("max_read")
        neg_chain = sem("neg_chain")
        y_ready = sem("y_ready")
        rec_ready = sem("rec_ready")
        ynT_ready = sem("ynT_ready")
        yn_ready = sem("yn_ready")
        o_ready = sem("o_ready")
        stats_ready = sem("stats_ready")
        mv_ready = sem("mv_ready")
        x_ready = sem("x_ready")
        maxcut_ready = sem("maxcut_ready")
        res_ready = sem("res_ready")
        kcut_ready = sem("kcut_ready")
        qmax_ready = sem("qmax_ready")
        qturn_ready = sem("qturn_ready")

        def at(i, k):
            return i * PERIOD + k

        def steps(eng, step):
            for k in range(PERIOD):
                step(-1, k)
            for k in range(PERIOD):
                step(0, k)
            with eng.Fori(1, NCH // PERIOD - 1) as i:
                for k in range(PERIOD):
                    step(i, k)
            for k in range(PERIOD):
                step(NCH // PERIOD - 1, k)

        block = ctx.enter_context(nc.Block())

        @block.sync
        def _(sp):
            def load_ctx(i, k):
                n = at(i, k)
                if there(n):
                    if isinstance(n, int):
                        src = ins["ctx"][n]
                    else:
                        src = ins["ctx"][bass.ds(sp.snap(n), 1)].rearrange("o d s -> (o d) s")
                    if isinstance(n, int) and n < 3:
                        return
                    wait(sp, vals_done, n - 2)
                    sp.dma_start(cT[:, k % 3, :], src).then_inc(ctx_loaded[k % 3], 16)

            def step(i, k):
                load_ctx(i, k + 6)
                n = at(i, k + 5)
                if isinstance(n, int) and 1 <= n < PERIOD:
                    sp.wait_ge(ones_ready, 1)
                    sp.dma_start(t.k_stack[SHIFT:128, n, :, :], t.k_stack[SHIFT:128, 0, :, :])\
                        .then_inc(ones_spread, 16)
                if there(n):
                    wait(sp, scores_done, 2 * NT * (n - 5))
                    sp.wait_ge(kcut_ready, n + 1)
                    for s in range(NSLOT):
                        sp.dma_start(t.k_stack[16 * s:16 * s + 16, (k + 5) % PERIOD, :, :],
                                     kp[:, (k + 5) % 3, K_PART[s], :]).then_inc(stack_loaded[(k + 5) % PERIOD], 16)

            x_rows = ins["x"].rearrange("(n par) q d -> par q n d", par=2)
            for par in range(2):
                sp.dma_start(t.x[64 * par:64 * par + SQ, :, :], x_rows[par]).then_inc(x_in, 16)
                sp.dma_start(t.x[64 * par + SQ:64 * par + 64, :, :], x_rows[par][0:64 - SQ]).then_inc(x_in, 16)
            for dst, src in ((wq[:, :], ins["Wq"]), (bq[:, :], ins["bq"]), (t.wk[:, :], ins["Wk"]),
                             (t.bk[:, :], ins["bk"])):
                sp.dma_start(dst, src).then_inc(w_in, 16)
            for n in range(3):
                sp.dma_start(cT[:, n, :], ins["ctx"][n]).then_inc(ctx_loaded[n], 16)
            for dst, src in ((t.wv[:, :], ins["Wv"]), (t.wo[:, :], ins["Wo"]),
                             (bv_col[:, :], ins["bv"].rearrange("a d -> d a")),
                             (t.neg_bv[:, :], ins["bv"].partition_broadcast(128)),
                             (bo_row[:, :], ins["bo"].partition_broadcast(128))):
                sp.dma_start(dst, src).then_inc(w_in, 16)
            sp.wait_ge(q_zero, 2)
            sp.wait_ge(q_ready, G)
            sp.wait_ge(q_cut, 1)
            for s in range(NSLOT):
                for h2 in range(2):
                    r = 16 * s + 8 * h2
                    sp.dma_start(t.q_stack[r:r + 8, :, h2, :, :].rearrange("p g b q -> p g (b q)"),
                                 qp[64 * h2:64 * h2 + 64, Q_PART[s], :, :].rearrange("p b q -> p (b q)"))\
                        .then_inc(q_stacked, 16)
            steps(sp, step)
            sp.wait_ge(w_in, 16 * 9)

        @block.gpsimd
        def _(g):
            g.memset(t.ident[:, :], 0.0).then_inc(pool, 1)
            g.wait_ge(pool, 1)
            g.affine_select(out=t.ident[:, :], in_=t.ident[:, :], compare_op=ALU.not_equal, fill=1.0, base=0,
                            pattern=[[-1, 128]], channel_multiplier=1).then_inc(ident, 1)
            g.wait_ge(ident, 1)
            g.memset(t.k_stack[SHIFT:128, 0, :, :].bitcast(U32), TWO_ONES).then_inc(ones_ready, 1)
            for c in range(2):
                g.wait_ge(ones_ready, 1)
                z = t.q_stack[:, 4 * c:4 * c + 4, :, :, :].bitcast(U32)
                g.memset(z, 0).then_inc(q_zero, 1)
            g.wait_ge(q_zero, 2)
            g.memset(t.q_turn[SHIFT:128, :, :], 0.0).then_inc(pool, 1)
            g.wait_ge(pool, 2)

            def step(i, k):
                b = 2 * i + (k + 6) // 3
                if k % 3 == 0 and there(b, B):
                    wait(g, maxs_done, HP * CPB * (b - 1))
                b = 2 * i + k // 3 + 1
                if k % 3 == 1 and there(b, B):
                    wait(g, scores_done, 2 * NT * CPB * (b - 1))
                n = at(i, k + 6)
                if there(n):
                    g.wait_ge(k1_ready, n + 1)
                    wait(g, kcut_ready, n)
                    g.tensor_tensor(kp[:, k % 3, 1, :], k32[:, k % 2, :], kp[:, k % 3, 0, :], ALU.subtract)
                    g.tensor_tensor(k_res[:, :], k32[:, k % 2, :], kp[:, k % 3, 0, :], ALU.subtract)\
                        .then_inc(res_ready, 1)
                    g.wait_ge(res_ready, n + 1)
                    g.tensor_tensor(kp[:, k % 3, 2, :], k_res[:, :], kp[:, k % 3, 1, :], ALU.subtract)\
                        .then_inc(kcut_ready, 1)
                b, kb = 2 * i + (k + 6) // 3, (k + 6) // 3
                if k % 3 == 0 and there(b, B):
                    if isinstance(b, int) and b == 0:
                        g.wait_ge(q_stacked, 16 * 2 * NSLOT)
                    g.tensor_copy(grid(q_max[:, kb % 2, :]), q_rows(b)).then_inc(qmax_ready, 1)
                b, kb = 2 * i + k // 3 + 1, k // 3 + 1
                if k % 3 == 1 and there(b, B):
                    g.tensor_copy(grid(t.q_turn[0:ROWS, kb % 2, :]), q_rows(b)).then_inc(qturn_ready, 1)

            def grid(a):
                return a.rearrange("p (g q) -> p g q", q=SQ)

            def q_rows(b):
                a = t.q_stack[:, :, :, :, :].rearrange("p g h b q -> p (g h) b q")
                if isinstance(b, int):
                    return a[:, :, b, :]
                return a[:, :, bass.ds(b, 1), :].rearrange("p g o q -> p g (o q)")

            steps(g, step)

        @block.scalar
        def _(a):
            def exp(i, k, tile, half):
                n = at(i, k)
                if there(n):
                    j = 2 * NT * k + 2 * tile + half
                    a.wait_ge(scores_done, 2 * NT * n + 2 * tile + half + 1)
                    if half == 0:
                        wait(a, pv_done, NT * n + tile - 2)
                    a.activation(probs[0:TK, (NT * k + tile) % 3, HALF * half:HALF * (half + 1)],
                                 s_bank[j % 3][0:TK, 0:HALF], ACT.Exp, scale=SCALE).then_inc(probs_ready, 1)

            a.wait_ge(var_done, 1)
            a.activation(st[:, 1, :], st[:, 0, :], ACT.Sqrt).then_inc(std_done, 1)
            for c in range(G):
                a.wait_ge(xT_done, c + 1)
                a.copy(xnT[:, 4 * c:4 * c + 4, :, :], ps[c][:, :].rearrange("p (n h q) -> p n h q", n=4, h=2)
                       ).then_inc(xT_copied, 1)
            a.wait_ge(w_in, 16 * 9)
            for c in range(G):
                a.wait_ge(q_done, c + 1)
                q_psum = ps[c][:, 0:8 * SQ].rearrange("p (b q) -> p b q", b=8)
                a.activation(q32[:, 8 * c:8 * c + 8, :], q_psum, ACT.Relu, bias=bq[:, 0:1])
                a.activation(qp[:, 0, 8 * c:8 * c + 8, :], q_psum, ACT.Relu, bias=bq[:, 0:1]).then_inc(q_ready, 1)

            def turn_back(i, k):
                b = 2 * i + k // 3 - 1
                if k % 3 == 1 and there(b, B):
                    a.wait_ge(yn_turned, b + 1)
                    wait(a, out_done, b)
                    a.copy(ynT[:, :], bank_b[:, 0:SQ]).then_inc(ynT_ready, 1)

            def step(i, k):
                n = at(i, k + 6)
                exp(i, k, 0, 0)
                exp(i, k, 0, 1)
                turn_back(i, k)
                exp(i, k, 1, 0)
                exp(i, k, 1, 1)
                if there(n):
                    a.wait_ge(keys_done, n + 1)
                    wait(a, kcut_ready, n - 1)
                    a.activation(k32[:, k % 2, :], bank_b[:, 0:CH], ACT.Relu, bias=t.bk[:, 0:1])\
                        .then_inc(k32_ready, 1)
                    wait(a, stack_loaded[(k + 3) % PERIOD], 16 * NSLOT * (i + (k + 3) // PERIOD + 1)
                         if there(at(i, k + 3)) else 0)
                    a.activation(kp[:, k % 3, 0, :], bank_b[:, 0:CH], ACT.Relu, bias=t.bk[:, 0:1])\
                        .then_inc(k1_ready, 1)
                exp(i, k, 2, 0)
                exp(i, k, 2, 1)
                b = 2 * i + (k + 1) // 3
                if k % 3 == 2 and there(b, B):
                    for half, bank in enumerate((bank_a, bank_b)):
                        a.wait_ge(mrow_done, 2 * b + half + 1)
                        a.copy(t.q_turn[SHIFT:SHIFT + 3, (k + 1) // 3 % 2, HALF * half:HALF * (half + 1)],
                               bank[SHIFT:SHIFT + 3, 0:HALF]).then_inc(shift_ready, 1)
                exp(i, k, 3, 0)
                exp(i, k, 3, 1)

            steps(a, step)
            turn_back(NCH // PERIOD, 1)

        @block.vector
        def _(v):
            def pair_max(i, k, pair):
                n, kk = at(i, k + 4), k + 4
                if there(n):
                    v.wait_ge(maxs_done, HP * n + pair + 1)
                    v.tensor_reduce(max_part[:, kk // CPB % 2, pair, kk % CPB:kk % CPB + 1],
                                    m_bank[pair % 2][0:PQ, 0:CH], AX_X, ALU.max).then_inc(max_read, 1)

            def finish_a(i, k):
                b = 2 * i + k // 3 - 1
                if k % 3 == 0 and there(b, B):
                    v.wait_ge(pv_done, NT * CPB * (b + 1))
                    v.tensor_copy(y_raw[:, :], y_bank[:, 0:YW]).then_inc(y_ready, 1)

            def finish_b(i, k):
                b = 2 * i + k // 3 - 1
                if k % 3 == 0 and there(b, B):
                    v.wait_ge(y_turned, b + 1)
                    wait(v, yn_turned, b)
                    for heads, tiles, first, col in ((3, 4, 0, 0), (2, 2, 12, 3 * 128)):
                        width = 32 * tiles
                        blocks = bank_b[0:SQ, col:col + heads * width].rearrange(
                            "p (j t c) -> p j t c", j=heads, t=tiles)
                        at_rec = y_rec[:, first:first + heads * tiles].rearrange("p (j t) -> p j t", j=heads)
                        v.reciprocal(at_rec, blocks[:, :, :, DK * heads]).then_inc(rec_ready, 1)
                    v.wait_ge(rec_ready, 2 * (b + 1))
                    for heads, tiles, first, col in ((3, 4, 0, 0), (2, 2, 12, 3 * 128)):
                        width = 32 * tiles
                        for j in range(heads):
                            src = bank_b[0:SQ, col + j * width:col + (j + 1) * width].rearrange(
                                "p (t c) -> p t c", t=tiles)[:, :, DK * j:DK * (j + 1)]
                            rec = y_rec[:, first + j * tiles:first + (j + 1) * tiles]
                            out = yn[0:SQ, DK * first:DK * (first + heads * tiles)].rearrange(
                                "p (t c) -> p t c", t=tiles)[:, :, DK * j:DK * (j + 1)]
                            m = v.tensor_tensor(out, src, rec.unsqueeze(2).broadcast_to([SQ, tiles, DK]), ALU.mult)
                    m.then_inc(yn_ready, 1)

            def finish_c(i, k):
                b = 2 * i + k // 3 - 1
                if k % 3 == 1 and there(b, B):
                    par, pair = (1, i - 1) if k == 1 else (0, i)
                    r = slice(64 * par, 64 * par + SQ)
                    xb = t.x[r, pair, :] if isinstance(pair, int) else t.x[r, bass.ds(pair, 1), :].rearrange(
                        "p o d -> p (o d)")
                    v.wait_ge(out_done, b + 1)
                    v.tensor_tensor(o_tmp[r, :], bank_b[r, OUT_COL:OUT_COL + D], t.const_row[r, :], ALU.add)\
                        .then_inc(o_ready, 1)
                    v.wait_ge(o_ready, b + 1)
                    v.scalar_tensor_tensor(out=x_new[r, :], in0=o_tmp[r, :], scalar=0.0, in1=xb, op0=ALU.max,
                                           op1=ALU.add).then_inc(x_ready, 1)
                    v.scalar_tensor_tensor(out=xb, in0=o_tmp[r, :], scalar=0.0, in1=xb, op0=ALU.max, op1=ALU.add)
                    v.wait_ge(x_ready, b + 1)

            def statistics_a(i, k):
                b = 2 * i + k // 3 - 1
                if k % 3 == 1 and there(b, B):
                    r = slice(64, 64 + SQ) if k == 1 else slice(0, SQ)
                    v.bn_stats(x_stats[r, :], x_new[r, :]).then_inc(stats_ready, 1)
                    v.wait_ge(stats_ready, b + 1)

            def statistics_b(i, k):
                b = 2 * i + k // 3 - 1
                if k % 3 == 1 and there(b, B):
                    r = slice(64, 64 + SQ) if k == 1 else slice(0, SQ)
                    v.bn_aggr(mv_new[r, :], x_stats[r, :]).then_inc(mv_ready, 1)
                    v.wait_ge(mv_ready, b + 1)

            def statistics_c(i, k):
                b = 2 * i + k // 3 - 1
                if k % 3 == 1 and there(b, B):
                    r, pair = (slice(64, 64 + SQ), i - 1) if k == 1 else (slice(0, SQ), i)
                    mv = t.mv[r, pair, :] if isinstance(pair, int) else t.mv[r, bass.ds(pair, 1), :].rearrange(
                        "p o d -> p (o d)")
                    v.tensor_copy(mv, mv_new[r, :])

            def values(i, k):
                n, kk = at(i, k + 5), k + 5
                if there(n):
                    v.wait_ge(vals_done, n + 1)
                    wait(v, pv_done, NT * (n - 5))
                    va = t.v_aug[:, kk % PERIOD, :, :]
                    pv = bank_a[0:TK, :].rearrange("p (t c) -> p t c", t=NT)
                    v.tensor_tensor(va[:, :, 0:100].rearrange("p t (j c) -> p t j c", c=25)[:, :, :, 0:24],
                                    pv[:, :, 0:96].rearrange("p t (j c) -> p t j c", c=24),
                                    t.neg_bv[0:TK, 0:96].rearrange("p (j c) -> p j c", c=24).unsqueeze(1)
                                    .broadcast_to([TK, NT, 4, 24]), ALU.max)
                    v.tensor_tensor(va[:, :, 100:134].rearrange("p t (j c) -> p t j c", c=17)[:, :, :, 0:16],
                                    pv[:, :, 96:128].rearrange("p t (j c) -> p t j c", c=16),
                                    t.neg_bv[0:TK, 96:128].rearrange("p (j c) -> p j c", c=16).unsqueeze(1)
                                    .broadcast_to([TK, NT, 2, 16]), ALU.max).then_inc(v_ready, 1)

            def step(i, k):
                parts_of_max(i, k)
                pair_max(i, k, 0)
                finish_a(i, k)
                pair_max(i, k, 1)
                finish_c(i, k)
                pair_max(i, k, 2)
                statistics_a(i, k)
                pair_max(i, k, 3)
                statistics_b(i, k)
                pair_max(i, k, 4)
                statistics_c(i, k)
                values(i, k)
                pair_max(i, k, 5)
                finish_b(i, k)
                pair_max(i, k, 6)
                pair_max(i, k, 7)

            def parts_of_max(i, k):
                b = 2 * i + (k + 1) // 3
                if k % 3 != 2 or not there(b, B):
                    return
                maxima = max_part[:, (k + 1) // 3 % 2, :, :]
                v.wait_ge(max_read, HP * CPB * (b + 1))
                wait(v, mrow_done, 2 * b)
                v.tensor_reduce(max_cut[:, :, 0], maxima, AX_X, ALU.max, negate=True)
                v.tensor_reduce(neg_max[:, :], maxima, AX_X, ALU.max, negate=True).then_inc(neg_chain, 1)
                v.wait_ge(neg_chain, 2 * b + 1)
                v.tensor_tensor(max_cut[:, :, 1], neg_max[:, :], max_cut[:, :, 0], ALU.subtract)
                v.tensor_tensor(max_res[:, :], neg_max[:, :], max_cut[:, :, 0], ALU.subtract).then_inc(neg_chain, 1)
                v.wait_ge(neg_chain, 2 * b + 2)
                v.tensor_tensor(max_cut[:, :, 2], max_res[:, :], max_cut[:, :, 1], ALU.subtract)\
                    .then_inc(maxcut_ready, 1)

            links = [0]

            def chain(ins):
                links[0] += 1
                ins.then_inc(dve, 1)
                v.wait_ge(dve, links[0])

            v.memset(t.v_aug[:, :, :, 24:100:25], 1.0)
            v.memset(t.v_aug[:, :, :, 116:134:17], 1.0)
            v.memset(t.y_sum[:, :], 0.0)
            v.memset(yn[:, :], 0.0)
            v.memset(t.mv[:, :, :], 0.0)
            v.wait_ge(ident, 1)
            v.tensor_copy(t.ident_b[:, :], t.ident[:, :])
            v.wait_ge(x_in, 64)
            for n in range(PAIRS):
                m = v.bn_stats(stats[:, n, :], t.x[:, n, :])
            chain(m)
            for n in range(PAIRS):
                m = v.bn_aggr(mv0[:, n, :], stats[:, n, :])
            chain(m)
            v.tensor_scalar(st[:, 0, :], mv0[:, :, 1], EPS_LN, None, ALU.add).then_inc(var_done, 1)
            chain(v.tensor_copy(st[:, 2, :], mv0[:, :, 0]))

            def of_rows(k, c):
                return st[:, k, 4 * c:4 * c + 4].unsqueeze(2).broadcast_to([128, 4, D])

            for c in range(G):
                r = slice(4 * c, 4 * c + 4)
                m = v.tensor_tensor(xn[:, r, :], t.x[:, r, :], of_rows(2, c), ALU.subtract)
            chain(m)
            v.wait_ge(std_done, 1)
            chain(v.reciprocal(st[:, 3, :], st[:, 1, :]))
            chain(v.tensor_tensor(st[:, 4, :], st[:, 0, :], st[:, 3, :], ALU.mult))
            chain(v.tensor_tensor(st[:, 4, :], st[:, 4, :], st[:, 3, :], ALU.mult))
            chain(v.tensor_scalar(st[:, 4, :], st[:, 4, :], -0.5, 1.5, ALU.mult, ALU.add))
            chain(v.tensor_tensor(st[:, 3, :], st[:, 3, :], st[:, 4, :], ALU.mult))
            for c in range(G):
                r = slice(4 * c, 4 * c + 4)
                v.tensor_tensor(xn[:, r, :], xn[:, r, :], of_rows(3, c), ALU.mult).then_inc(xn_done, 1)
            v.wait_ge(w_in, 16 * 9)
            v.tensor_scalar(t.neg_bv[:, :], t.neg_bv[:, :], -1.0, None, ALU.mult)
            v.tensor_copy(bv_wide[:, :], bv_col[:, 0:1].broadcast_to([D, D])).then_inc(bvw, 1)
            v.wait_ge(c_done, 1)
            v.tensor_tensor(t.const_row[:, :], ps[4][:, 0:D], bo_row[:, :], ALU.add)
            for c in range(G):
                r = slice(8 * c, 8 * c + 8)
                v.wait_ge(q_ready, c + 1)
                chain(v.tensor_tensor(qres[:, r, :], q32[:, r, :], qp[:, 0, r, :], ALU.subtract))
                chain(v.tensor_copy(qp[:, 1, r, :], qres[:, r, :]))
                m = v.tensor_tensor(qp[:, 2, r, :], qres[:, r, :], qp[:, 1, r, :], ALU.subtract)
            m.then_inc(q_cut, 1)

            steps(v, step)
            finish_a(NCH // PERIOD, 0)
            finish_b(NCH // PERIOD, 0)
            finish_c(NCH // PERIOD, 1)
            statistics_a(NCH // PERIOD, 1)
            statistics_b(NCH // PERIOD, 1)
            statistics_c(NCH // PERIOD, 1)

        @block.tensor
        def _(pe):
            def scores(i, k, tile):
                n = at(i, k)
                if not there(n):
                    return
                if k % 3 == 0 and tile == 0:
                    b = 2 * i + k // 3
                    if isinstance(b, int) and b == 0:
                        pe.wait_ge(ones_spread, 16 * (PERIOD - 1))
                    pe.wait_ge(qturn_ready, b + 1)
                    pe.wait_ge(shift_ready, 2 * (b + 1))
                for half in range(2):
                    j = 2 * NT * k + 2 * tile + half
                    wait(pe, probs_ready, 2 * NT * n + 2 * tile + half - 2)
                    for p in range(4):
                        g = 4 * half + p
                        m = pe.matmul(s_bank[j % 3][0:TK, PQ * p:PQ * (p + 1)],
                                      t.k_stack[:, k % PERIOD, g, TK * tile:TK * (tile + 1)],
                                      t.q_turn[:, k // 3 % 2, PQ * g:PQ * (g + 1)], start=True, stop=True)
                    m.then_inc(scores_done, 1)

            def max_scores(i, k, pair):
                n, kk = at(i, k + 4), k + 4
                if not there(n):
                    return
                if pair == 0:
                    pe.wait_ge(stack_loaded[kk % PERIOD], 16 * NSLOT * (i + kk // PERIOD + 1))
                    if kk % CPB == 0:
                        pe.wait_ge(qmax_ready, 2 * i + kk // CPB + 1)
                wait(pe, max_read, HP * n + pair - 1)
                pe.matmul(m_bank[pair % 2][0:PQ, 0:CH], q_max[:, kk // CPB % 2, PQ * pair:PQ * (pair + 1)],
                          t.k_stack[0:ROWS, kk % PERIOD, pair, :], start=True, stop=True).then_inc(maxs_done, 1)

            def pv(i, k, tile):
                n = at(i, k)
                if not there(n):
                    return
                first, last = k % 3 == 0 and tile == 0, k % 3 == 2 and tile == NT - 1
                if first:
                    wait(pe, y_ready, 2 * i + k // 3)
                if tile == 0:
                    pe.wait_ge(v_ready, n + 1)
                pe.wait_ge(probs_ready, 2 * NT * n + 2 * tile + 2)
                for head, cnt, col_tile, col, vcol in GROUPS:
                    wd = DK * cnt + 1
                    m = pe.matmul(y_bank[32 * col_tile:32 * col_tile + wd, col:col + SQ * cnt],
                                  t.v_aug[:, k % PERIOD, tile, vcol:vcol + wd],
                                  probs[0:TK, (NT * k + tile) % 3, SQ * head:SQ * (head + cnt)],
                                  start=first and col == 0, stop=last, skip_group_check=True)
                m.then_inc(pv_done, 1)

            def keys(i, k):
                n = at(i, k + 6)
                if not there(n):
                    return
                pe.wait_ge(ctx_loaded[k % 3], 16 * (2 * i + (k + 6) // 3 + 1))
                wait(pe, k1_ready, n)
                if k % 3 == 1:
                    wait(pe, o_ready, 2 * i + k // 3)
                if k % 3 == 0:
                    wait(pe, shift_ready, 2 * (2 * i + k // 3 + 1))
                pe.matmul(bank_b[:, 0:CH], t.wk[:, :], cT[:, k % 3, :], start=True, stop=True).then_inc(keys_done, 1)

            def values(i, k):
                n, kk = at(i, k + 5), k + 5
                if not there(n):
                    return
                wait(pe, v_ready, n)
                if k % 3 == 0:
                    wait(pe, shift_ready, 2 * (2 * i + k // 3) + 1)
                for tile in range(NT):
                    m = pe.matmul(bank_a[0:TK, D * tile:D * (tile + 1)], cT[:, kk % 3, TK * tile:TK * (tile + 1)],
                                  t.wv[:, :], start=True, stop=True)
                m.then_inc(vals_done, 1)

            def max_rows(i, k):
                b = 2 * i + (k + 1) // 3
                if k % 3 != 2 or not there(b, B):
                    return
                pe.wait_ge(maxcut_ready, b + 1)
                n = at(i, k)
                if not there(n + 6):
                    pe.wait_ge(o_ready, b - 1)
                for half, bank in enumerate((bank_a, bank_b)):
                    if half == 0:
                        pe.wait_ge(v_ready, min_chunk(n + 6))
                    else:
                        pe.wait_ge(k1_ready, min_chunk(n + 7))
                    for p in range(4):
                        m = pe.matmul(bank[SHIFT:SHIFT + 3, PQ * p:PQ * (p + 1)], max_cut[:, 4 * half + p, :],
                                      t.ident_b[0:PQ, 0:PQ], start=True, stop=True)
                    m.then_inc(mrow_done, 1)

            def min_chunk(n):
                return min(n, NCH) if isinstance(n, int) else n

            def y_turn(i, k):
                b = 2 * i + k // 3 - 1
                if k % 3 != 0 or not there(b, B):
                    return
                pe.wait_ge(y_ready, b + 1)
                pe.wait_ge(k1_ready, min_chunk(at(i, k + 7)))
                pe.transpose(bank_b[:, 0:128], y_raw[:, 0:128], t.ident[:, :])
                for j in range(1, 5):
                    rows, col = (128, 128 * j) if j < 3 else (64, 3 * 128 + 64 * (j - 3))
                    m = pe.transpose(bank_b[0:SQ, col:col + rows], y_raw[0:rows, SQ * j:SQ * (j + 1)],
                                     t.ident[0:rows, 0:rows])
                m.then_inc(y_turned, 1)

            def y_back(i, k):
                b = 2 * i + k // 3 - 1
                if k % 3 != 0 or not there(b, B):
                    return
                pe.wait_ge(yn_ready, b + 1)
                pe.transpose(bank_b[:, 0:128], yn[:, :], t.ident[:, :]).then_inc(yn_turned, 1)

            def out_proj(i, k):
                b = 2 * i + k // 3 - 1
                if k % 3 != 1 or not there(b, B):
                    return
                r = 64 if k == 1 else 0
                pe.wait_ge(ynT_ready, b + 1)
                pe.matmul(bank_b[r:r + SQ, OUT_COL:OUT_COL + D], ynT[:, :], t.wo[:, :], start=True,
                          stop=True).then_inc(out_done, 1)

            def step(i, k):
                scores(i, k, 0)
                max_scores(i, k, 0)
                pv(i if k else i - 1, k - 1 if k else PERIOD - 1, 3)
                max_scores(i, k, 1)
                scores(i, k, 1)
                out_proj(i, k)
                max_scores(i, k, 2)
                pv(i, k, 0)
                max_scores(i, k, 3)
                keys(i, k)
                max_scores(i, k, 4)
                values(i, k)
                max_scores(i, k, 5)
                scores(i, k, 2)
                y_turn(i, k)
                max_scores(i, k, 6)
                pv(i, k, 1)
                max_rows(i, k)
                scores(i, k, 3)
                max_scores(i, k, 7)
                pv(i, k, 2)
                y_back(i, k)

            pe.wait_ge(ident, 1)
            for c in range(G):
                pe.wait_ge(xn_done, c + 1)
                for n in range(4):
                    m = pe.transpose(ps[c][:, 128 * n:128 * n + 128], xn[:, 4 * c + n, :], t.ident[:, :])
                m.then_inc(xT_done, 1)
            pe.wait_ge(w_in, 16 * 9)
            pe.wait_ge(bvw, 1)
            pe.matmul(ps[4][:, 0:D], bv_wide[:, :], t.wo[:, :], start=True, stop=True).then_inc(c_done, 1)
            for c in range(G):
                pe.wait_ge(xT_copied, c + 1)
                pe.matmul(ps[c][:, 0:8 * SQ], wq[:, :], xnT[:, 4 * c:4 * c + 4, :, 0:SQ], start=True,
                          stop=True).then_inc(q_done, 1)
            steps(pe, step)
            pv(NCH // PERIOD - 1, PERIOD - 1, 3)
            y_turn(NCH // PERIOD, 0)
            y_back(NCH // PERIOD, 0)
            out_proj(NCH // PERIOD, 1)


class Tiles:
    pass


def program(nc, ins, out):
    with ExitStack() as ctx:
        t = Tiles()

        def sb(name, shape, dt=F32):
            return ctx.enter_context(nc.sbuf_tensor(name, shape, dt))

        t.x = sb("x", [128, PAIRS, D])
        t.ident = sb("ident", [128, 128])
        t.mv = sb("mv", [128, PAIRS, 2])
        with ExitStack() as attn:
            def sa(name, shape, dt=F32):
                return attn.enter_context(nc.sbuf_tensor(name, shape, dt))

            t.ident_b = sa("ident_b", [128, 128], BF16)
            t.wk = sa("wk", [D, D])
            t.bk = sa("bk", [D, 1])
            t.wv = sa("wv", [D, D])
            t.neg_bv = sa("neg_bv", [128, D])
            t.wo = sa("wo", [D, D])
            t.const_row = sa("const_row", [128, D])
            t.k_stack = sa("k_stack", [128, PERIOD, HP, CH], BF16)
            t.q_turn = sa("q_turn", [128, 2, HP * PQ], BF16)
            t.v_aug = sa("v_aug", [TK, PERIOD, NT, VW])
            t.q_stack = sa("q_stack", [ROWS, HP, 2, B, SQ], BF16)
            t.y_sum = attn.enter_context(nc.psum_tensor("y_sum", [128, 512], F32))
            cross_attention(nc, ins, t)
        feed_forward(nc, ins, t, out)


def feed_forward(nc, ins, t, out):
    with ExitStack() as ctx:
        def sb(name, shape, dt=F32):
            return ctx.enter_context(nc.sbuf_tensor(name, shape, dt))

        def sem(name):
            return ctx.enter_context(nc.semaphore(name))

        xl = sb("xl", [128, PAIRS, D])
        nx = sb("nx", [128, PAIRS, D])
        st = sb("ff_st", [128, 9, PAIRS])
        xl_stats = sb("xl_stats", [128, PAIRS, 6])
        xl_mv = sb("xl_mv", [128, PAIRS, 2])
        nT = sb("nT", [D, W])
        q_head = sb("q_head", [D, FH, W])
        kT = sb("kT", [D, W])
        vc = sb("vc", [SQ, B, FDK])
        p = sb("p", [128, PAIRS * FH, SQ])
        pmax = sb("pmax", [128, PAIRS * FH])
        psum_ = sb("psum_", [128, PAIRS * FH])
        prec = sb("prec", [128, PAIRS * FH])
        pT = sb("pT", [SQ, PAIRS * FH, 128])
        oT = sb("oT", [D, W])
        hmask = sb("hmask", [D, FH])
        g1 = sb("g1", [D, 1])
        g2 = sb("g2", [D, 1])
        wq = sb("ff_wq", [D, D])
        wkc = sb("ff_wkc", [D, FH, FDK])
        wvc = sb("ff_wvc", [D, FDK])
        wo = sb("ff_wo", [D, D])
        wr = sb("ff_wr", [D, NE])
        ebias = sb("ebias", [128, NE])
        rank = sb("rank", [128, NE])
        rw = sb("rw", [128, PAIRS, NE])
        hot = sb("hot", [128, 2, PAIRS, NE])
        tmp = sb("tmp", [128, PAIRS, NE])
        rs = sb("rs", [128, 8, PAIRS])
        comb = sb("comb", [128, NE + 1, PAIRS])
        comb_e = sb("comb_e", [128, SLOTS, PAIRS])
        w1 = sb("w1", [D, SLOTS, FF])
        w3 = sb("w3", [D, SLOTS, FF])
        w2 = sb("w2", [FF, SLOTS, D])
        th = sb("th", [FF, 3, 8 * SQ])
        ga = sb("ga", [FF, 2, 8 * SQ])
        hid = sb("hid", [FF, 3, 8, 64])
        bank = [ctx.enter_context(nc.psum_tensor(f"ff_bank{i}", [128, 512], F32)) for i in range(8)]

        w_in = sem("ff_w_in")
        w_slot = [sem(f"w_slot{j}") for j in range(SLOTS)]
        dve = sem("ff_dve")
        ranked = sem("ranked")
        sums_ready = sem("sums_ready")
        roots_ready = sem("roots_ready")
        nx_ready = sem("nx_ready")
        nx_turned = sem("nx_turned")
        nT_ready = sem("nT_ready")
        hmask_ready = sem("hmask_ready")
        q_done = sem("ff_q_done")
        k_done = sem("ff_k_done")
        q01_taken = sem("q01_taken")
        q23_taken = sem("q23_taken")
        k_taken = sem("k_taken")
        vc_done = sem("vc_done")
        vc_taken = sem("vc_taken")
        s_done = sem("s_done")
        less_max = sem("less_max")
        p_exp = sem("p_exp")
        p_ready = sem("p_ready")
        p_turned = sem("p_turned")
        pT_ready = sem("pT_ready")
        o_done = sem("ff_o_done")
        oT_ready = sem("oT_ready")
        proj_done = sem("proj_done")
        xl_ready = sem("xl_ready")
        logit_done = sem("logit_done")
        r_less = sem("r_less")
        r_exp = sem("r_exp")
        gate_less = sem("gate_less")
        gate_exp = sem("gate_exp")
        up_done = sem("up_done")
        th_ready = sem("th_ready")
        ga_ready = sem("ga_ready")
        hid_ready = sem("hid_ready")
        down_done = sem("down_done")
        acc_ready = sem("acc_ready")
        comb_ready = sem("comb_ready")
        stored = sem("stored")

        NC = 8
        s_bank, pt_bank, o_bank, proj_bank = bank[2:5], bank[5:7], bank[0:2], bank[7]
        gate_bank, up_bank, down_bank = bank[0:3], bank[3:6], bank[6:8]
        block = ctx.enter_context(nc.Block())

        @block.sync
        def _(sp):
            for dst, src in ((g1[:, :], ins["g1"]), (g2[:, :], ins["g2"]), (wq[:, :], ins["fWq"]),
                             (wvc[:, :], ins["Wvc"]), (wo[:, :], ins["fWo"]), (wr[:, :], ins["Wr"]),
                             (ebias[:, :], ins["eb"].partition_broadcast(128))):
                sp.dma_start(dst, src).then_inc(w_in, 16)
            for h in range(FH):
                sp.dma_start(wkc[:, h, :], ins["Wkc"]).then_inc(w_in, 16)

            def load(e, j):
                for dst, name in ((w1, "W1"), (w3, "W3"), (w2, "W2")):
                    src = ins[name][e] if isinstance(e, int) else \
                        ins[name][bass.ds(e, 1)].rearrange("o p f -> (o p) f")
                    sp.dma_start(dst[:, j, :], src).then_inc(w_slot[j], 16)

            for j in range(SLOTS):
                load(j, j)
            with sp.Fori(1, (NE + 1) // SLOTS) as i:
                for j in range(SLOTS):
                    e = sp.snap(i * SLOTS + j)
                    sp.wait_ge(down_done, i * (G * SLOTS) + G * (j + 1 - SLOTS))
                    load(e, j)
            for c in range(G):
                sp.wait_ge(acc_ready, G * NE + c + 1)
                for par in range(2):
                    sp.dma_start(out.rearrange("(n par) q d -> par q n d", par=2)[par][:, 4 * c:4 * c + 4, :],
                                 t.x[64 * par:64 * par + SQ, 4 * c:4 * c + 4, :]).then_inc(stored, 16)
            sp.wait_ge(w_in, 16 * 11)
            sp.wait_ge(stored, 16 * 2 * G)

        @block.gpsimd
        def _(g):
            for e in range(NE):
                g.memset(rank[:, e:e + 1], float(NE - e))
            g.memset(hid[:, :, :, SQ:64], 0.0).then_inc(ranked, 1)

        @block.vector
        def _(v):
            links = [0]

            def chain(ins):
                links[0] += 1
                ins.then_inc(dve, 1)
                v.wait_ge(dve, links[0])

            def group(c):
                return (slice(None), slice(4 * c, 4 * c + 4), slice(None))

            def wide(k, c):
                return st[:, k, 4 * c:4 * c + 4].unsqueeze(2).broadcast_to([128, 4, D])

            mean, var = t.mv[:, :, 0], t.mv[:, :, 1]
            def inverse_roots(r, roots, squares, tmp):
                chain(v.reciprocal(r, roots))
                chain(v.tensor_tensor(tmp, squares, r, ALU.mult))
                chain(v.tensor_tensor(tmp, tmp, r, ALU.mult))
                chain(v.tensor_scalar(tmp, tmp, -0.5, 1.5, ALU.mult, ALU.add))
                chain(v.tensor_tensor(r, r, tmp, ALU.mult))

            chain(v.tensor_scalar(st[:, 0, :], var, EPS_LN, None, ALU.add))
            v.scalar_tensor_tensor(out=st[:, 1, :], in0=st[:, 0, :], scalar=EPS_RMS, in1=var, op0=ALU.mult,
                                   op1=ALU.add).then_inc(sums_ready, 1)
            chain(v.tensor_reduce(hmask[:, :], t.ident[:, :].rearrange("p (h x) -> p h x", x=FDK), AX_X, ALU.add))
            v.tensor_copy(st[:, 8, :], mean).then_inc(hmask_ready, 1)
            v.wait_ge(hmask_ready, 1)
            for c in range(G):
                m = v.tensor_tensor(xl[group(c)], t.x[group(c)], wide(8, c), ALU.subtract)
            chain(m)
            v.wait_ge(roots_ready, 1)
            inverse_roots(st[:, 2:4, :], st[:, 4:6, :], st[:, 0:2, :], st[:, 6:8, :])
            for c in range(G):
                v.tensor_tensor(nx[group(c)], xl[group(c)], wide(3, c), ALU.mult).then_inc(nx_ready, 1)

            for c in range(G):
                m = v.tensor_tensor(xl[group(c)], xl[group(c)], wide(2, c), ALU.mult)
                if c == G - 1:
                    chain(m)
                v.wait_ge(q_done, c + 1)
                for h in range(2):
                    m = v.tensor_scalar(q_head[:, h, 512 * c:512 * c + 512], bank[c][:, :], hmask[:, h:h + 1], None,
                                        ALU.mult)
                m.then_inc(q01_taken, 1)
            chain(v.tensor_tensor(t.x[:, :, :], t.x[:, :, :], xl[:, :, :], ALU.add))
            for c in range(2):
                v.wait_ge(vc_done, c + 1)
                v.tensor_copy(vc[:, 16 * c:16 * c + 16, :], bank[c][0:SQ, :].rearrange("p (b d) -> p b d", d=FDK))\
                    .then_inc(vc_taken, 1)

            def less(c):
                r = slice(8 * c, 8 * c + 8)
                s = s_bank[c % 3][:, 0:8 * SQ].rearrange("p (r k) -> p r k", k=SQ)
                v.wait_ge(s_done, c + 1)
                chain(v.tensor_reduce(pmax[:, r], s, AX_X, ALU.max))
                v.tensor_tensor(p[:, r, :], s, pmax[:, r].unsqueeze(2).broadcast_to([128, 8, SQ]), ALU.subtract)\
                    .then_inc(less_max, 1)

            def normalise(c):
                r = slice(8 * c, 8 * c + 8)
                v.wait_ge(p_exp, c + 1)
                chain(v.tensor_reduce(psum_[:, r], p[:, r, :], AX_X, ALU.add))
                chain(v.reciprocal(prec[:, r], psum_[:, r]))
                v.tensor_tensor(p[:, r, :], p[:, r, :], prec[:, r].unsqueeze(2).broadcast_to([128, 8, SQ]), ALU.mult)\
                    .then_inc(p_ready, 1)

            def residual(c):
                v.wait_ge(proj_done, c + 1)
                o4 = proj_bank[:, :].rearrange("p (n d) -> p n d", d=D)
                chain(v.tensor_tensor(xl[group(c)], o4, xl[group(c)], ALU.add))
                v.tensor_tensor(t.x[group(c)], o4, t.x[group(c)], ALU.add).then_inc(xl_ready, 1)
                for n in range(4 * c, 4 * c + 4):
                    m = v.bn_stats(xl_stats[:, n, :], xl[:, n, :])
                chain(m)
                for n in range(4 * c, 4 * c + 4):
                    m = v.bn_aggr(xl_mv[:, n, :], xl_stats[:, n, :])
                return m

            less(0)
            for c in range(1, NC):
                less(c)
                normalise(c - 1)
                if c >= 5 and c % 2:
                    residual((c - 5) // 2)
            normalise(NC - 1)
            residual(2)
            chain(residual(3))
            chain(v.tensor_tensor(st[:, 6, :], xl_mv[:, :, 0], xl_mv[:, :, 0], ALU.mult))
            v.scalar_tensor_tensor(out=st[:, 0, :], in0=st[:, 6, :], scalar=EPS_RMS, in1=xl_mv[:, :, 1],
                                   op0=ALU.add, op1=ALU.add).then_inc(sums_ready, 1)
            v.wait_ge(roots_ready, 2)
            inverse_roots(st[:, 2, :], st[:, 4, :], st[:, 0, :], st[:, 7, :])
            for c in range(G):
                v.tensor_tensor(nx[group(c)], xl[group(c)], wide(2, c), ALU.mult).then_inc(nx_ready, 1)

            e8 = [128, PAIRS, NE]
            lg = bank[7][:, 0:PAIRS * NE].rearrange("p (n e) -> p n e", e=NE)

            def over_experts(a):
                return a.unsqueeze(2).broadcast_to(e8)

            def logits_less_max():
                v.wait_ge(w_in, 16 * 11)
                v.wait_ge(ranked, 1)
                v.wait_ge(logit_done, 1)
                chain(v.tensor_tensor(rw[:, :, :], lg, ebias[:, :].unsqueeze(1).broadcast_to(e8), ALU.add))
                chain(v.tensor_reduce(rs[:, 0, :], rw[:, :, :], AX_X, ALU.max))
                v.tensor_tensor(rw[:, :, :], rw[:, :, :], over_experts(rs[:, 0, :]), ALU.subtract)\
                    .then_inc(r_less, 1)

            def probabilities():
                v.wait_ge(r_exp, 1)
                chain(v.tensor_reduce(rs[:, 1, :], rw[:, :, :], AX_X, ALU.add))
                chain(v.reciprocal(rs[:, 2, :], rs[:, 1, :]))
                chain(v.tensor_tensor(rw[:, :, :], rw[:, :, :], over_experts(rs[:, 2, :]), ALU.mult))

            def largest(k):
                top, first = rs[:, 3 + k, :], rs[:, 5, :]
                chain(v.tensor_reduce(top, rw[:, :, :], AX_X, ALU.max))
                chain(v.tensor_tensor(tmp[:, :, :], rw[:, :, :], over_experts(top), ALU.is_ge))
                chain(v.tensor_tensor(tmp[:, :, :], tmp[:, :, :], rank[:, :].unsqueeze(1).broadcast_to(e8), ALU.mult))
                chain(v.tensor_reduce(first, tmp[:, :, :], AX_X, ALU.max))
                chain(v.tensor_tensor(hot[:, k, :, :], tmp[:, :, :], over_experts(first), ALU.is_equal))
                if k == 0:
                    chain(v.scalar_tensor_tensor(out=rw[:, :, :], in0=hot[:, 0, :, :], scalar=-2.0, in1=rw[:, :, :],
                                                 op0=ALU.mult, op1=ALU.add))
                else:
                    v.tensor_tensor(rs[:, 6, :], rs[:, 4, :], rs[:, 3, :], ALU.subtract).then_inc(gate_less, 1)

            def combine():
                v.wait_ge(gate_exp, 1)
                chain(v.tensor_scalar(rs[:, 7, :], rs[:, 6, :], 1.0, None, ALU.add))
                chain(v.reciprocal(rs[:, 0, :], rs[:, 7, :]))
                chain(v.tensor_tensor(rs[:, 1, :], rs[:, 6, :], rs[:, 0, :], ALU.mult))
                chain(v.tensor_tensor(tmp[:, :, :], hot[:, 0, :, :], over_experts(rs[:, 0, :]), ALU.mult))
                chain(v.tensor_tensor(rw[:, :, :], hot[:, 1, :, :], over_experts(rs[:, 1, :]), ALU.mult))
                chain(v.tensor_tensor(comb[:, 1:NE + 1, :].rearrange("p e n -> p n e"), tmp[:, :, :], rw[:, :, :],
                                      ALU.add))

            def hidden(u, k):
                v.wait_ge(th_ready, u + 1)
                v.scalar_tensor_tensor(out=ga[:, k % 2, :], in0=th[:, k % 3, :], scalar=1.0,
                                       in1=gate_bank[k % 3][:, 0:8 * SQ], op0=ALU.add, op1=ALU.mult)\
                    .then_inc(ga_ready, 1)
                v.wait_ge(ga_ready, u + 1)
                wait(v, down_done, u - 2)
                v.scalar_tensor_tensor(out=hid[:, k % 3, :, 0:SQ],
                                       in0=up_bank[k % 3][:, 0:8 * SQ].rearrange("p (n q) -> p n q", q=SQ),
                                       scalar=0.5, in1=ga[:, k % 2, :].rearrange("p (n q) -> p n q", q=SQ),
                                       op0=ALU.mult, op1=ALU.mult).then_inc(hid_ready, 1)

            def collect(u, k):
                v.wait_ge(down_done, u + 1)
                wait(v, acc_ready, u + 1 - G)
                k %= UNITS
                c = k % G
                for n in range(4):
                    xs = t.x[:, 4 * c + n, :]
                    m = v.scalar_tensor_tensor(out=xs, in0=down_bank[k % 2][:, D * n:D * n + D],
                                               scalar=comb_e[:, k // G, 4 * c + n:4 * c + n + 1],
                                               in1=xs, op0=ALU.mult, op1=ALU.add)
                m.then_inc(acc_ready, 1)

            def weights(i, j):
                e = SLOTS * i + j
                src = comb[:, e, :] if isinstance(e, int) else comb[:, bass.ds(e, 1), :].rearrange("p o n -> p (o n)")
                v.tensor_copy(comb_e[:, j, :], src).then_inc(comb_ready, 1)
                v.wait_ge(comb_ready, e + 1)

            v.memset(comb[:, 0, :], 1.0).then_inc(comb_ready, 1)
            v.wait_ge(comb_ready, 1)
            v.tensor_copy(comb_e[:, 0, :], comb[:, 0, :])
            logits_less_max()
            router = {0: probabilities, 1: lambda: largest(0), 2: lambda: largest(1), 3: combine}

            def units(i):
                for k in range(UNITS):
                    u = UNITS * i + k
                    hidden(u, k)
                    if isinstance(i, int) and k in router:
                        router[k]()
                    if there(u - 2):
                        collect(u - 2, k - 2)
                    if k % G == 1 and not (isinstance(i, int) and k == 1):
                        weights(i, k // G)

            units(0)
            with v.Fori(1, (NE + 1) // SLOTS) as i:
                units(i)
            for k in (UNITS - 2, UNITS - 1):
                collect(G * NE + G - UNITS + k, k)

        @block.scalar
        def _(a):
            def turn(n, g):
                for c in range(G):
                    a.wait_ge(nx_turned, G * n + c + 1)
                    a.activation(nT[:, 512 * c:512 * c + 512], bank[c][:, :], ACT.Copy, scale=g)\
                        .then_inc(nT_ready, 1)

            a.wait_ge(sums_ready, 1)
            a.activation(st[:, 4:6, :], st[:, 0:2, :], ACT.Sqrt).then_inc(roots_ready, 1)
            a.wait_ge(w_in, 16 * 11)
            turn(0, g1[:, 0:1])
            a.wait_ge(hmask_ready, 1)
            for c in range(G):
                a.wait_ge(k_done, c + 1)
                a.copy(kT[:, 512 * c:512 * c + 512], bank[4 + c][:, :]).then_inc(k_taken, 1)
                a.wait_ge(q01_taken, c + 1)
                for h in range(2, FH):
                    m = a.activation(q_head[:, h, 512 * c:512 * c + 512], bank[c][:, :], ACT.Copy,
                                     scale=hmask[:, h:h + 1])
                m.then_inc(q23_taken, 1)

            def turned_back(c):
                for n in (2 * c, 2 * c + 1):
                    a.wait_ge(p_turned, n + 1)
                    a.copy(pT[:, FH * n:FH * n + FH, :], pt_bank[n % 2][0:SQ, :].rearrange("p (h q) -> p h q", h=FH))\
                        .then_inc(pT_ready, 1)

            def attended(c):
                a.wait_ge(o_done, c + 1)
                a.copy(oT[:, 512 * c:512 * c + 512], o_bank[c % 2][:, :]).then_inc(oT_ready, 1)

            for c in range(NC):
                a.wait_ge(less_max, c + 1)
                a.activation(p[:, 8 * c:8 * c + 8, :], p[:, 8 * c:8 * c + 8, :], ACT.Exp, scale=FDK ** -0.5)\
                    .then_inc(p_exp, 1)
                if c >= 2:
                    turned_back(c - 2)
                if c >= 4 and c % 2 == 0:
                    attended(c // 2 - 2)
            turned_back(NC - 2)
            attended(2)
            turned_back(NC - 1)
            attended(3)
            a.wait_ge(sums_ready, 2)
            a.activation(st[:, 4, :], st[:, 0, :], ACT.Sqrt).then_inc(roots_ready, 1)
            turn(1, g2[:, 0:1])

            def squash(u, k):
                a.wait_ge(up_done, u + 1)
                wait(a, ga_ready, u - 2)
                a.activation(th[:, k % 3, :], gate_bank[k % 3][:, 0:8 * SQ], ACT.Tanh, scale=0.5)\
                    .then_inc(th_ready, 1)

            for k in range(UNITS):
                squash(k, k)
                if k == 0:
                    a.wait_ge(r_less, 1)
                    a.activation(rw[:, :, :], rw[:, :, :], ACT.Exp).then_inc(r_exp, 1)
                if k == 2:
                    a.wait_ge(gate_less, 1)
                    a.activation(rs[:, 6, :], rs[:, 6, :], ACT.Exp).then_inc(gate_exp, 1)
            with a.Fori(1, (NE + 1) // SLOTS) as i:
                for k in range(UNITS):
                    squash(UNITS * i + k, k)

        @block.tensor
        def _(pe):
            def turn(n):
                for c in range(G):
                    pe.wait_ge(nx_ready, G * n + c + 1)
                    for k in range(4):
                        m = pe.transpose(bank[c][:, 128 * k:128 * k + 128], nx[:, 4 * c + k, :], t.ident[:, :])
                    m.then_inc(nx_turned, 1)

            turn(0)
            for c in range(G):
                pe.wait_ge(nT_ready, c + 1)
                cols = nT[:, 512 * c:512 * c + 512]
                pe.matmul(bank[c][:, :], wq[:, :], cols, start=True, stop=True).then_inc(q_done, 1)
                pe.matmul(bank[4 + c][:, :], wkc[:, :, :].rearrange("p h d -> p (h d)"), cols, start=True,
                          stop=True).then_inc(k_done, 1)
            for c in range(2):
                pe.wait_ge(q01_taken, c + 1)
                pe.wait_ge(q23_taken, c + 1)
                for b in range(16):
                    m = pe.matmul(bank[c][0:SQ, FDK * b:FDK * b + FDK],
                                  nT[:, 64 * (16 * c + b):64 * (16 * c + b) + SQ], wvc[:, :], start=True, stop=True)
                m.then_inc(vc_done, 1)

            def scores(c):
                pe.wait_ge(q01_taken, G)
                pe.wait_ge(q23_taken, G)
                if c >= 3:
                    pe.wait_ge(less_max, c - 2)
                for n in range(2):
                    for h in range(FH):
                        for par in range(2):
                            tok = 64 * (2 * (2 * c + n) + par)
                            m = pe.matmul(s_bank[c % 3][64 * par:64 * par + 64,
                                                        SQ * (FH * n + h):SQ * (FH * n + h) + SQ],
                                          q_head[:, h, tok:tok + 64], kT[:, tok:tok + SQ], start=True, stop=True)
                m.then_inc(s_done, 1)

            def turn_p(c):
                pe.wait_ge(p_ready, c + 1)
                for n in (2 * c, 2 * c + 1):
                    if n >= 2:
                        pe.wait_ge(pT_ready, n - 1)
                    for h in range(FH):
                        m = pe.transpose(pt_bank[n % 2][0:SQ, 128 * h:128 * h + 128], p[:, FH * n + h, :],
                                         t.ident[:, :])
                    m.then_inc(p_turned, 1)

            def attend(c):
                pe.wait_ge(vc_taken, 2)
                for n in (2 * c, 2 * c + 1):
                    g = n // 4
                    pe.wait_ge(pT_ready, n + 1)
                    if g >= 2:
                        pe.wait_ge(oT_ready, g - 1)
                    for par in range(2):
                        for h in range(FH):
                            col = 64 * (2 * (n % 4) + par)
                            m = pe.matmul(o_bank[g % 2][FDK * h:FDK * h + FDK, col:col + 64],
                                          vc[:, 2 * n + par, :], pT[:, FH * n + h, 64 * par:64 * par + 64],
                                          start=True, stop=True)
                    if n % 4 == 3:
                        m.then_inc(o_done, 1)

            def project(c):
                pe.wait_ge(oT_ready, c + 1)
                if c:
                    pe.wait_ge(xl_ready, c)
                for n in range(4):
                    tok = 128 * (4 * c + n)
                    m = pe.matmul(proj_bank[:, D * n:D * n + D], oT[:, tok:tok + 128], wo[:, :], start=True,
                                  stop=True)
                m.then_inc(proj_done, 1)

            for c in range(NC):
                scores(c)
                if c >= 5 and c % 2:
                    project((c - 5) // 2)
                if c >= 2:
                    turn_p(c - 2)
                if c >= 3:
                    attend(c - 3)
            turn_p(NC - 2)
            attend(NC - 3)
            turn_p(NC - 1)
            attend(NC - 2)
            project(2)
            attend(NC - 1)
            project(3)
            turn(1)
            pe.wait_ge(nT_ready, 2 * G)
            pe.wait_ge(xl_ready, G)
            for n in range(PAIRS):
                m = pe.matmul(bank[7][:, NE * n:NE * n + NE], nT[:, 128 * n:128 * n + 128], wr[:, :], start=True,
                              stop=True)
            m.then_inc(logit_done, 1)

            def up(u, k):
                c, slot = k % G, k // G
                wait(pe, hid_ready, u - 2)
                cols = nT[:, 512 * c:512 * c + 512].rearrange("p (n q) -> p n q", q=64)[:, :, 0:SQ]
                pe.matmul(gate_bank[k % 3][:, 0:8 * SQ], w1[:, slot, :], cols, start=True, stop=True)
                pe.matmul(up_bank[k % 3][:, 0:8 * SQ], w3[:, slot, :], cols, start=True, stop=True)\
                    .then_inc(up_done, 1)

            def down(u, k):
                k %= UNITS
                pe.wait_ge(hid_ready, u + 1)
                wait(pe, acc_ready, u - 1)
                for n in range(4):
                    m = pe.matmul(down_bank[k % 2][:, D * n:D * n + D],
                                  hid[:, k % 3, 2 * n:2 * n + 2, :].rearrange("p n q -> p (n q)"),
                                  w2[:, k // G, :], start=True, stop=True)
                m.then_inc(down_done, 1)

            def units(i):
                for k in range(UNITS):
                    u = UNITS * i + k
                    if k % G == 0:
                        pe.wait_ge(w_slot[k // G], 16 * 3 * (i + 1))
                    up(u, k)
                    if there(u - 2):
                        down(u - 2, k - 2)

            units(0)
            with pe.Fori(1, (NE + 1) // SLOTS) as i:
                units(i)
            for k in (UNITS - 2, UNITS - 1):
                down(G * NE + G - UNITS + k, k)


def _layouts(a):
    import numpy as np
    c = np.ascontiguousarray
    f = {k: np.asarray(x) for k, x in a.items()}
    qcols = np.arange(D).reshape(HP, 2, DK).transpose(1, 2, 0).reshape(D)
    return {
        "x": c(f["x"]),
        "ctx": c(f["ctx_1024"].reshape(NCH, CH, D).transpose(0, 2, 1)),
        "Wq": c(f["L0_xattn_Wq"][:, qcols]), "bq": c(f["L0_xattn_bq"][qcols].reshape(D, 1)),
        "Wk": c(f["L0_xattn_Wk"][:, qcols]), "bk": c(f["L0_xattn_bk"][qcols].reshape(D, 1)),
        "Wv": c(f["L0_xattn_Wv"]), "bv": c(f["L0_xattn_bv"].reshape(1, D)),
        "Wo": c(f["L0_xattn_Wo"]), "bo": c(f["L0_xattn_bo"].reshape(1, D)),
        "g1": c(f["L0_ffn_g1"].reshape(D, 1)), "g2": c(f["L0_ffn_g2"].reshape(D, 1)),
        "fWq": c(f["L0_ffn_Wq"].T), "Wkc": c(f["L0_ffn_Wkc"].T), "Wvc": c(f["L0_ffn_Wvc"].T),
        "fWo": c(f["L0_ffn_Wo"].T), "Wr": c(f["L0_ffn_Wr"].T), "eb": c(f["L0_ffn_expert_bias"].reshape(1, NE)),
        **{f"W{k}": c(np.concatenate([f[f"L0_ffn_sW{k}"][None], f[f"L0_ffn_eW{k}"]]).transpose(0, 2, 1))
           for k in (1, 2, 3)},
    }


def kernel(**inputs):
    import concourse.bacc as _bacc
    from concourse.bass_utils import run_bass_kernel_spmd as _run

    nc = _bacc.Bacc("TRN2", target_bir_lowering=False, num_devices=1)
    arrays, aps = {}, {}
    for name, a in _layouts(inputs).items():
        arrays[f"in_{name}"] = a
        aps[name] = nc.dram_tensor(f"in_{name}", a.shape, F32, kind="ExternalInput").ap()
    out = nc.dram_tensor("out_0", (B, SQ, D), F32, kind="ExternalOutput").ap()
    program(nc, aps, out)
    r = _run(nc, [arrays], core_ids=[0])
    return r.results[0]["out_0"]
```

```python
import concourse.bass as bass
from concourse import mybir
from contextlib import ExitStack

F32 = mybir.dt.float32
BF16 = mybir.dt.bfloat16
U32 = mybir.dt.uint32
ALU = mybir.AluOpType
ACT = mybir.ActivationFunctionType
AX_X = mybir.AxisListType.X

D = 128
B, SQ, SK = 32, 56, 1500
H, DK = 16, 8
HP = H // 2
PQ = 2 * SQ
CH = 500
TK = 125
NT = CH // TK
CPB = SK // CH
NCH = B * CPB
PERIOD = 2 * CPB
PAIRS = B // 2
B_FIRST = 2
HALF = HP // 2 * PQ
K_PART = [0, 0, 0, 1, 1, 2]
Q_PART = [0, 1, 2, 0, 1, 0]
NSLOT = len(K_PART)
ROWS = 16 * NSLOT
SHIFT = ROWS
SCALE = DK ** -0.5
TWO_ONES = 0x3F803F80
EPS_LN, EPS_RMS = 1e-5, 1e-6

GROUPS = [(0, 3, 0, 0, 0), (3, 3, 1, 0, 25), (6, 3, 2, 0, 50), (9, 3, 3, 0, 75),
          (12, 2, 0, 3 * SQ, 100), (14, 2, 1, 3 * SQ, 117)]
VW = 134
YW = 5 * SQ
OUT_COL = 128

FH, FDK = 4, 32
NE, FF = 8, 128
W = 64 * B
G = W // 512
SLOTS = 3
UNITS = SLOTS * G


def wait(eng, sem, value):
    if not isinstance(value, int) or value > 0:
        eng.wait_ge(sem, value)


def there(n, count=NCH):
    return not isinstance(n, int) or 0 <= n < count


def newton_step(v, chain, r, squares, tmp):
    chain(v.reciprocal(r, r))
    chain(v.tensor_tensor(tmp, squares, r, ALU.mult))
    chain(v.tensor_tensor(tmp, tmp, r, ALU.mult))
    chain(v.tensor_scalar(tmp, tmp, -0.5, 1.5, ALU.mult, ALU.add))
    chain(v.tensor_tensor(r, r, tmp, ALU.mult))


def of_rows(a):
    return a.unsqueeze(2).broadcast_to([128, 4, D])


def cross_attention(nc, ins, t):
    with ExitStack() as ctx:
        def sb(name, shape, dt=F32):
            return ctx.enter_context(nc.sbuf_tensor(name, shape, dt))

        def pb(name):
            return ctx.enter_context(nc.psum_tensor(name, [128, 512], F32))

        def sem(name):
            return ctx.enter_context(nc.semaphore(name))

        cT = sb("cT", [D, 3, CH])
        k32 = sb("k32", [D, 2, CH])
        k_res = sb("k_res", [D, CH])
        kp = sb("kp", [D, 3, 3, CH], BF16)
        probs = sb("probs", [128, 3, H * SQ])
        q_max = sb("q_max", [ROWS, 2, HP * PQ], BF16)
        max_part = sb("max_part", [PQ, 2, HP, CPB])
        neg_max = sb("neg_max", [PQ, HP])
        max_res = sb("max_res", [PQ, HP])
        max_cut = sb("max_cut", [PQ, HP, 3], BF16)
        y_raw = sb("y_raw", [128, YW])
        y_rec = sb("y_rec", [SQ, H])
        yn = sb("yn", [128, D])
        ynT = sb("ynT", [D, SQ])
        o_tmp = sb("o_tmp", [128, D])
        x_new = sb("x_new", [128, D])
        x_stats = sb("x_stats", [128, 6])
        mv_new = sb("mv_new", [128, 2])

        bq = sb("bq", [D, 1])
        bv_col = sb("bv_col", [D, 1])
        bv_wide = sb("bv_wide", [D, D])
        bo_row = sb("bo_row", [D, D])
        wq = sb("wq", [D, D])
        st = sb("st", [128, 6, PAIRS])
        stats = sb("stats", [128, PAIRS, 6])
        mv0 = sb("mv0", [128, PAIRS, 2])
        qp = sb("qp", [D, 3, B, SQ], BF16)
        xn = probs[:, :, :].rearrange("p s c -> p (s c)")[:, 0:PAIRS * D].rearrange("p (n d) -> p n d", d=D)
        early = t.k_stack[:, PERIOD // 2:PERIOD, :, :].rearrange("p s g c -> p (s g c)").bitcast(F32)
        xnT = early[:, 0:W].rearrange("p (n h q) -> p n h q", h=2, q=64)
        q32 = early[:, W:W + B * SQ].rearrange("p (b q) -> p b q", q=SQ)
        qres = early[:, W + B * SQ:W + 2 * B * SQ].rearrange("p (b q) -> p b q", q=SQ)

        s_bank = [pb(f"s_bank{i}") for i in range(3)]
        m_bank = [pb(f"m_bank{i}") for i in range(2)]
        bank_a = pb("bank_a")
        bank_b = pb("bank_b")
        y_bank = t.y_sum
        ps = s_bank + m_bank

        x_in = sem("x_in")
        x_first = sem("x_first")
        wqk_in = sem("wqk_in")
        w_in = sem("w_in")
        ff_in = sem("ff_in")
        dve = sem("dve_chain")
        pool = sem("pool_chain")
        ident = sem("ident_ready")
        ones_ready = sem("ones_ready")
        ones_spread = sem("ones_spread")
        var_done = sem("var_done")
        std_done = sem("std_done")
        xn_done = sem("xn_done")
        xT_done = sem("xT_done")
        xT_copied = sem("xT_copied")
        q_done = sem("q_done")
        q_ready = sem("q_ready")
        q_cut = sem("q_cut")
        q_zero = sem("q_zero")
        q_stacked = sem("q_stacked")
        q_rest_stacked = sem("q_rest_stacked")
        c_done = sem("c_done")
        bvw = sem("bvw")
        row_ready = sem("row_ready")

        ctx_loaded = [sem(f"ctx_loaded{i}") for i in range(3)]
        stack_loaded = [sem(f"stack_loaded{i}") for i in range(PERIOD)]
        keys_done = sem("keys_done")
        vals_done = sem("vals_done")
        maxs_done = sem("maxs_done")
        scores_done = sem("scores_done")
        pv_done = sem("pv_done")
        mrow_done = sem("mrow_done")
        y_turned = sem("y_turned")
        yn_turned = sem("yn_turned")
        out_done = sem("out_done")
        k1_ready = sem("k1_ready")
        probs_ready = sem("probs_ready")
        shift_ready = sem("shift_ready")
        v_ready = sem("v_ready")
        max_read = sem("max_read")
        neg_chain = sem("neg_chain")
        y_ready = sem("y_ready")
        rec_ready = sem("rec_ready")
        ynT_ready = sem("ynT_ready")
        yn_ready = sem("yn_ready")
        o_ready = sem("o_ready")
        stats_ready = sem("stats_ready")
        mv_ready = sem("mv_ready")
        x_ready = sem("x_ready")
        maxcut_ready = sem("maxcut_ready")
        res_ready = sem("res_ready")
        kcut_ready = sem("kcut_ready")
        qmax_ready = sem("qmax_ready")
        qturn_ready = sem("qturn_ready")

        def at(i, k):
            return i * PERIOD + k

        def steps(eng, step):
            for k in range(1, PERIOD):
                step(-1, k)
            for k in range(PERIOD):
                step(0, k)
            with eng.Fori(1, NCH // PERIOD - 1) as i:
                for k in range(PERIOD):
                    step(i, k)
            for k in range(PERIOD):
                step(NCH // PERIOD - 1, k)

        block = ctx.enter_context(nc.Block())

        @block.sync
        def _(sp):
            def load_ctx(i, k):
                n = at(i, k)
                if there(n):
                    if isinstance(n, int):
                        src = ins["ctx"][n]
                    else:
                        src = ins["ctx"][bass.ds(sp.snap(n), 1)].rearrange("o d s -> (o d) s")
                    if isinstance(n, int) and n < 3:
                        return
                    wait(sp, vals_done, n - 2)
                    sp.dma_start(cT[:, k % 3, :], src).then_inc(ctx_loaded[k % 3], 16)

            def step(i, k):
                if isinstance(i, int) and i < 0 and k >= 2:
                    sp.wait_ge(q_zero, 3)
                    sp.wait_ge(q_ready, G)
                    sp.wait_ge(q_cut, G)
                    for j in range(3 * (k - 2), 3 * (k - 1)):
                        stack_q(j // 2, j % 2, slice(B_FIRST, B), q_rest_stacked)
                load_ctx(i, k + 6)
                n = at(i, k + 5)
                if isinstance(n, int) and 1 <= n < PERIOD:
                    sp.wait_ge(ones_ready, 1)
                    sp.dma_start(t.k_stack[SHIFT:128, n, :, :], t.k_stack[SHIFT:128, 0, :, :])\
                        .then_inc(ones_spread, 16)
                if there(n):
                    wait(sp, scores_done, 2 * NT * (n - 5))
                    sp.wait_ge(kcut_ready, n + 1)
                    for s in range(NSLOT):
                        sp.dma_start(t.k_stack[16 * s:16 * s + 16, (k + 5) % PERIOD, :, :],
                                     kp[:, (k + 5) % 3, K_PART[s], :]).then_inc(stack_loaded[(k + 5) % PERIOD], 16)

            x_rows = ins["x"].rearrange("(n par) q d -> par q n d", par=2)

            def load_x(pairs, done):
                for par in range(2):
                    sp.dma_start(t.x[64 * par:64 * par + SQ, pairs, :], x_rows[par][:, pairs, :]).then_inc(done, 16)
                    sp.dma_start(t.x[64 * par + SQ:64 * par + 64, pairs, :], x_rows[par][0:64 - SQ, pairs, :])\
                        .then_inc(done, 16)

            load_x(slice(0, 4), x_first)
            for dst, src in ((wq[:, :], ins["Wq"]), (bq[:, :], ins["bq"]), (t.wk[:, :], ins["Wk"]),
                             (t.bk[:, :], ins["bk"])):
                sp.dma_start(dst, src).then_inc(wqk_in, 16)
            load_x(slice(4, PAIRS), x_in)
            for n in range(3):
                sp.dma_start(cT[:, n, :], ins["ctx"][n]).then_inc(ctx_loaded[n], 16)
            for dst, src in ((t.wv[:, :], ins["Wv"]), (t.wo[:, :], ins["Wo"]),
                             (bv_col[:, :], ins["bv"].rearrange("a d -> d a")),
                             (t.neg_bv[:, :], ins["bv"].partition_broadcast(128)),
                             (bo_row[:, :], ins["bo"].partition_broadcast(128))):
                sp.dma_start(dst, src).then_inc(w_in, 16)
            sp.wait_ge(q_zero, 1)

            def stack_q(s, h2, batches, done):
                r = 16 * s + 8 * h2
                sp.dma_start(t.q_stack[r:r + 8, :, h2, batches, :].rearrange("p g b q -> p g (b q)"),
                             qp[64 * h2:64 * h2 + 64, Q_PART[s], batches, :].rearrange("p b q -> p (b q)"))\
                    .then_inc(done, 16)

            sp.wait_ge(q_ready, 1)
            sp.wait_ge(q_cut, 1)
            for s in range(NSLOT):
                for h2 in range(2):
                    stack_q(s, h2, slice(0, B_FIRST), q_stacked)
            step(-1, 0)
            steps(sp, step)
            for dst, src in ((t.g1[:, :], ins["g1"]), (t.g2[:, :], ins["g2"]), (t.ff_wq[:, :], ins["fWq"]),
                             (t.wvc[:, :], ins["Wvc"]), (t.ff_wo[:, :], ins["fWo"]), (t.wr[:, :], ins["Wr"]),
                             (t.ebias[:, :], ins["eb"].partition_broadcast(128))):
                sp.dma_start(dst, src).then_inc(ff_in, 16)
            for h in range(FH):
                sp.dma_start(t.wkc[:, h, :], ins["Wkc"]).then_inc(ff_in, 16)
            sp.wait_ge(w_in, 16 * 5)
            sp.wait_ge(ff_in, 16 * 11)

        @block.gpsimd
        def _(g):
            g.memset(t.ident[:, :], 0.0).then_inc(pool, 1)
            g.wait_ge(pool, 1)
            g.affine_select(out=t.ident[:, :], in_=t.ident[:, :], compare_op=ALU.not_equal, fill=1.0, base=0,
                            pattern=[[-1, 128]], channel_multiplier=1).then_inc(ident, 1)
            g.wait_ge(ident, 1)
            g.memset(t.q_stack[:, :, :, 0:B_FIRST, :].rearrange("p g h b q -> p (g h) (b q)").bitcast(U32), 0)\
                .then_inc(q_zero, 1)
            g.wait_ge(q_zero, 1)
            g.memset(t.k_stack[SHIFT:128, 0, :, :].bitcast(U32), TWO_ONES).then_inc(ones_ready, 1)
            g.wait_ge(ones_ready, 1)
            for c in range(2):
                z = t.q_stack[:, 4 * c:4 * c + 4, :, B_FIRST:B, :].rearrange("p g h b q -> p (g h) (b q)")
                g.memset(z.bitcast(U32), 0).then_inc(q_zero, 1)
                g.wait_ge(q_zero, 2 + c)
            g.memset(t.q_turn[SHIFT:128, :, :], 0.0).then_inc(pool, 1)
            g.wait_ge(pool, 2)

            def step(i, k):
                b = 2 * i + (k + 6) // 3
                if k % 3 == 0 and there(b, B):
                    wait(g, maxs_done, HP * CPB * (b - 1))
                b = 2 * i + k // 3 + 1
                if k % 3 == 1 and there(b, B):
                    wait(g, scores_done, 2 * NT * CPB * (b - 1))
                n = at(i, k + 6)
                if there(n):
                    g.wait_ge(k1_ready, n + 1)
                    wait(g, kcut_ready, n)
                    g.tensor_tensor(kp[:, k % 3, 1, :], k32[:, k % 2, :], kp[:, k % 3, 0, :], ALU.subtract)
                    g.tensor_tensor(k_res[:, :], k32[:, k % 2, :], kp[:, k % 3, 0, :], ALU.subtract)\
                        .then_inc(res_ready, 1)
                    g.wait_ge(res_ready, n + 1)
                    g.tensor_tensor(kp[:, k % 3, 2, :], k_res[:, :], kp[:, k % 3, 1, :], ALU.subtract)\
                        .then_inc(kcut_ready, 1)
                b, kb = 2 * i + (k + 6) // 3, (k + 6) // 3
                if k % 3 == 0 and there(b, B):
                    if isinstance(b, int) and b in (0, 2):
                        g.wait_ge(q_stacked if b == 0 else q_rest_stacked, 16 * 2 * NSLOT)
                    g.tensor_copy(grid(q_max[:, kb % 2, :]), q_rows(b)).then_inc(qmax_ready, 1)
                b, kb = 2 * i + k // 3 + 1, k // 3 + 1
                if k % 3 == 1 and there(b, B):
                    g.tensor_copy(grid(t.q_turn[0:ROWS, kb % 2, :]), q_rows(b)).then_inc(qturn_ready, 1)

            def grid(a):
                return a.rearrange("p (g q) -> p g q", q=SQ)

            def q_rows(b):
                a = t.q_stack[:, :, :, :, :].rearrange("p g h b q -> p (g h) b q")
                if isinstance(b, int):
                    return a[:, :, b, :]
                return a[:, :, bass.ds(b, 1), :].rearrange("p g o q -> p g (o q)")

            step(-1, 0)
            steps(g, step)

        @block.scalar
        def _(a):
            def exp(i, k, tile, half):
                n = at(i, k)
                if there(n):
                    j = 2 * NT * k + 2 * tile + half
                    a.wait_ge(scores_done, 2 * NT * n + 2 * tile + half + 1)
                    if half == 0:
                        wait(a, pv_done, NT * n + tile - 2)
                    a.activation(probs[0:TK, (NT * k + tile) % 3, HALF * half:HALF * (half + 1)],
                                 s_bank[j % 3][0:TK, 0:HALF], ACT.Exp, scale=SCALE).then_inc(probs_ready, 1)

            def turn_back(i, k):
                b = 2 * i + k // 3 - 1
                if k % 3 == 1 and there(b, B):
                    a.wait_ge(yn_turned, b + 1)
                    wait(a, out_done, b)
                    a.copy(ynT[:, :], bank_b[:, 0:SQ]).then_inc(ynT_ready, 1)

            def step(i, k):
                n = at(i, k + 6)
                exp(i, k, 0, 0)
                exp(i, k, 0, 1)
                turn_back(i, k)
                exp(i, k, 1, 0)
                exp(i, k, 1, 1)
                if there(n):
                    a.wait_ge(keys_done, n + 1)
                    wait(a, kcut_ready, n - 1)
                    a.activation(k32[:, k % 2, :], bank_b[:, 0:CH], ACT.Relu, bias=t.bk[:, 0:1])
                    wait(a, stack_loaded[(k + 3) % PERIOD], 16 * NSLOT * (i + (k + 3) // PERIOD + 1)
                         if there(at(i, k + 3)) else 0)
                    a.activation(kp[:, k % 3, 0, :], bank_b[:, 0:CH], ACT.Relu, bias=t.bk[:, 0:1])\
                        .then_inc(k1_ready, 1)
                exp(i, k, 2, 0)
                exp(i, k, 2, 1)
                b = 2 * i + (k + 1) // 3
                if k % 3 == 2 and there(b, B):
                    for half, bank in enumerate((bank_a, bank_b)):
                        a.wait_ge(mrow_done, 2 * b + half + 1)
                        a.copy(t.q_turn[SHIFT:SHIFT + 3, (k + 1) // 3 % 2, HALF * half:HALF * (half + 1)],
                               bank[SHIFT:SHIFT + 3, 0:HALF]).then_inc(shift_ready, 1)
                exp(i, k, 3, 0)
                exp(i, k, 3, 1)

            def turned(c):
                a.wait_ge(xT_done, c + 1)
                a.copy(xnT[:, 4 * c:4 * c + 4, :, :], ps[c][:, :].rearrange("p (n h q) -> p n h q", n=4, h=2)
                       ).then_inc(xT_copied, 1)

            def queries(c):
                a.wait_ge(q_done, c + 1)
                q_psum = ps[c][:, 0:8 * SQ].rearrange("p (b q) -> p b q", b=8)
                a.activation(q32[:, 8 * c:8 * c + 8, :], q_psum, ACT.Relu, bias=bq[:, 0:1])
                a.activation(qp[:, 0, 8 * c:8 * c + 8, :], q_psum, ACT.Relu, bias=bq[:, 0:1]).then_inc(q_ready, 1)

            for n, r in enumerate((slice(0, 4), slice(4, PAIRS))):
                a.wait_ge(var_done, n + 1)
                a.activation(st[:, 1, r], st[:, 0, r], ACT.Sqrt).then_inc(std_done, 1)
            turned(0)
            a.wait_ge(wqk_in, 16 * 4)
            queries(0)
            step(-1, 0)
            for c in range(1, G):
                turned(c)
            for c in range(1, G):
                queries(c)

            steps(a, step)
            turn_back(NCH // PERIOD, 1)

        @block.vector
        def _(v):
            def pair_max(i, k, pair):
                n, kk = at(i, k + 4), k + 4
                if there(n):
                    v.wait_ge(maxs_done, HP * n + pair + 1)
                    v.tensor_reduce(max_part[:, kk // CPB % 2, pair, kk % CPB:kk % CPB + 1],
                                    m_bank[pair % 2][0:PQ, 0:CH], AX_X, ALU.max).then_inc(max_read, 1)

            def finish_a(i, k):
                b = 2 * i + k // 3 - 1
                if k % 3 == 0 and there(b, B):
                    v.wait_ge(pv_done, NT * CPB * (b + 1))
                    v.tensor_copy(y_raw[:, :], y_bank[:, 0:YW]).then_inc(y_ready, 1)

            def finish_b(i, k):
                b = 2 * i + k // 3 - 1
                if k % 3 == 0 and there(b, B):
                    v.wait_ge(y_turned, b + 1)
                    wait(v, yn_turned, b)
                    for heads, tiles, first, col in ((3, 4, 0, 0), (2, 2, 12, 3 * 128)):
                        width = 32 * tiles
                        blocks = bank_b[0:SQ, col:col + heads * width].rearrange(
                            "p (j t c) -> p j t c", j=heads, t=tiles)
                        at_rec = y_rec[:, first:first + heads * tiles].rearrange("p (j t) -> p j t", j=heads)
                        v.reciprocal(at_rec, blocks[:, :, :, DK * heads]).then_inc(rec_ready, 1)
                    v.wait_ge(rec_ready, 2 * (b + 1))
                    for heads, tiles, first, col in ((3, 4, 0, 0), (2, 2, 12, 3 * 128)):
                        width = 32 * tiles
                        for j in range(heads):
                            src = bank_b[0:SQ, col + j * width:col + (j + 1) * width].rearrange(
                                "p (t c) -> p t c", t=tiles)[:, :, DK * j:DK * (j + 1)]
                            rec = y_rec[:, first + j * tiles:first + (j + 1) * tiles]
                            out = yn[0:SQ, DK * first:DK * (first + heads * tiles)].rearrange(
                                "p (t c) -> p t c", t=tiles)[:, :, DK * j:DK * (j + 1)]
                            m = v.tensor_tensor(out, src, rec.unsqueeze(2).broadcast_to([SQ, tiles, DK]), ALU.mult)
                    m.then_inc(yn_ready, 1)

            def finish_c(i, k):
                b = 2 * i + k // 3 - 1
                if k % 3 == 1 and there(b, B):
                    par, pair = (1, i - 1) if k == 1 else (0, i)
                    r = slice(64 * par, 64 * par + SQ)
                    xb = t.x[r, pair, :] if isinstance(pair, int) else t.x[r, bass.ds(pair, 1), :].rearrange(
                        "p o d -> p (o d)")
                    v.wait_ge(out_done, b + 1)
                    v.tensor_tensor(o_tmp[r, :], bank_b[r, OUT_COL:OUT_COL + D], t.const_row[r, :], ALU.add)\
                        .then_inc(o_ready, 1)
                    v.wait_ge(o_ready, b + 1)
                    v.scalar_tensor_tensor(out=x_new[r, :], in0=o_tmp[r, :], scalar=0.0, in1=xb, op0=ALU.max,
                                           op1=ALU.add).then_inc(x_ready, 1)
                    v.scalar_tensor_tensor(out=xb, in0=o_tmp[r, :], scalar=0.0, in1=xb, op0=ALU.max, op1=ALU.add)
                    v.wait_ge(x_ready, b + 1)

            def statistics_a(i, k):
                b = 2 * i + k // 3 - 1
                if k % 3 == 1 and there(b, B):
                    r = slice(64, 64 + SQ) if k == 1 else slice(0, SQ)
                    v.bn_stats(x_stats[r, :], x_new[r, :]).then_inc(stats_ready, 1)
                    v.wait_ge(stats_ready, b + 1)

            def statistics_b(i, k):
                b = 2 * i + k // 3 - 1
                if k % 3 == 1 and there(b, B):
                    r = slice(64, 64 + SQ) if k == 1 else slice(0, SQ)
                    v.bn_aggr(mv_new[r, :], x_stats[r, :]).then_inc(mv_ready, 1)
                    v.wait_ge(mv_ready, b + 1)

            def statistics_c(i, k):
                b = 2 * i + k // 3 - 1
                if k % 3 == 1 and there(b, B):
                    r, pair = (slice(64, 64 + SQ), i - 1) if k == 1 else (slice(0, SQ), i)
                    mv = t.mv[r, pair, :] if isinstance(pair, int) else t.mv[r, bass.ds(pair, 1), :].rearrange(
                        "p o d -> p (o d)")
                    v.tensor_copy(mv, mv_new[r, :])

            def values(i, k):
                n, kk = at(i, k + 5), k + 5
                if there(n):
                    v.wait_ge(vals_done, n + 1)
                    wait(v, pv_done, NT * (n - 5))
                    va = t.v_aug[:, kk % PERIOD, :, :]
                    pv = bank_a[0:TK, :].rearrange("p (t c) -> p t c", t=NT)
                    v.tensor_tensor(va[:, :, 0:100].rearrange("p t (j c) -> p t j c", c=25)[:, :, :, 0:24],
                                    pv[:, :, 0:96].rearrange("p t (j c) -> p t j c", c=24),
                                    t.neg_bv[0:TK, 0:96].rearrange("p (j c) -> p j c", c=24).unsqueeze(1)
                                    .broadcast_to([TK, NT, 4, 24]), ALU.max)
                    v.tensor_tensor(va[:, :, 100:134].rearrange("p t (j c) -> p t j c", c=17)[:, :, :, 0:16],
                                    pv[:, :, 96:128].rearrange("p t (j c) -> p t j c", c=16),
                                    t.neg_bv[0:TK, 96:128].rearrange("p (j c) -> p j c", c=16).unsqueeze(1)
                                    .broadcast_to([TK, NT, 2, 16]), ALU.max).then_inc(v_ready, 1)

            def step(i, k):
                parts_of_max(i, k)
                pair_max(i, k, 0)
                finish_a(i, k)
                pair_max(i, k, 1)
                finish_c(i, k)
                pair_max(i, k, 2)
                statistics_a(i, k)
                pair_max(i, k, 3)
                statistics_b(i, k)
                pair_max(i, k, 4)
                statistics_c(i, k)
                values(i, k)
                pair_max(i, k, 5)
                finish_b(i, k)
                pair_max(i, k, 6)
                pair_max(i, k, 7)

            def parts_of_max(i, k):
                b = 2 * i + (k + 1) // 3
                if k % 3 != 2 or not there(b, B):
                    return
                maxima = max_part[:, (k + 1) // 3 % 2, :, :]
                v.wait_ge(max_read, HP * CPB * (b + 1))
                wait(v, mrow_done, 2 * b)
                v.tensor_reduce(max_cut[:, :, 0], maxima, AX_X, ALU.max, negate=True)
                v.tensor_reduce(neg_max[:, :], maxima, AX_X, ALU.max, negate=True).then_inc(neg_chain, 1)
                v.wait_ge(neg_chain, 2 * b + 1)
                v.tensor_tensor(max_cut[:, :, 1], neg_max[:, :], max_cut[:, :, 0], ALU.subtract)
                v.tensor_tensor(max_res[:, :], neg_max[:, :], max_cut[:, :, 0], ALU.subtract).then_inc(neg_chain, 1)
                v.wait_ge(neg_chain, 2 * b + 2)
                v.tensor_tensor(max_cut[:, :, 2], max_res[:, :], max_cut[:, :, 1], ALU.subtract)\
                    .then_inc(maxcut_ready, 1)

            links = [0]

            def chain(ins):
                links[0] += 1
                ins.then_inc(dve, 1)
                v.wait_ge(dve, links[0])

            v.memset(t.v_aug[:, :, :, 24:100:25], 1.0)
            v.memset(t.v_aug[:, :, :, 116:134:17], 1.0)
            v.memset(t.y_sum[:, :], 0.0)
            v.memset(yn[:, :], 0.0)
            v.memset(t.mv[:, :, :], 0.0)
            v.wait_ge(ident, 1)
            v.tensor_copy(t.ident_b[:, :], t.ident[:, :])
            def statistics(r):
                for n in range(PAIRS)[r]:
                    m = v.bn_stats(stats[:, n, :], t.x[:, n, :])
                chain(m)
                for n in range(PAIRS)[r]:
                    m = v.bn_aggr(mv0[:, n, :], stats[:, n, :])
                chain(m)
                v.tensor_scalar(st[:, 0, r], mv0[:, r, 1], EPS_LN, None, ALU.add).then_inc(var_done, 1)

            def centre(c):
                r = slice(4 * c, 4 * c + 4)
                return v.tensor_tensor(xn[:, r, :], t.x[:, r, :], of_rows(mv0[:, r, 0]), ALU.subtract)

            def scale(c):
                r = slice(4 * c, 4 * c + 4)
                v.tensor_tensor(xn[:, r, :], xn[:, r, :], of_rows(st[:, 1, r]), ALU.mult).then_inc(xn_done, 1)

            def cut(c):
                r = slice(8 * c, 8 * c + 8)
                v.wait_ge(q_ready, c + 1)
                chain(v.tensor_tensor(qres[:, r, :], q32[:, r, :], qp[:, 0, r, :], ALU.subtract))
                chain(v.tensor_copy(qp[:, 1, r, :], qres[:, r, :]))
                v.tensor_tensor(qp[:, 2, r, :], qres[:, r, :], qp[:, 1, r, :], ALU.subtract).then_inc(q_cut, 1)

            first, rest = slice(0, 4), slice(4, PAIRS)
            v.wait_ge(x_first, 64)
            statistics(first)
            chain(centre(0))
            v.wait_ge(std_done, 1)
            newton_step(v, chain, st[:, 1, first], st[:, 0, first], st[:, 2, first])
            scale(0)
            v.wait_ge(x_in, 64)
            statistics(rest)
            for c in range(1, G):
                m = centre(c)
            chain(m)
            cut(0)
            v.wait_ge(std_done, 2)
            newton_step(v, chain, st[:, 1, rest], st[:, 0, rest], st[:, 2, rest])
            for c in range(1, G):
                scale(c)
            v.wait_ge(w_in, 16 * 5)
            v.tensor_scalar(t.neg_bv[:, :], t.neg_bv[:, :], -1.0, None, ALU.mult)
            v.tensor_copy(bv_wide[:, :], bv_col[:, 0:1].broadcast_to([D, D])).then_inc(bvw, 1)
            v.wait_ge(c_done, 1)
            v.tensor_tensor(t.const_row[:, :], ps[4][:, 0:D], bo_row[:, :], ALU.add).then_inc(row_ready, 1)
            for c in range(1, G):
                cut(c)

            step(-1, 0)
            steps(v, step)
            finish_a(NCH // PERIOD, 0)
            finish_b(NCH // PERIOD, 0)
            finish_c(NCH // PERIOD, 1)
            statistics_a(NCH // PERIOD, 1)
            statistics_b(NCH // PERIOD, 1)
            statistics_c(NCH // PERIOD, 1)

        @block.tensor
        def _(pe):
            def scores(i, k, tile):
                n = at(i, k)
                if not there(n):
                    return
                if k % 3 == 0 and tile == 0:
                    b = 2 * i + k // 3
                    if isinstance(b, int) and b == 0:
                        pe.wait_ge(ones_spread, 16 * (PERIOD - 1))
                    pe.wait_ge(qturn_ready, b + 1)
                    pe.wait_ge(shift_ready, 2 * (b + 1))
                for half in range(2):
                    j = 2 * NT * k + 2 * tile + half
                    wait(pe, probs_ready, 2 * NT * n + 2 * tile + half - 2)
                    for p in range(4):
                        g = 4 * half + p
                        m = pe.matmul(s_bank[j % 3][0:TK, PQ * p:PQ * (p + 1)],
                                      t.k_stack[:, k % PERIOD, g, TK * tile:TK * (tile + 1)],
                                      t.q_turn[:, k // 3 % 2, PQ * g:PQ * (g + 1)], start=True, stop=True)
                    m.then_inc(scores_done, 1)

            def max_scores(i, k, pair):
                n, kk = at(i, k + 4), k + 4
                if not there(n):
                    return
                if pair == 0:
                    if isinstance(n, int) and n == 0:
                        pe.wait_ge(row_ready, 1)
                        pe.wait_ge(q_ready, G)
                    pe.wait_ge(stack_loaded[kk % PERIOD], 16 * NSLOT * (i + kk // PERIOD + 1))
                    if kk % CPB == 0:
                        pe.wait_ge(qmax_ready, 2 * i + kk // CPB + 1)
                wait(pe, max_read, HP * n + pair - 1)
                pe.matmul(m_bank[pair % 2][0:PQ, 0:CH], q_max[:, kk // CPB % 2, PQ * pair:PQ * (pair + 1)],
                          t.k_stack[0:ROWS, kk % PERIOD, pair, :], start=True, stop=True).then_inc(maxs_done, 1)

            def pv(i, k, tile):
                n = at(i, k)
                if not there(n):
                    return
                first, last = k % 3 == 0 and tile == 0, k % 3 == 2 and tile == NT - 1
                if first:
                    wait(pe, y_ready, 2 * i + k // 3)
                if tile == 0:
                    pe.wait_ge(v_ready, n + 1)
                pe.wait_ge(probs_ready, 2 * NT * n + 2 * tile + 2)
                for head, cnt, col_tile, col, vcol in GROUPS:
                    wd = DK * cnt + 1
                    m = pe.matmul(y_bank[32 * col_tile:32 * col_tile + wd, col:col + SQ * cnt],
                                  t.v_aug[:, k % PERIOD, tile, vcol:vcol + wd],
                                  probs[0:TK, (NT * k + tile) % 3, SQ * head:SQ * (head + cnt)],
                                  start=first and col == 0, stop=last, skip_group_check=True)
                m.then_inc(pv_done, 1)

            def keys(i, k):
                n = at(i, k + 6)
                if not there(n):
                    return
                pe.wait_ge(ctx_loaded[k % 3], 16 * (2 * i + (k + 6) // 3 + 1))
                wait(pe, k1_ready, n)
                if k % 3 == 1:
                    wait(pe, o_ready, 2 * i + k // 3)
                if k % 3 == 0:
                    wait(pe, shift_ready, 2 * (2 * i + k // 3 + 1))
                pe.matmul(bank_b[:, 0:CH], t.wk[:, :], cT[:, k % 3, :], start=True, stop=True).then_inc(keys_done, 1)

            def values(i, k):
                n, kk = at(i, k + 5), k + 5
                if not there(n):
                    return
                wait(pe, v_ready, n)
                if k % 3 == 0:
                    wait(pe, shift_ready, 2 * (2 * i + k // 3) + 1)
                for tile in range(NT):
                    m = pe.matmul(bank_a[0:TK, D * tile:D * (tile + 1)], cT[:, kk % 3, TK * tile:TK * (tile + 1)],
                                  t.wv[:, :], start=True, stop=True)
                m.then_inc(vals_done, 1)

            def max_rows(i, k):
                b = 2 * i + (k + 1) // 3
                if k % 3 != 2 or not there(b, B):
                    return
                pe.wait_ge(maxcut_ready, b + 1)
                n = at(i, k)
                if not there(n + 6):
                    pe.wait_ge(o_ready, b - 1)
                for half, bank in enumerate((bank_a, bank_b)):
                    if half == 0:
                        pe.wait_ge(v_ready, min_chunk(n + 6))
                    else:
                        pe.wait_ge(k1_ready, min_chunk(n + 7))
                    for p in range(4):
                        m = pe.matmul(bank[SHIFT:SHIFT + 3, PQ * p:PQ * (p + 1)], max_cut[:, 4 * half + p, :],
                                      t.ident_b[0:PQ, 0:PQ], start=True, stop=True)
                    m.then_inc(mrow_done, 1)

            def min_chunk(n):
                return min(n, NCH) if isinstance(n, int) else n

            def y_turn(i, k):
                b = 2 * i + k // 3 - 1
                if k % 3 != 0 or not there(b, B):
                    return
                pe.wait_ge(y_ready, b + 1)
                pe.wait_ge(k1_ready, min_chunk(at(i, k + 7)))
                pe.transpose(bank_b[:, 0:128], y_raw[:, 0:128], t.ident[:, :])
                for j in range(1, 5):
                    rows, col = (128, 128 * j) if j < 3 else (64, 3 * 128 + 64 * (j - 3))
                    m = pe.transpose(bank_b[0:SQ, col:col + rows], y_raw[0:rows, SQ * j:SQ * (j + 1)],
                                     t.ident[0:rows, 0:rows])
                m.then_inc(y_turned, 1)

            def y_back(i, k):
                b = 2 * i + k // 3 - 1
                if k % 3 != 0 or not there(b, B):
                    return
                pe.wait_ge(yn_ready, b + 1)
                pe.transpose(bank_b[:, 0:128], yn[:, :], t.ident[:, :]).then_inc(yn_turned, 1)

            def out_proj(i, k):
                b = 2 * i + k // 3 - 1
                if k % 3 != 1 or not there(b, B):
                    return
                r = 64 if k == 1 else 0
                pe.wait_ge(ynT_ready, b + 1)
                pe.matmul(bank_b[r:r + SQ, OUT_COL:OUT_COL + D], ynT[:, :], t.wo[:, :], start=True,
                          stop=True).then_inc(out_done, 1)

            def step(i, k):
                scores(i, k, 0)
                max_scores(i, k, 0)
                pv(i if k else i - 1, k - 1 if k else PERIOD - 1, 3)
                max_scores(i, k, 1)
                scores(i, k, 1)
                out_proj(i, k)
                max_scores(i, k, 2)
                pv(i, k, 0)
                max_scores(i, k, 3)
                keys(i, k)
                max_scores(i, k, 4)
                values(i, k)
                max_scores(i, k, 5)
                scores(i, k, 2)
                y_turn(i, k)
                max_scores(i, k, 6)
                pv(i, k, 1)
                max_rows(i, k)
                scores(i, k, 3)
                max_scores(i, k, 7)
                pv(i, k, 2)
                y_back(i, k)

            pe.wait_ge(ident, 1)

            def turn_x(c):
                pe.wait_ge(xn_done, c + 1)
                for n in range(4):
                    m = pe.transpose(ps[c][:, 128 * n:128 * n + 128], xn[:, 4 * c + n, :], t.ident[:, :])
                m.then_inc(xT_done, 1)

            def queries(c):
                pe.wait_ge(xT_copied, c + 1)
                pe.matmul(ps[c][:, 0:8 * SQ], wq[:, :], xnT[:, 4 * c:4 * c + 4, :, 0:SQ], start=True,
                          stop=True).then_inc(q_done, 1)

            turn_x(0)
            pe.wait_ge(wqk_in, 16 * 4)
            queries(0)
            step(-1, 0)
            for c in range(1, G):
                turn_x(c)
            pe.wait_ge(w_in, 16 * 5)
            pe.wait_ge(bvw, 1)
            pe.matmul(ps[4][:, 0:D], bv_wide[:, :], t.wo[:, :], start=True, stop=True).then_inc(c_done, 1)
            for c in range(1, G):
                queries(c)
            steps(pe, step)
            pv(NCH // PERIOD - 1, PERIOD - 1, 3)
            y_turn(NCH // PERIOD, 0)
            y_back(NCH // PERIOD, 0)
            out_proj(NCH // PERIOD, 1)


class Tiles:
    pass


def program(nc, ins, out):
    with ExitStack() as ctx:
        t = Tiles()

        def sb(name, shape, dt=F32):
            return ctx.enter_context(nc.sbuf_tensor(name, shape, dt))

        t.x = sb("x", [128, PAIRS, D])
        t.ident = sb("ident", [128, 128])
        t.mv = sb("mv", [128, PAIRS, 2])
        t.g1 = sb("g1", [D, 1])
        t.g2 = sb("g2", [D, 1])
        t.ff_wq = sb("ff_wq", [D, D])
        t.wkc = sb("wkc", [D, FH, FDK])
        t.wvc = sb("wvc", [D, FDK])
        t.ff_wo = sb("ff_wo", [D, D])
        t.wr = sb("wr", [D, NE])
        t.ebias = sb("ebias", [128, NE])
        with ExitStack() as attn:
            def sa(name, shape, dt=F32):
                return attn.enter_context(nc.sbuf_tensor(name, shape, dt))

            t.ident_b = sa("ident_b", [128, 128], BF16)
            t.wk = sa("wk", [D, D])
            t.bk = sa("bk", [D, 1])
            t.wv = sa("wv", [D, D])
            t.neg_bv = sa("neg_bv", [128, D])
            t.wo = sa("wo", [D, D])
            t.const_row = sa("const_row", [128, D])
            t.k_stack = sa("k_stack", [128, PERIOD, HP, CH], BF16)
            t.q_turn = sa("q_turn", [128, 2, HP * PQ], BF16)
            t.v_aug = sa("v_aug", [TK, PERIOD, NT, VW])
            t.q_stack = sa("q_stack", [ROWS, HP, 2, B, SQ], BF16)
            t.y_sum = attn.enter_context(nc.psum_tensor("y_sum", [128, 512], F32))
            cross_attention(nc, ins, t)
        feed_forward(nc, ins, t, out)


def feed_forward(nc, ins, t, out):
    with ExitStack() as ctx:
        def sb(name, shape, dt=F32):
            return ctx.enter_context(nc.sbuf_tensor(name, shape, dt))

        def sem(name):
            return ctx.enter_context(nc.semaphore(name))

        g1, g2, wq, wkc, wvc, wo, wr, ebias = t.g1, t.g2, t.ff_wq, t.wkc, t.wvc, t.ff_wo, t.wr, t.ebias
        xl = sb("xl", [128, PAIRS, D])
        nx = sb("nx", [128, PAIRS, D])
        st = sb("ff_st", [128, 7, PAIRS])
        xl_stats = sb("xl_stats", [128, PAIRS, 6])
        xl_mv = sb("xl_mv", [128, PAIRS, 2])
        spare = sb("spare", [128, 1])
        nT = sb("nT", [D, W])
        q_head = sb("q_head", [D, FH, W])
        kT = sb("kT", [D, W])
        vc = sb("vc", [128, B, FDK])
        p = sb("p", [128, PAIRS * FH, SQ])
        pmax = sb("pmax", [128, PAIRS * FH])
        psum_ = sb("psum_", [128, PAIRS * FH])
        prec = sb("prec", [128, PAIRS * FH])
        pT = sb("pT", [128, PAIRS * FH, 128])
        oT = sb("oT", [D, W])
        hmask = sb("hmask", [D, FH])
        rank = sb("rank", [128, NE])
        rw = sb("rw", [128, PAIRS, NE])
        hot = sb("hot", [128, 2, PAIRS, NE])
        tmp = sb("tmp", [128, PAIRS, NE])
        rs = sb("rs", [128, 8, PAIRS])
        comb = sb("comb", [128, NE + 1, PAIRS])
        comb_e = sb("comb_e", [128, SLOTS, PAIRS])
        w1 = sb("w1", [D, SLOTS, FF])
        w3 = sb("w3", [D, SLOTS, FF])
        w2 = sb("w2", [FF, SLOTS, D])
        th = sb("th", [FF, 3, 8 * SQ])
        ga = sb("ga", [FF, 2, 8 * SQ])
        hid = sb("hid", [FF, 3, 8, 64])
        bank = [ctx.enter_context(nc.psum_tensor(f"ff_bank{i}", [128, 512], F32)) for i in range(8)]

        w_slot = [sem(f"w_slot{j}") for j in range(SLOTS)]
        dve = sem("ff_dve")
        rows_zero = sem("rows_zero")
        squares_ready = sem("squares_ready")
        roots_ready = sem("roots_ready")
        x_summed = sem("x_summed")
        ranked = sem("ranked")
        nx_ready = sem("nx_ready")
        nx_turned = sem("nx_turned")
        nT_ready = sem("nT_ready")
        hmask_ready = sem("hmask_ready")
        q_done = sem("ff_q_done")
        k_done = sem("ff_k_done")
        q01_taken = sem("q01_taken")
        q23_taken = sem("q23_taken")
        vc_done = sem("vc_done")
        vc_taken = sem("vc_taken")
        s_done = sem("s_done")
        less_max = sem("less_max")
        p_exp = sem("p_exp")
        p_ready = sem("p_ready")
        p_turned = sem("p_turned")
        pT_ready = sem("pT_ready")
        o_done = sem("ff_o_done")
        oT_ready = sem("oT_ready")
        proj_done = sem("proj_done")
        xl_ready = sem("xl_ready")
        logit_done = sem("logit_done")
        r_less = sem("r_less")
        r_exp = sem("r_exp")
        gate_less = sem("gate_less")
        gate_exp = sem("gate_exp")
        up_done = sem("up_done")
        th_ready = sem("th_ready")
        ga_ready = sem("ga_ready")
        hid_ready = sem("hid_ready")
        down_done = sem("down_done")
        acc_ready = sem("acc_ready")
        comb_ready = sem("comb_ready")
        stored = sem("stored")

        NC = 8
        s_bank, pt_bank, o_bank = bank[2:5], bank[5:7], bank[0:2]
        proj_bank = [bank[7], bank[7], bank[7], bank[2]]
        turn_bank = [bank[0:4], [bank[4], bank[5], bank[6], bank[5]]]
        gate_bank, up_bank, down_bank = bank[0:3], bank[3:6], bank[6:8]
        block = ctx.enter_context(nc.Block())

        @block.sync
        def _(sp):
            def load(e, j):
                for dst, name in ((w1, "W1"), (w3, "W3"), (w2, "W2")):
                    src = ins[name][e] if isinstance(e, int) else \
                        ins[name][bass.ds(e, 1)].rearrange("o p f -> (o p) f")
                    sp.dma_start(dst[:, j, :], src).then_inc(w_slot[j], 16)

            for j in range(SLOTS):
                load(j, j)
            with sp.Fori(1, (NE + 1) // SLOTS) as i:
                for j in range(SLOTS):
                    e = sp.snap(i * SLOTS + j)
                    sp.wait_ge(down_done, i * (G * SLOTS) + G * (j + 1 - SLOTS))
                    load(e, j)
            for c in range(G):
                sp.wait_ge(acc_ready, G * NE + c + 1)
                for par in range(2):
                    sp.dma_start(out.rearrange("(n par) q d -> par q n d", par=2)[par][:, 4 * c:4 * c + 4, :],
                                 t.x[64 * par:64 * par + SQ, 4 * c:4 * c + 4, :]).then_inc(stored, 16)
            sp.wait_ge(stored, 16 * 2 * G)

        @block.gpsimd
        def _(g):
            g.memset(vc[:, :, :], 0.0).then_inc(rows_zero, 1)
            g.memset(pT[:, :, :], 0.0).then_inc(rows_zero, 1)
            for e in range(NE):
                g.memset(rank[:, e:e + 1], float(NE - e))
            g.memset(hid[:, :, :, SQ:64], 0.0).then_inc(ranked, 1)
            for c in range(G):
                g.wait_ge(xl_ready, c + 1)
                g.tensor_tensor(t.x[:, 4 * c:4 * c + 4, :], t.x[:, 4 * c:4 * c + 4, :], xl[:, 4 * c:4 * c + 4, :],
                                ALU.add).then_inc(x_summed, 1)

        @block.vector
        def _(v):
            links = [0]

            def chain(ins):
                links[0] += 1
                ins.then_inc(dve, 1)
                v.wait_ge(dve, links[0])

            def group(c):
                return (slice(None), slice(4 * c, 4 * c + 4), slice(None))

            mean, var = t.mv[:, :, 0], t.mv[:, :, 1]
            chain(v.tensor_scalar(st[:, 0, :], t.mv[:, :, 1], EPS_LN, None, ALU.add))
            v.scalar_tensor_tensor(out=st[:, 1, :], in0=st[:, 0, :], scalar=EPS_RMS, in1=t.mv[:, :, 1],
                                   op0=ALU.mult, op1=ALU.add).then_inc(squares_ready, 1)
            m = v.tensor_tensor(xl[group(0)], t.x[group(0)], of_rows(t.mv[:, 0:4, 0]), ALU.subtract)
            chain(m)
            v.wait_ge(roots_ready, 1)
            newton_step(v, chain, st[:, 2:4, :], st[:, 0:2, :], st[:, 4:6, :])
            for c in range(G):
                r = slice(4 * c, 4 * c + 4)
                if c:
                    chain(v.tensor_tensor(xl[group(c)], t.x[group(c)], of_rows(t.mv[:, r, 0]), ALU.subtract))
                v.tensor_tensor(nx[group(c)], xl[group(c)], of_rows(st[:, 3, r]), ALU.mult).then_inc(nx_ready, 1)
            v.tensor_reduce(hmask[:, :], t.ident[:, :].rearrange("p (h x) -> p h x", x=FDK), AX_X, ALU.add)\
                .then_inc(hmask_ready, 1)
            v.wait_ge(hmask_ready, 1)
            for c in range(G):
                r = slice(4 * c, 4 * c + 4)
                m = v.tensor_tensor(xl[group(c)], xl[group(c)], of_rows(st[:, 2, r]), ALU.mult)
                if c == G - 1:
                    chain(m)
                v.wait_ge(q_done, c + 1)
                for h in range(2):
                    m = v.tensor_scalar(q_head[:, h, 512 * c:512 * c + 512], bank[c][:, :], hmask[:, h:h + 1], None,
                                        ALU.mult)
                m.then_inc(q01_taken, 1)
            v.wait_ge(rows_zero, 1)
            for c in range(2):
                v.wait_ge(vc_done, c + 1)
                v.tensor_copy(vc[0:SQ, 16 * c:16 * c + 16, :], bank[c][0:SQ, :].rearrange("p (b d) -> p b d", d=FDK))\
                    .then_inc(vc_taken, 1)

            def less(c):
                r = slice(8 * c, 8 * c + 8)
                s = s_bank[c % 3][:, 0:8 * SQ].rearrange("p (r k) -> p r k", k=SQ)
                v.wait_ge(s_done, c + 1)
                chain(v.tensor_reduce(pmax[:, r], s, AX_X, ALU.max))
                v.tensor_tensor(p[:, r, :], s, pmax[:, r].unsqueeze(2).broadcast_to([128, 8, SQ]), ALU.subtract)\
                    .then_inc(less_max, 1)

            def normalise(c):
                r = slice(8 * c, 8 * c + 8)
                v.wait_ge(p_exp, c + 1)
                chain(v.tensor_reduce(psum_[:, r], p[:, r, :], AX_X, ALU.add))
                chain(v.reciprocal(prec[:, r], psum_[:, r]))
                v.tensor_tensor(p[:, r, :], p[:, r, :], prec[:, r].unsqueeze(2).broadcast_to([128, 8, SQ]), ALU.mult)\
                    .then_inc(p_ready, 1)

            def residual(c):
                v.wait_ge(proj_done, c + 1)
                r = slice(4 * c, 4 * c + 4)
                o4 = proj_bank[c][:, :].rearrange("p (n d) -> p n d", d=D)
                v.tensor_tensor(xl[group(c)], o4, xl[group(c)], ALU.add).then_inc(xl_ready, 1)
                v.wait_ge(xl_ready, c + 1)
                for n in range(4 * c, 4 * c + 4):
                    m = v.bn_stats(xl_stats[:, n, :], xl[:, n, :])
                chain(m)
                for n in range(4 * c, 4 * c + 4):
                    m = v.bn_aggr(xl_mv[:, n, :], xl_stats[:, n, :])
                chain(m)
                chain(v.tensor_tensor(st[:, 6, r], xl_mv[:, r, 0], xl_mv[:, r, 0], ALU.mult))
                v.scalar_tensor_tensor(out=st[:, 0, r], in0=st[:, 6, r], scalar=EPS_RMS, in1=xl_mv[:, r, 1],
                                       op0=ALU.add, op1=ALU.add).then_inc(squares_ready, 1)

            def norm(c):
                r = slice(4 * c, 4 * c + 4)
                v.wait_ge(roots_ready, c + 2)
                newton_step(v, chain, st[:, 2, r], st[:, 0, r], st[:, 4, r])
                v.tensor_tensor(nx[group(c)], xl[group(c)], of_rows(st[:, 2, r]), ALU.mult).then_inc(nx_ready, 1)

            less(0)
            for c in range(1, NC):
                less(c)
                normalise(c - 1)
                if c == 5:
                    residual(0)
            normalise(NC - 1)
            residual(1)
            norm(0)
            norm(1)
            residual(2)
            norm(2)
            residual(3)
            norm(3)

            e8 = [128, PAIRS, NE]
            lg = bank[7][:, 0:PAIRS * NE].rearrange("p (n e) -> p n e", e=NE)

            def over_experts(a):
                return a.unsqueeze(2).broadcast_to(e8)

            def logits_less_max():
                v.wait_ge(logit_done, G)
                chain(v.tensor_tensor(rw[:, :, :], lg, ebias[:, :].unsqueeze(1).broadcast_to(e8), ALU.add))
                chain(v.tensor_reduce(rs[:, 0, :], rw[:, :, :], AX_X, ALU.max))
                v.tensor_tensor(rw[:, :, :], rw[:, :, :], over_experts(rs[:, 0, :]), ALU.subtract)\
                    .then_inc(r_less, 1)

            def probabilities():
                v.wait_ge(r_exp, 1)
                chain(v.tensor_reduce(rs[:, 1, :], rw[:, :, :], AX_X, ALU.add))
                chain(v.reciprocal(rs[:, 2, :], rs[:, 1, :]))
                chain(v.tensor_tensor(rw[:, :, :], rw[:, :, :], over_experts(rs[:, 2, :]), ALU.mult))

            def largest(k):
                top, first = rs[:, 3 + k, :], rs[:, 5, :]
                chain(v.tensor_reduce(top, rw[:, :, :], AX_X, ALU.max))
                chain(v.tensor_tensor(tmp[:, :, :], rw[:, :, :], over_experts(top), ALU.is_ge))
                chain(v.tensor_tensor(tmp[:, :, :], tmp[:, :, :], rank[:, :].unsqueeze(1).broadcast_to(e8), ALU.mult))
                chain(v.tensor_reduce(first, tmp[:, :, :], AX_X, ALU.max))
                chain(v.tensor_tensor(hot[:, k, :, :], tmp[:, :, :], over_experts(first), ALU.is_equal))
                if k == 0:
                    chain(v.scalar_tensor_tensor(out=rw[:, :, :], in0=hot[:, 0, :, :], scalar=-2.0, in1=rw[:, :, :],
                                                 op0=ALU.mult, op1=ALU.add))
                else:
                    v.tensor_tensor(rs[:, 6, :], rs[:, 4, :], rs[:, 3, :], ALU.subtract).then_inc(gate_less, 1)

            def combine():
                v.wait_ge(gate_exp, 1)
                chain(v.tensor_scalar(rs[:, 7, :], rs[:, 6, :], 1.0, None, ALU.add))
                chain(v.reciprocal(rs[:, 0, :], rs[:, 7, :]))
                chain(v.tensor_tensor(rs[:, 1, :], rs[:, 6, :], rs[:, 0, :], ALU.mult))
                chain(v.tensor_tensor(tmp[:, :, :], hot[:, 0, :, :], over_experts(rs[:, 0, :]), ALU.mult))
                chain(v.tensor_tensor(rw[:, :, :], hot[:, 1, :, :], over_experts(rs[:, 1, :]), ALU.mult))
                chain(v.tensor_tensor(comb[:, 1:NE + 1, :].rearrange("p e n -> p n e"), tmp[:, :, :], rw[:, :, :],
                                      ALU.add))

            def hidden(u, k):
                v.wait_ge(th_ready, u + 1)
                v.scalar_tensor_tensor(out=ga[:, k % 2, :], in0=th[:, k % 3, :], scalar=1.0,
                                       in1=gate_bank[k % 3][:, 0:8 * SQ], op0=ALU.add, op1=ALU.mult)\
                    .then_inc(ga_ready, 1)
                v.wait_ge(ga_ready, u + 1)
                wait(v, down_done, u - 2)
                v.scalar_tensor_tensor(out=hid[:, k % 3, :, 0:SQ],
                                       in0=up_bank[k % 3][:, 0:8 * SQ].rearrange("p (n q) -> p n q", q=SQ),
                                       scalar=0.5, in1=ga[:, k % 2, :].rearrange("p (n q) -> p n q", q=SQ),
                                       op0=ALU.mult, op1=ALU.mult).then_inc(hid_ready, 1)

            def collect(u, k):
                v.wait_ge(down_done, u + 1)
                wait(v, acc_ready, u + 1 - G)
                if isinstance(u, int) and u < G:
                    v.wait_ge(x_summed, u + 1)
                k %= UNITS
                c = k % G
                for n in range(4):
                    xs = t.x[:, 4 * c + n, :]
                    m = v.scalar_tensor_tensor(out=xs, in0=down_bank[k % 2][:, D * n:D * n + D],
                                               scalar=comb_e[:, k // G, 4 * c + n:4 * c + n + 1],
                                               in1=xs, op0=ALU.mult, op1=ALU.add)
                m.then_inc(acc_ready, 1)

            def weights(i, j):
                e = SLOTS * i + j
                src = comb[:, e, :] if isinstance(e, int) else comb[:, bass.ds(e, 1), :].rearrange("p o n -> p (o n)")
                v.tensor_copy(comb_e[:, j, :], src).then_inc(comb_ready, 1)
                v.wait_ge(comb_ready, e + 1)

            v.memset(comb[:, 0, :], 1.0).then_inc(comb_ready, 1)
            v.wait_ge(comb_ready, 1)
            v.tensor_copy(comb_e[:, 0, :], comb[:, 0, :])
            v.wait_ge(ranked, 1)
            router = {0: logits_less_max, 1: probabilities, 2: lambda: largest(0), 3: lambda: largest(1), 4: combine}

            def units(i):
                for k in range(UNITS):
                    u = UNITS * i + k
                    hidden(u, k)
                    if isinstance(i, int) and k in router:
                        router[k]()
                    if there(u - 2):
                        collect(u - 2, k - 2)
                    if k % G == 1 and not (isinstance(i, int) and k == 1):
                        weights(i, k // G)

            units(0)
            with v.Fori(1, (NE + 1) // SLOTS) as i:
                units(i)
            for k in (UNITS - 2, UNITS - 1):
                collect(G * NE + G - UNITS + k, k)

        @block.scalar
        def _(a):
            def load_table(func):
                a.activation(spare[:, :], t.ident[:, 0:1], func)

            def turn(n, c, g):
                a.wait_ge(nx_turned, G * n + c + 1)
                a.activation(nT[:, 512 * c:512 * c + 512], turn_bank[n][c][:, :], ACT.Copy, scale=g)\
                    .then_inc(nT_ready, 1)

            def roots(c):
                r = slice(4 * c, 4 * c + 4)
                a.wait_ge(squares_ready, c + 2)
                a.activation(st[:, 2, r], st[:, 0, r], ACT.Sqrt).then_inc(roots_ready, 1)

            load_table(ACT.Sqrt)
            a.wait_ge(squares_ready, 1)
            a.activation(st[:, 2:4, :], st[:, 0:2, :], ACT.Sqrt).then_inc(roots_ready, 1)
            for c in range(G):
                turn(0, c, g1[:, 0:1])
            a.wait_ge(hmask_ready, 1)
            for c in range(G):
                a.wait_ge(k_done, c + 1)
                a.copy(kT[:, 512 * c:512 * c + 512], bank[4 + c][:, :])
                a.wait_ge(q01_taken, c + 1)
                for h in range(2, FH):
                    m = a.activation(q_head[:, h, 512 * c:512 * c + 512], bank[c][:, :], ACT.Copy,
                                     scale=hmask[:, h:h + 1])
                m.then_inc(q23_taken, 1)

            a.wait_ge(rows_zero, 2)

            def turned_back(c):
                for n in (2 * c, 2 * c + 1):
                    a.wait_ge(p_turned, n + 1)
                    a.copy(pT[0:SQ, FH * n:FH * n + FH, :], pt_bank[n % 2][0:SQ, :].rearrange("p (h q) -> p h q", h=FH))\
                        .then_inc(pT_ready, 1)

            def attended(c):
                a.wait_ge(o_done, c + 1)
                a.copy(oT[:, 512 * c:512 * c + 512], o_bank[c % 2][:, :]).then_inc(oT_ready, 1)

            for c in range(NC):
                a.wait_ge(less_max, c + 1)
                a.activation(p[:, 8 * c:8 * c + 8, :], p[:, 8 * c:8 * c + 8, :], ACT.Exp, scale=FDK ** -0.5)\
                    .then_inc(p_exp, 1)
                if c >= 2:
                    turned_back(c - 2)
                if c >= 4 and c % 2 == 0:
                    attended(c // 2 - 2)
            turned_back(NC - 2)
            attended(2)
            roots(0)
            roots(1)
            turned_back(NC - 1)
            attended(3)
            turn(1, 0, g2[:, 0:1])
            turn(1, 1, g2[:, 0:1])
            roots(2)
            turn(1, 2, g2[:, 0:1])
            roots(3)
            load_table(ACT.Tanh)
            turn(1, 3, g2[:, 0:1])

            def squash(u, k):
                a.wait_ge(up_done, u + 1)
                wait(a, ga_ready, u - 2)
                a.activation(th[:, k % 3, :], gate_bank[k % 3][:, 0:8 * SQ], ACT.Tanh, scale=0.5)\
                    .then_inc(th_ready, 1)

            for k in range(UNITS):
                squash(k, k)
                if k == 1:
                    a.wait_ge(r_less, 1)
                    a.activation(rw[:, :, :], rw[:, :, :], ACT.Exp).then_inc(r_exp, 1)
                if k == 3:
                    a.wait_ge(gate_less, 1)
                    a.activation(rs[:, 6, :], rs[:, 6, :], ACT.Exp).then_inc(gate_exp, 1)
            with a.Fori(1, (NE + 1) // SLOTS) as i:
                for k in range(UNITS):
                    squash(UNITS * i + k, k)

        @block.tensor
        def _(pe):
            def turn(n, c):
                pe.wait_ge(nx_ready, G * n + c + 1)
                for k in range(4):
                    m = pe.transpose(turn_bank[n][c][:, 128 * k:128 * k + 128], nx[:, 4 * c + k, :], t.ident[:, :])
                m.then_inc(nx_turned, 1)

            def queries_keys(c):
                pe.wait_ge(nT_ready, c + 1)
                cols = nT[:, 512 * c:512 * c + 512]
                pe.matmul(bank[c][:, :], wq[:, :], cols, start=True, stop=True).then_inc(q_done, 1)
                pe.matmul(bank[4 + c][:, :], wkc[:, :, :].rearrange("p h d -> p (h d)"), cols, start=True,
                          stop=True).then_inc(k_done, 1)

            turn(0, 0)
            for c in range(1, G):
                turn(0, c)
                queries_keys(c - 1)
            queries_keys(G - 1)
            for c in range(2):
                pe.wait_ge(q01_taken, c + 1)
                pe.wait_ge(q23_taken, c + 1)
                for b in range(16):
                    m = pe.matmul(bank[c][0:SQ, FDK * b:FDK * b + FDK],
                                  nT[:, 64 * (16 * c + b):64 * (16 * c + b) + SQ], wvc[:, :], start=True, stop=True)
                m.then_inc(vc_done, 1)

            def scores(c):
                pe.wait_ge(q01_taken, G)
                pe.wait_ge(q23_taken, G)
                if c >= 3:
                    pe.wait_ge(less_max, c - 2)
                for n in range(2):
                    for h in range(FH):
                        for par in range(2):
                            tok = 64 * (2 * (2 * c + n) + par)
                            m = pe.matmul(s_bank[c % 3][64 * par:64 * par + 64,
                                                        SQ * (FH * n + h):SQ * (FH * n + h) + SQ],
                                          q_head[:, h, tok:tok + 64], kT[:, tok:tok + SQ], start=True, stop=True)
                m.then_inc(s_done, 1)

            def turn_p(c):
                pe.wait_ge(p_ready, c + 1)
                for n in (2 * c, 2 * c + 1):
                    if n >= 2:
                        pe.wait_ge(pT_ready, n - 1)
                    for h in range(FH):
                        m = pe.transpose(pt_bank[n % 2][0:SQ, 128 * h:128 * h + 128], p[:, FH * n + h, :],
                                         t.ident[:, :])
                    m.then_inc(p_turned, 1)

            def attend(c):
                pe.wait_ge(vc_taken, 2)
                for n in (2 * c, 2 * c + 1):
                    g = n // 4
                    pe.wait_ge(pT_ready, n + 1)
                    if g >= 2:
                        pe.wait_ge(oT_ready, g - 1)
                    for par in range(2):
                        for h in range(FH):
                            col = 64 * (2 * (n % 4) + par)
                            m = pe.matmul(o_bank[g % 2][FDK * h:FDK * h + FDK, col:col + 64],
                                          vc[:, 2 * n + par, :], pT[:, FH * n + h, 64 * par:64 * par + 64],
                                          start=True, stop=True)
                    if n % 4 == 3:
                        m.then_inc(o_done, 1)

            def project(c):
                pe.wait_ge(oT_ready, c + 1)
                if c < G - 1:
                    if c:
                        pe.wait_ge(xl_ready, c)
                else:
                    pe.wait_ge(less_max, NC)
                for n in range(4):
                    tok = 128 * (4 * c + n)
                    m = pe.matmul(proj_bank[c][:, D * n:D * n + D], oT[:, tok:tok + 128], wo[:, :], start=True,
                                  stop=True)
                m.then_inc(proj_done, 1)

            for c in range(NC):
                scores(c)
                if c >= 2:
                    turn_p(c - 2)
                if c >= 3:
                    attend(c - 3)
                if c >= 5 and c % 2:
                    project((c - 5) // 2)
            turn_p(NC - 2)
            attend(NC - 3)
            turn_p(NC - 1)
            attend(NC - 2)
            project(2)
            attend(NC - 1)
            project(3)
            def up(u, k):
                c, slot = k % G, k // G
                wait(pe, hid_ready, u - 2)
                cols = nT[:, 512 * c:512 * c + 512].rearrange("p (n q) -> p n q", q=64)[:, :, 0:SQ]
                pe.matmul(gate_bank[k % 3][:, 0:8 * SQ], w1[:, slot, :], cols, start=True, stop=True)
                pe.matmul(up_bank[k % 3][:, 0:8 * SQ], w3[:, slot, :], cols, start=True, stop=True)\
                    .then_inc(up_done, 1)

            def down(u, k):
                k %= UNITS
                pe.wait_ge(hid_ready, u + 1)
                wait(pe, acc_ready, u - 1)
                for n in range(4):
                    m = pe.matmul(down_bank[k % 2][:, D * n:D * n + D],
                                  hid[:, k % 3, 2 * n:2 * n + 2, :].rearrange("p n q -> p (n q)"),
                                  w2[:, k // G, :], start=True, stop=True)
                m.then_inc(down_done, 1)

            def logits(c):
                pe.wait_ge(nT_ready, G + c + 1)
                for n in range(4 * c, 4 * c + 4):
                    m = pe.matmul(bank[7][:, NE * n:NE * n + NE], nT[:, 128 * n:128 * n + 128], wr[:, :],
                                  start=True, stop=True)
                m.then_inc(logit_done, 1)

            pe.wait_ge(pT_ready, PAIRS)
            turn(1, 0)
            turn(1, 1)
            pe.wait_ge(w_slot[0], 16 * 3)
            pe.wait_ge(nT_ready, G + 1)
            pe.wait_ge(oT_ready, G)
            up(0, 0)
            turn(1, 2)
            pe.wait_ge(nT_ready, G + 2)
            up(1, 1)
            pe.wait_ge(xl_ready, 3)
            for c in range(3):
                logits(c)
            turn(1, 3)
            logits(3)
            pe.wait_ge(xl_ready, G)

            def units(i):
                for k in range(UNITS):
                    u = UNITS * i + k
                    if k % G == 0:
                        pe.wait_ge(w_slot[k // G], 16 * 3 * (i + 1))
                    if not (isinstance(u, int) and u < 2):
                        up(u, k)
                    if there(u - 2):
                        down(u - 2, k - 2)

            units(0)
            with pe.Fori(1, (NE + 1) // SLOTS) as i:
                units(i)
            for k in (UNITS - 2, UNITS - 1):
                down(G * NE + G - UNITS + k, k)


def _layouts(a):
    import numpy as np
    c = np.ascontiguousarray
    f = {k: np.asarray(x) for k, x in a.items()}
    qcols = np.arange(D).reshape(HP, 2, DK).transpose(1, 2, 0).reshape(D)
    return {
        "x": c(f["x"]),
        "ctx": c(f["ctx_1024"].reshape(NCH, CH, D).transpose(0, 2, 1)),
        "Wq": c(f["L0_xattn_Wq"][:, qcols]), "bq": c(f["L0_xattn_bq"][qcols].reshape(D, 1)),
        "Wk": c(f["L0_xattn_Wk"][:, qcols]), "bk": c(f["L0_xattn_bk"][qcols].reshape(D, 1)),
        "Wv": c(f["L0_xattn_Wv"]), "bv": c(f["L0_xattn_bv"].reshape(1, D)),
        "Wo": c(f["L0_xattn_Wo"]), "bo": c(f["L0_xattn_bo"].reshape(1, D)),
        "g1": c(f["L0_ffn_g1"].reshape(D, 1)), "g2": c(f["L0_ffn_g2"].reshape(D, 1)),
        "fWq": c(f["L0_ffn_Wq"].T), "Wkc": c(f["L0_ffn_Wkc"].T), "Wvc": c(f["L0_ffn_Wvc"].T),
        "fWo": c(f["L0_ffn_Wo"].T), "Wr": c(f["L0_ffn_Wr"].T), "eb": c(f["L0_ffn_expert_bias"].reshape(1, NE)),
        **{f"W{k}": c(np.concatenate([f[f"L0_ffn_sW{k}"][None], f[f"L0_ffn_eW{k}"]]).transpose(0, 2, 1))
           for k in (1, 2, 3)},
    }


def kernel(**inputs):
    import concourse.bacc as _bacc
    from concourse.bass_utils import run_bass_kernel_spmd as _run

    nc = _bacc.Bacc("TRN2", target_bir_lowering=False, num_devices=1)
    arrays, aps = {}, {}
    for name, a in _layouts(inputs).items():
        arrays[f"in_{name}"] = a
        aps[name] = nc.dram_tensor(f"in_{name}", a.shape, F32, kind="ExternalInput").ap()
    out = nc.dram_tensor("out_0", (B, SQ, D), F32, kind="ExternalOutput").ap()
    program(nc, aps, out)
    r = _run(nc, [arrays], core_ids=[0])
    return r.results[0]["out_0"]
```
